# Optimizing a Trainium2 kernel written in Bass

```python
import numpy as np
import jax
import jax.numpy as jnp

def _softmax(x, axis=-1):
    return jax.nn.softmax(x, axis=axis)

def _gelu(x):
    return jax.nn.gelu(x, approximate=True)

def _silu(x):
    return jax.nn.silu(x)

def _sigmoid(x):
    return jax.nn.sigmoid(x)

def _layernorm(x, axis=-1, eps=1e-05):
    m = jnp.mean(x, axis=axis, keepdims=True)
    v = jnp.var(x, axis=axis, keepdims=True)
    return (x - m) / jnp.sqrt(v + eps)

def _scatter_add(tgt, idx, src, axis=0):
    return tgt.at[idx].add(src)

def _segment_sum(src, seg, n):
    return jax.ops.segment_sum(src, seg, n)
kernel_name = 'mk_gnn_ffn_d2_gnn_r8_eeffc4'

def setup_inputs(seed: int=0):
    np.random.seed(seed)
    _w = jnp.asarray

    def _rec_inputs():
        import jax
        import jax.numpy as jnp
        _gk = jax.random.key(seed)
        x = -0.0003713 + 1 * jax.random.normal(jax.random.fold_in(_gk, 1), (6250, 256), jnp.float32)
        src = jax.random.randint(jax.random.fold_in(_gk, 2), (100000,), 0, 6250, jnp.int32)
        dst = jnp.minimum((6250 * jax.random.uniform(jax.random.fold_in(_gk, 3), (100000,)) ** 2.0).astype(jnp.int32), 49999)
        _o = jnp.argsort(dst, stable=True)
        src = src[_o]
        dst = dst[_o]
        edge_type_16 = jax.random.randint(jax.random.fold_in(_gk, 13), (100000,), 0, 16, jnp.int32)
        return (x, src, dst, edge_type_16)
    x, src, dst, edge_type_16 = _rec_inputs()

    def _L0_gnn_setup():
        import jax, jax.numpy as jnp
        import numpy as np
        N_NODES = 6250
        N_EDGES = 100000
        HDIM = 256
        NUMRELS = 16

        def _gru_cell(x, h, w_ih, w_hh, b_ih, b_hh):
            gi = x @ w_ih.T + b_ih
            gh = h @ w_hh.T + b_hh
            i_r, i_z, i_n = jnp.split(gi, 3, axis=-1)
            h_r, h_z, h_n = jnp.split(gh, 3, axis=-1)
            r = jax.nn.sigmoid(i_r + h_r)
            z = jax.nn.sigmoid(i_z + h_z)
            n = jnp.tanh(i_n + r * h_n)
            return (1.0 - z) * n + z * h
        key = jax.random.key(seed)
        ks = jax.random.split(key, 9)
        h = jax.random.normal(ks[0], (N_NODES, HDIM), dtype=jnp.float32)
        relvectors = jax.random.normal(ks[1], (NUMRELS, HDIM), dtype=jnp.float32)
        s = 1.0 / np.sqrt(HDIM)
        w_ih = jax.random.uniform(ks[2], (3 * HDIM, HDIM), minval=-s, maxval=s, dtype=jnp.float32)
        w_hh = jax.random.uniform(ks[3], (3 * HDIM, HDIM), minval=-s, maxval=s, dtype=jnp.float32)
        b_ih = jax.random.uniform(ks[4], (3 * HDIM,), minval=-s, maxval=s, dtype=jnp.float32)
        b_hh = jax.random.uniform(ks[5], (3 * HDIM,), minval=-s, maxval=s, dtype=jnp.float32)
        edge_src = jax.random.randint(ks[6], (N_EDGES,), 0, N_NODES, dtype=jnp.int32)
        edge_dst = jax.random.randint(ks[7], (N_EDGES,), 0, N_NODES, dtype=jnp.int32)
        edge_rel = jax.random.randint(ks[8], (N_EDGES,), 0, NUMRELS, dtype=jnp.int32)
        return {'h': h, 'relvectors': relvectors, 'w_ih': w_ih, 'w_hh': w_hh, 'b_ih': b_ih, 'b_hh': b_hh, 'edge_src': edge_src, 'edge_dst': edge_dst, 'edge_rel': edge_rel}
    _L0_gnn_all = _L0_gnn_setup()
    _L0_gnn_in = {k: v for k, v in _L0_gnn_all.items() if k in ('relvectors', 'w_ih', 'w_hh', 'b_ih', 'b_hh')}
    del _L0_gnn_all

    def _L0_ffn_setup():
        import jax, jax.numpy as jnp
        import numpy as np
        B, A = (512, 8)
        IN, OUT = (256, 256)
        SH1, SH2 = (256, 128)
        EH1, EH2 = (128, 64)
        E, TOPK = (4, 2)

        def _shared_mlp(x, W1, b1, W2, b2, W3, b3):
            h = jax.nn.relu(x @ W1 + b1)
            h = jax.nn.relu(h @ W2 + b2)
            return h @ W3 + b3

        def _experts_mlp(x, eW1, eb1, eW2, eb2, eW3, eb3):
            h = jax.nn.relu(jnp.einsum('baf,efh->ebah', x, eW1) + eb1[:, None, None, :])
            h = jax.nn.relu(jnp.einsum('ebah,ehg->ebag', h, eW2) + eb2[:, None, None, :])
            o = jnp.einsum('ebag,ego->ebao', h, eW3) + eb3[:, None, None, :]
            return jnp.moveaxis(o, 0, -1)
        key = jax.random.key(seed)
        ks = jax.random.split(key, 16)
        s = 0.05
        return {'x': jax.random.normal(ks[0], (B, A, IN), jnp.float32), 'sW1': jax.random.normal(ks[1], (IN, SH1), jnp.float32) * s, 'sb1': jnp.zeros((SH1,), jnp.float32), 'sW2': jax.random.normal(ks[2], (SH1, SH2), jnp.float32) * s, 'sb2': jnp.zeros((SH2,), jnp.float32), 'sW3': jax.random.normal(ks[3], (SH2, OUT), jnp.float32) * s, 'sb3': jnp.zeros((OUT,), jnp.float32), 'eW1': jax.random.normal(ks[4], (E, IN, EH1), jnp.float32) * s, 'eb1': jnp.zeros((E, EH1), jnp.float32), 'eW2': jax.random.normal(ks[5], (E, EH1, EH2), jnp.float32) * s, 'eb2': jnp.zeros((E, EH2), jnp.float32), 'eW3': jax.random.normal(ks[6], (E, EH2, OUT), jnp.float32) * s, 'eb3': jnp.zeros((E, OUT), jnp.float32), 'gW': jax.random.normal(ks[7], (IN, E), jnp.float32) * s, 'gb': jnp.zeros((E,), jnp.float32)}
    _L0_ffn_all = _L0_ffn_setup()
    _L0_ffn_in = {k: v for k, v in _L0_ffn_all.items() if k in ('sW1', 'sb1', 'sW2', 'sb2', 'sW3', 'sb3', 'eW1', 'eb1', 'eW2', 'eb2', 'eW3', 'eb3', 'gW', 'gb')}
    del _L0_ffn_all

    def _L1_gnn_setup():
        import jax, jax.numpy as jnp
        import numpy as np
        N_NODES = 12500
        N_EDGES = 200000
        IN_DIM = 256
        OUT_DIM = 256
        key = jax.random.key(seed)
        k1, k2, k3 = jax.random.split(key, 3)
        x = jax.random.normal(k1, (N_NODES, IN_DIM), dtype=jnp.float32)
        limit = 0.1 * np.sqrt(6.0 / (IN_DIM + OUT_DIM))
        W = jax.random.uniform(k2, (OUT_DIM, IN_DIM), dtype=jnp.float32, minval=-limit, maxval=limit)
        b = jnp.zeros((OUT_DIM,), dtype=jnp.float32)
        edge_index = jax.random.randint(k3, (2, N_EDGES), 0, N_NODES, dtype=jnp.int64)
        return {'x': x, 'W': W, 'b': b, 'edge_index': edge_index}
    _L1_gnn_all = _L1_gnn_setup()
    _L1_gnn_in = {k: v for k, v in _L1_gnn_all.items() if k in ('W', 'b')}
    del _L1_gnn_all

    def _L1_ffn_setup():
        import jax, jax.numpy as jnp
        import numpy as np
        TOP_K = 2
        LN_EPS = 1e-05
        key = jax.random.key(seed)
        ks = jax.random.split(key, 8)
        B, S, D, E, H = (16, 1024, 256, 8, 1024)
        x = jax.random.normal(ks[0], (B, S, D), dtype=jnp.float32)
        Wr = jax.random.normal(ks[1], (D, E), dtype=jnp.float32) * 0.1
        br = jnp.zeros((E,), dtype=jnp.float32)
        ln_g = jnp.ones((E, D), dtype=jnp.float32)
        ln_b = jnp.zeros((E, D), dtype=jnp.float32)
        W1 = jax.random.normal(ks[2], (E, D, H), dtype=jnp.float32) * (1.0 / np.sqrt(D))
        b1 = jnp.zeros((E, H), dtype=jnp.float32)
        W2 = jax.random.normal(ks[3], (E, H, D), dtype=jnp.float32) * (1.0 / np.sqrt(H))
        b2 = jnp.zeros((E, D), dtype=jnp.float32)
        return {'x': x, 'Wr': Wr, 'br': br, 'ln_g': ln_g, 'ln_b': ln_b, 'W1': W1, 'b1': b1, 'W2': W2, 'b2': b2}
    _L1_ffn_all = _L1_ffn_setup()
    _L1_ffn_in = {k: v for k, v in _L1_ffn_all.items() if k in ('Wr', 'br', 'ln_g', 'ln_b', 'W1', 'b1', 'W2', 'b2')}
    del _L1_ffn_all
    return {'x': x, 'src': src, 'dst': dst, 'edge_type_16': edge_type_16, 'L0_gnn_relvectors': _L0_gnn_in['relvectors'], 'L0_gnn_w_ih': _L0_gnn_in['w_ih'], 'L0_gnn_w_hh': _L0_gnn_in['w_hh'], 'L0_gnn_b_ih': _L0_gnn_in['b_ih'], 'L0_gnn_b_hh': _L0_gnn_in['b_hh'], 'L0_ffn_sW1': _L0_ffn_in['sW1'], 'L0_ffn_sb1': _L0_ffn_in['sb1'], 'L0_ffn_sW2': _L0_ffn_in['sW2'], 'L0_ffn_sb2': _L0_ffn_in['sb2'], 'L0_ffn_sW3': _L0_ffn_in['sW3'], 'L0_ffn_sb3': _L0_ffn_in['sb3'], 'L0_ffn_eW1': _L0_ffn_in['eW1'], 'L0_ffn_eb1': _L0_ffn_in['eb1'], 'L0_ffn_eW2': _L0_ffn_in['eW2'], 'L0_ffn_eb2': _L0_ffn_in['eb2'], 'L0_ffn_eW3': _L0_ffn_in['eW3'], 'L0_ffn_eb3': _L0_ffn_in['eb3'], 'L0_ffn_gW': _L0_ffn_in['gW'], 'L0_ffn_gb': _L0_ffn_in['gb'], 'L1_gnn_W': _L1_gnn_in['W'], 'L1_gnn_b': _L1_gnn_in['b'], 'L1_ffn_Wr': _L1_ffn_in['Wr'], 'L1_ffn_br': _L1_ffn_in['br'], 'L1_ffn_ln_g': _L1_ffn_in['ln_g'], 'L1_ffn_ln_b': _L1_ffn_in['ln_b'], 'L1_ffn_W1': _L1_ffn_in['W1'], 'L1_ffn_b1': _L1_ffn_in['b1'], 'L1_ffn_W2': _L1_ffn_in['W2'], 'L1_ffn_b2': _L1_ffn_in['b2']}

def reference(x, src, dst, edge_type_16, L0_gnn_relvectors, L0_gnn_w_ih, L0_gnn_w_hh, L0_gnn_b_ih, L0_gnn_b_hh, L0_ffn_sW1, L0_ffn_sb1, L0_ffn_sW2, L0_ffn_sb2, L0_ffn_sW3, L0_ffn_sb3, L0_ffn_eW1, L0_ffn_eb1, L0_ffn_eW2, L0_ffn_eb2, L0_ffn_eW3, L0_ffn_eb3, L0_ffn_gW, L0_ffn_gb, L1_gnn_W, L1_gnn_b, L1_ffn_Wr, L1_ffn_br, L1_ffn_ln_g, L1_ffn_ln_b, L1_ffn_W1, L1_ffn_b1, L1_ffn_W2, L1_ffn_b2):
    import jax
    import jax.numpy as jnp

    def _L0_gnn_ref(h, relvectors, w_ih, w_hh, b_ih, b_hh, edge_src, edge_dst, edge_rel):
        import jax, jax.numpy as jnp
        import numpy as np
        N_NODES = 6250
        N_EDGES = 100000
        HDIM = 256
        NUMRELS = 16

        def _gru_cell(x, h, w_ih, w_hh, b_ih, b_hh):
            gi = x @ w_ih.T + b_ih
            gh = h @ w_hh.T + b_hh
            i_r, i_z, i_n = jnp.split(gi, 3, axis=-1)
            h_r, h_z, h_n = jnp.split(gh, 3, axis=-1)
            r = jax.nn.sigmoid(i_r + h_r)
            z = jax.nn.sigmoid(i_z + h_z)
            n = jnp.tanh(i_n + r * h_n)
            return (1.0 - z) * n + z * h
        msg = h[edge_src] + relvectors[edge_rel]
        red = jax.ops.segment_sum(msg, edge_dst, num_segments=h.shape[0])
        return _gru_cell(red, h, w_ih, w_hh, b_ih, b_hh)

    def _L0_ffn_ref(x, sW1, sb1, sW2, sb2, sW3, sb3, eW1, eb1, eW2, eb2, eW3, eb3, gW, gb):
        import jax, jax.numpy as jnp
        import numpy as np
        B, A = (512, 8)
        IN, OUT = (256, 256)
        SH1, SH2 = (256, 128)
        EH1, EH2 = (128, 64)
        E, TOPK = (4, 2)

        def _shared_mlp(x, W1, b1, W2, b2, W3, b3):
            h = jax.nn.relu(x @ W1 + b1)
            h = jax.nn.relu(h @ W2 + b2)
            return h @ W3 + b3

        def _experts_mlp(x, eW1, eb1, eW2, eb2, eW3, eb3):
            h = jax.nn.relu(jnp.einsum('baf,efh->ebah', x, eW1) + eb1[:, None, None, :])
            h = jax.nn.relu(jnp.einsum('ebah,ehg->ebag', h, eW2) + eb2[:, None, None, :])
            o = jnp.einsum('ebag,ego->ebao', h, eW3) + eb3[:, None, None, :]
            return jnp.moveaxis(o, 0, -1)
        all_out = _experts_mlp(x, eW1, eb1, eW2, eb2, eW3, eb3)
        shared = _shared_mlp(x, sW1, sb1, sW2, sb2, sW3, sb3)
        gates = jax.nn.softmax(x @ gW + gb, axis=-1)
        topv, topi = jax.lax.top_k(gates, TOPK)
        topw = jax.nn.softmax(topv, axis=-1)
        sel = jnp.take_along_axis(all_out, topi[:, :, None, :], axis=-1)
        gated = jnp.sum(sel * topw[:, :, None, :], axis=-1)
        return shared + gated

    def _L1_gnn_ref(x, W, b, edge_index):
        import jax, jax.numpy as jnp
        import numpy as np
        N_NODES = 12500
        N_EDGES = 200000
        IN_DIM = 256
        OUT_DIM = 256
        num_nodes = x.shape[0]
        src, tgt = (edge_index[0], edge_index[1])
        xt = jnp.einsum('ni,oi->no', x, W) + b
        out = jax.ops.segment_sum(xt[src], tgt, num_segments=num_nodes)
        deg = jax.ops.segment_sum(jnp.ones_like(tgt, dtype=x.dtype), tgt, num_segments=num_nodes)
        out = out / (deg + 1.0)[:, None]
        return out

    def _L1_ffn_ref(x, Wr, br, ln_g, ln_b, W1, b1, W2, b2):
        import jax, jax.numpy as jnp
        import numpy as np
        TOP_K = 2
        LN_EPS = 1e-05
        B, S, D = x.shape
        N = B * S
        xt = x.reshape(N, D)
        logits = xt @ Wr + br
        probs = jax.nn.softmax(logits, axis=-1)
        top_p, top_idx = jax.lax.top_k(probs, TOP_K)
        weights = top_p / top_p.sum(axis=-1, keepdims=True)
        mu = xt.mean(axis=-1, keepdims=True)
        var = ((xt - mu) ** 2).mean(axis=-1, keepdims=True)
        xn = (xt - mu) * jax.lax.rsqrt(var + LN_EPS)
        xe = xn[None, :, :] * ln_g[:, None, :] + ln_b[:, None, :]
        h = jax.nn.gelu(jnp.einsum('end,edh->enh', xe, W1) + b1[:, None, :], approximate=False)
        y = jnp.einsum('enh,ehd->end', h, W2) + b2[:, None, :]
        y_tok = jnp.transpose(y, (1, 0, 2))
        sel = jnp.take_along_axis(y_tok, top_idx[:, :, None], axis=1)
        out = (weights[:, :, None] * sel).sum(axis=1)
        return out.reshape(B, S, D)
    edge_index = jnp.stack([src, dst])
    x = x + _L0_gnn_ref(_layernorm(x, axis=-1), L0_gnn_relvectors, L0_gnn_w_ih, L0_gnn_w_hh, L0_gnn_b_ih, L0_gnn_b_hh, src, dst, edge_type_16)
    x = x + _L0_ffn_ref(_layernorm(x, axis=-1)[None], L0_ffn_sW1, L0_ffn_sb1, L0_ffn_sW2, L0_ffn_sb2, L0_ffn_sW3, L0_ffn_sb3, L0_ffn_eW1, L0_ffn_eb1, L0_ffn_eW2, L0_ffn_eb2, L0_ffn_eW3, L0_ffn_eb3, L0_ffn_gW, L0_ffn_gb)[0]
    x = x + _L1_gnn_ref(_layernorm(x, axis=-1), L1_gnn_W, L1_gnn_b, edge_index)
    x = x + _L1_ffn_ref(_layernorm(x, axis=-1)[None], L1_ffn_Wr, L1_ffn_br, L1_ffn_ln_g, L1_ffn_ln_b, L1_ffn_W1, L1_ffn_b1, L1_ffn_W2, L1_ffn_b2)[0]
    return x

_drawn_inputs = setup_inputs


def setup_inputs(seed=0):
    import zlib

    import numpy as np

    out = dict(_drawn_inputs(seed))
    spreads = {'L0_ffn_sb1': (0.0, 0.312),
     'L0_ffn_sb2': (0.0, 0.1),
     'L0_ffn_sb3': (0.0, 0.1),
     'L0_ffn_eb1': (0.0, 0.597),
     'L0_ffn_eb2': (0.0, 0.383),
     'L0_ffn_eb3': (0.0, 0.1),
     'L0_ffn_gb': (0.0, 0.415),
     'L1_gnn_b': (0.0, 0.1),
     'L1_ffn_br': (0.0, 0.1),
     'L1_ffn_ln_g': (1.0, 0.2),
     'L1_ffn_ln_b': (0.0, 0.1),
     'L1_ffn_b1': (0.0, 0.1),
     'L1_ffn_b2': (0.0, 0.1)}
    factors = {'L0_gnn_b_ih': 3.516, 'L0_gnn_b_hh': 4.639}
    for name, (base, spread) in spreads.items():
        noise = np.random.default_rng([zlib.crc32(name.encode()), seed]).standard_normal(out[name].shape)
        drawn = base * np.exp(spread * noise) if base else spread * noise
        out[name] = jnp.asarray(drawn.astype(out[name].dtype))
    for name, factor in factors.items():
        out[name] = (out[name] * factor).astype(out[name].dtype)
    return out
```

```python
from contextlib import ExitStack

import concourse.bass as bass
from concourse import mybir

F32 = mybir.dt.float32
BF16 = mybir.dt.bfloat16
I32 = mybir.dt.int32
ALU = mybir.AluOpType
ACT = mybir.ActivationFunctionType
AX = mybir.AxisListType.X
ds = bass.ds

P = 128
N = 6250
D = 256
C = D // P
NE = 100000
RELS = 16
NT = (N + P - 1) // P
NPAD = NT * P
GW = 4
GROUPS = NT // GW
W = GW * P
EP, EJ = 112, 7
CHUNKS = EP * EJ
U = 4
M = 4
KCOLS = CHUNKS + U
PARTS = 3
BIG = float(1 << 20)
EPS = 1e-5
H = 1024
HC = H // P
E0 = 4
E1 = 8
TT = 256
SUB = TT // P
CAP = NPAD + TT
RW = D + 1
CREDIT = 1
LOOP = "the loop's bounds and the edge windows keep it inside"


def program(nc, a, out):
    assert NT == GROUPS * GW + 1 and EP * EJ * P >= NE

    def narrow(value, low, high):
        return nc.s_assert_within(value, low, high, skip_runtime_bounds_check_because=LOOP)

    with ExitStack() as ctx:
        def sem(name):
            return ctx.enter_context(nc.semaphore(name))

        def sb(name, shape, dt, where=None):
            return (where or ctx).enter_context(nc.sbuf_tensor(name, shape, dt))

        bank = [ctx.enter_context(nc.psum_tensor(f"bank{i}", [P, 512], F32)) for i in range(8)]

        table1 = nc.dram_tensor("table1", (NPAD, PARTS * D), BF16).ap()
        table2 = nc.dram_tensor("table2", (NPAD, PARTS * D), BF16).ap()
        routed = nc.dram_tensor("routed", (E1 * CAP, RW), F32).ap()
        results = nc.dram_tensor("results", (2 * NPAD + TT, D), F32).ap()

        x_res = sb("x_res", [P, NT * D], F32)
        ident = sb("ident", [P, P], F32)
        ustrict = sb("ustrict", [P, P], F32)
        ones = sb("ones", [P, P], F32)
        eps = sb("eps", [P, 1], F32)
        zeros = sb("zeros", [P, W], F32)
        inv_deg = sb("inv_deg", [P, NT], F32)
        row_wt = sb("row_wt", [P, NT * 2], F32)
        place = sb("place", [P, NT * 2], I32)
        filler = sb("filler", [P, SUB, RW], F32)
        lists = sb("lists", [1, 3 * E1 + 1], I32)
        ts_idx = sb("ts_idx", [P, GW, E1], F32)

        def x_cols(first, count):
            return x_res[:, ds(first * D, count * D)]

        graph = ctx.enter_context(ExitStack())
        dstT = sb("dstT", [P, KCOLS], F32, graph)
        typeT = sb("typeT", [P, KCOLS], F32, graph)
        srcT = sb("srcT", [P, KCOLS], I32, graph)
        windows = sb("windows", [1, 3 * NT], I32, graph)
        rounds = sb("rounds", [1, NT + 1], I32, graph)
        tbase = sb("tbase", [P, NT], F32, graph)
        iota_row = sb("iota_row", [P, P], BF16, graph)
        zlhs = zeros[:, 0:P // 2].bitcast(BF16)
        zrhs = zeros[:, 0:136].bitcast(BF16)
        rows = sb("rows", [P, M * U, PARTS * D], BF16, graph)
        onehot = sb("onehot", [P, M * U, P], BF16, graph)
        typehot = sb("typehot", [P, M * U, RELS], BF16, graph)
        idx = sb("idx", [P, M * U], I32, graph)
        spare = sb("spare", [P, 4], F32, graph)
        h4 = sb("h4", [P, GW, D], F32, graph)
        stats = sb("stats", [P, GW, 6], F32, graph)
        mean_var = sb("mean_var", [P, GW, 2], F32, graph)
        stdev = sb("stdev", [P, GW], F32, graph)
        rstd = sb("rstd", [P, GW], F32, graph)
        part = sb("part", [P, GW, PARTS * D], BF16, graph)
        rest = sb("rest", [P, 2, 2, D], F32, graph)
        ln_mean = sb("ln_mean", [P, NT], F32, graph)
        ln_rstd = sb("ln_rstd", [P, NT], F32, graph)
        t0 = sb("t0", [P, C, W], F32, graph)

        consts_ready = sem("consts_ready")
        filler_clear = sem("filler_clear")
        loads_done = sem("loads_done")
        x_loaded = sem("x_loaded")
        x_tail_loaded = sem("x_tail_loaded")

        waits_passed = sem("waits_passed")

        def settled(eng):
            eng.sem_inc(waits_passed, 1)

        class Chain:

            def __init__(self, eng, name, per):
                self.eng, self.sem, self.per = eng, sem(name), per

            def begin(self, round_):
                base = round_ * self.per
                self.base, self.n = base if isinstance(base, int) else self.eng.snap(base), 0

            def link(self, instruction):
                self.n += 1
                instruction.then_inc(self.sem, 1)
                self.eng.wait_ge(self.sem, self.base + self.n)

            def end(self):
                assert self.n <= self.per, self.n
                if self.n < self.per:
                    self.eng.sem_inc(self.sem, self.per - self.n)

        def ln_stats(dve, chain, var_ready, std_ready, g, w):
            settled(dve)
            for i in range(w):
                last = nc.vector.bn_stats(stats[:, i, :], x_cols(g * GW + i, 1))
            chain.link(last)
            settled(dve)
            for i in range(w):
                last = nc.vector.bn_aggr(mean_var[:, i, :], stats[:, i, :])
            last.then_inc(var_ready, 1)
            dve.wait_ge(std_ready, g + 1)
            chain.link(nc.vector.reciprocal(rstd[:, 0:w], stdev[:, 0:w]))

        def ln_apply(g, w):
            for i in range(w):
                last = nc.vector.tensor_scalar(h4[:, i, :], x_cols(g * GW + i, 1), mean_var[:, i, 0:1],
                                               rstd[:, i:i + 1], ALU.subtract, ALU.mult)
            return last

        def ln_sqrt(act, var_ready, std_ready, g, w):
            act.wait_ge(var_ready, g + 1)
            nc.scalar.activation(stdev[:, 0:w], mean_var[:, 0:w, 1], ACT.Sqrt,
                                 bias=eps[:, 0:1]).then_inc(std_ready, 1)

        setup = ctx.enter_context(ExitStack())
        weights = {}

        layer0 = graph.enter_context(ExitStack())

        def wt(name, shape):
            weights[name] = sb(name, shape, F32, layer0)
            return weights[name]

        wihT = wt("wihT", [P, C, 3 * D])
        whhT = wt("whhT", [P, C, 3 * D])
        gcnT = wt("gcnT", [P, C, D])
        relvec = wt("relvec", [RELS, D])
        sW1 = wt("sW1", [P, C, D])
        sW2 = wt("sW2", [P, C, P])
        sW3 = wt("sW3", [P, D])
        eW1 = wt("eW1", [P, E0, C, P])
        eW2 = wt("eW2", [P, E0, 64])
        eW3 = wt("eW3", [P, 2, D])
        gW = wt("gW", [P, C, E0])
        Wr = wt("Wr", [P, C, E1])
        bih = wt("bih", [P, 6])
        bhh = wt("bhh", [P, 6])
        brz = wt("brz", [P, 4])
        b_l1 = wt("b_l1", [P, 6])
        b_l2 = wt("b_l2", [P, 3])
        b_l3 = wt("b_l3", [E0 + 1, D])
        gb = wt("gb", [1, E0])
        gcn_b = wt("gcn_b", [1, D])
        br = wt("br", [1, E1])

        edge_i = [sb(f"edge_i{n}", [P, EJ * P], I32, setup) for n in range(3)]
        edge_f = [sb(f"edge_f{n}", [P, EJ * P], F32, setup) for n in range(3)]
        iw = [sb(f"iw{n}", [P, n_], I32, setup) for n, n_ in enumerate((P, NT, NT * EJ, EJ, GW * E1))]
        wlow = sb("wlow", [P, NT, EJ], F32, setup)
        kidx = sb("kidx", [P, EJ], F32, setup)
        kmb = sb("kmb", [P, EJ], F32, setup)
        ov = sb("ov", [P, NT, EJ], F32, setup)
        ov2 = sb("ov2", [P, NT, EJ], F32, setup)
        bmm = sb("bmm", [P, 2, EJ], F32, setup)
        lohi = sb("lohi", [P, 2, NT], F32, setup)
        col = sb("col", [64, 8], F32, setup)
        coli = sb("coli", [64, 2], I32, setup)
        wraw = [sb(f"wraw{n}", [P, 6 if n < 2 else 2, D], F32, setup) for n in range(3)]

        edges_clear = sem("edges_clear")
        edges_loaded = sem("edges_loaded")
        edges_float = sem("edges_float")
        edges_turned = sem("edges_turned")
        edges_copied = sem("edges_copied")
        lohi_ready = sem("lohi_ready")
        lohi_turned = sem("lohi_turned")
        col_ready = sem("col_ready")
        row_ready = sem("row_ready")
        raw_turned = sem("raw_turned")
        raw_copied = sem("raw_copied")
        iotas = sem("iotas")
        s_var = sem("s_var")
        s_std = sem("s_std")
        s_h = sem("s_h")
        s_hi = sem("s_hi")
        s_r1 = sem("s_r1")
        s_mid = sem("s_mid")
        s_r2 = sem("s_r2")
        s_lo = sem("s_lo")
        s_out = sem("s_out")
        s_left = sem("s_left")
        WEIGHT_LOADS = 30

        with nc.Block() as block:
            @block.sync
            def _(sp):
                sp.dma_start(x_res[:, 0:(NT - 1) * D].rearrange("p (t d) -> p t d", d=D),
                             a["x"][0:(NT - 1) * P, :].rearrange("(t p) d -> p t d", p=P)).then_inc(x_loaded, 16)
                sp.wait_ge(edges_clear, 1)
                full = NE // (EJ * P)
                left = NE - full * EJ * P
                for n, name in enumerate(("dst", "src", "edge_type_16")):
                    e = a[name]
                    sp.dma_start(edge_i[n][0:full, :],
                                 e[0:full * EJ * P].rearrange("(p c) -> p c", p=full)).then_inc(edges_loaded, 16)
                    sp.dma_start(edge_i[n][full:full + 1, 0:left],
                                 e[full * EJ * P:NE].rearrange("(p c) -> p c", p=1)).then_inc(edges_loaded, 16)
                sp.dma_start(x_res[0:N - (NT - 1) * P, (NT - 1) * D:NT * D],
                             a["x"][(NT - 1) * P:N, :]).then_inc(x_tail_loaded, 16)
                sp.sem_inc(s_left, CREDIT)
                def store(g, w):
                    sp.wait_ge(s_lo, CREDIT + 2 * g + (2 if w > 1 else 1))
                    sp.dma_start(table1[ds(g * W, w * P), :].rearrange("(t p) d -> p t d", p=P),
                                 part[:, 0:w, :]).then_inc(s_out, 16)
                    sp.wait_ge(s_out, 16 * g + 16)
                    sp.sem_inc(s_left, 1)
                with sp.Fori(0, GROUPS) as g:
                    store(g, GW)
                store(GROUPS, 1)

            @block.gpsimd
            def _(pool):
                nc.gpsimd.iota(iw[0][:, :], pattern=[[1, P]], base=0, channel_multiplier=0).then_inc(iotas, 1)
                nc.gpsimd.iota(iw[1][:, :], pattern=[[P, NT]], base=0, channel_multiplier=0).then_inc(iotas, 1)
                nc.gpsimd.iota(iw[2][:, :], pattern=[[P, NT], [0, EJ]], base=0, channel_multiplier=0).then_inc(iotas, 1)
                nc.gpsimd.iota(iw[3][:, :], pattern=[[1, EJ]], base=0, channel_multiplier=EJ).then_inc(iotas, 1)
                nc.gpsimd.iota(iw[4][:, :], pattern=[[0, GW], [1, E1]], base=0, channel_multiplier=0).then_inc(iotas, 1)
                nc.gpsimd.iota(place[:, :], pattern=[[2 * P, NT], [1, 2]], base=0, channel_multiplier=2)
                nc.gpsimd.memset(filler[:, :, :], 0.0).then_inc(filler_clear, 1)
                pool.wait_ge(filler_clear, 1)
                nc.gpsimd.iota(filler[:, :, D:RW].bitcast(I32), pattern=[[1, SUB], [1, 1]], base=2 * NPAD,
                               channel_multiplier=SUB)
                nc.gpsimd.memset(ident[:, :], 0.0).then_inc(consts_ready, 1)
                nc.gpsimd.memset(ones[:, :], 1.0).then_inc(consts_ready, 1)
                nc.gpsimd.memset(zeros[:, :], 0.0).then_inc(consts_ready, 1)
                nc.gpsimd.memset(eps[:, :], EPS).then_inc(consts_ready, 1)
                pool.wait_ge(consts_ready, 4)
                nc.gpsimd.affine_select(out=ident[:, :], in_=ident[:, :], compare_op=ALU.not_equal, fill=1.0,
                                        base=0, pattern=[[-1, P]], channel_multiplier=1).then_inc(consts_ready, 1)
                nc.gpsimd.affine_select(out=ustrict[:, :], in_=ones[:, :], compare_op=ALU.is_gt, fill=0.0,
                                        base=0, pattern=[[1, P]], channel_multiplier=-1).then_inc(consts_ready, 1)

            @block.scalar
            def _(act):
                n = 0

                def load(dst, src):
                    nonlocal n
                    n += 1
                    act.dma_start(dst, src, allow_slow_non_contiguous=True).then_inc(loads_done, 16)

                load(wraw[0][:, :, :], a["L0_gnn_w_ih"].rearrange("(j p) i -> p j i", p=P))
                load(wraw[1][:, :, :], a["L0_gnn_w_hh"].rearrange("(j p) i -> p j i", p=P))
                load(wraw[2][:, :, :], a["L1_gnn_W"].rearrange("(j p) i -> p j i", p=P))
                load(relvec[:, :], a["L0_gnn_relvectors"])
                load(bih[:, :], a["L0_gnn_b_ih"].rearrange("(j p) -> p j", p=P))
                load(bhh[:, :], a["L0_gnn_b_hh"].rearrange("(j p) -> p j", p=P))
                load(sW1[:, :, :], a["L0_ffn_sW1"].rearrange("(c p) o -> p c o", p=P))
                load(sW2[:, :, :], a["L0_ffn_sW2"].rearrange("(c p) o -> p c o", p=P))
                load(sW3[:, :], a["L0_ffn_sW3"])
                for e in range(E0):
                    load(eW1[:, e, :, :], a["L0_ffn_eW1"][e].rearrange("(c p) o -> p c o", p=P))
                load(eW2[:, :, :], a["L0_ffn_eW2"].rearrange("e p o -> p e o"))
                load(eW3[:, :, :], a["L0_ffn_eW3"].rearrange("(q r) k o -> (r k) q o", r=2))
                load(gW[:, :, :], a["L0_ffn_gW"].rearrange("(c p) o -> p c o", p=P))
                load(Wr[:, :, :], a["L1_ffn_Wr"].rearrange("(c p) o -> p c o", p=P))
                load(b_l1[:, 0:2], a["L0_ffn_sb1"].rearrange("(j p) -> p j", p=P))
                load(b_l1[:, 2:6], a["L0_ffn_eb1"].rearrange("e p -> p e"))
                load(b_l2[:, 0:1], a["L0_ffn_sb2"].rearrange("(p j) -> p j", j=1))
                load(b_l2[:, 1:3], a["L0_ffn_eb2"].rearrange("(q r) k -> (r k) q", r=2))
                load(b_l3[0:E0, :], a["L0_ffn_eb3"])
                load(b_l3[E0:E0 + 1, :], a["L0_ffn_sb3"].rearrange("(j p) -> j p", j=1))
                load(gb[:, :], a["L0_ffn_gb"].rearrange("(j p) -> j p", j=1))
                load(gcn_b[:, :], a["L1_gnn_b"].rearrange("(j p) -> j p", j=1))
                load(br[:, :], a["L1_ffn_br"].rearrange("(j p) -> j p", j=1))
                weights["loads"] = n

                def group(g, w):
                    ln_sqrt(act, s_var, s_std, g, w)
                    for half in range((w + 1) // 2):
                        k = min(2, w - 2 * half)
                        lo = 2 * half
                        act.wait_ge(s_h, g + 1)
                        act.wait_ge(s_left, g + CREDIT)
                        nc.scalar.activation(part[:, lo:lo + k, 0:D], h4[:, lo:lo + k, :],
                                             ACT.Copy).then_inc(s_hi, 1)
                    for half in range((w + 1) // 2):
                        k = min(2, w - 2 * half)
                        lo = 2 * half
                        act.wait_ge(s_r1, 2 * g + half + 1)
                        nc.scalar.activation(part[:, lo:lo + k, D:2 * D], rest[:, half, 0:k, :],
                                             ACT.Copy).then_inc(s_mid, 1)
                    for half in range((w + 1) // 2):
                        k = min(2, w - 2 * half)
                        lo = 2 * half
                        act.wait_ge(s_r2, 2 * g + half + 1)
                        nc.scalar.activation(part[:, lo:lo + k, 2 * D:3 * D], rest[:, half, 0:k, :],
                                             ACT.Copy).then_inc(s_lo, 1)

                act.wait_ge(consts_ready, 4)
                act.sem_inc(s_mid, CREDIT)
                act.sem_inc(s_lo, CREDIT)
                with act.Fori(0, GROUPS) as g:
                    group(g, GW)
                group(GROUPS, 1)
                act.wait_ge(loads_done, 16 * n)

            @block.vector
            def _(dve):
                chain = Chain(dve, "setup_chain", 64)
                chain.begin(0)
                nc.vector.memset(edge_i[0][:, :], -1)
                nc.vector.memset(edge_i[1][:, :], 0)
                nc.vector.memset(edge_i[2][:, :], 0)
                nc.vector.memset(x_res[:, (NT - 1) * D:NT * D], 0.0).then_inc(edges_clear, 1)
                nc.vector.memset(dstT[:, CHUNKS:KCOLS], -1.0)
                nc.vector.memset(typeT[:, CHUNKS:KCOLS], 0.0)
                nc.vector.memset(srcT[:, CHUNKS:KCOLS], 0)
                dve.wait_ge(iotas, 5)
                nc.vector.tensor_copy(iota_row[:, :], iw[0][:, :])
                nc.vector.tensor_copy(tbase[:, :], iw[1][:, :])
                nc.vector.tensor_copy(wlow[:, :, :], iw[2][:, :].rearrange("p (t j) -> p t j", j=EJ))
                nc.vector.tensor_copy(ts_idx[:, :, :], iw[4][:, :].rearrange("p (t j) -> p t j", j=E1))
                nc.vector.tensor_scalar(kmb[:, :], iw[3][:, :], BIG, None, ALU.subtract)
                chain.link(nc.vector.tensor_scalar(kidx[:, :], iw[3][:, :], 1.0, None, ALU.add))
                dve.wait_ge(edges_loaded, 6 * 16)
                for n in range(3):
                    nc.vector.tensor_copy(edge_f[n][0:EP, :], edge_i[n][0:EP, :]).then_inc(edges_float, 1)
                dve.wait_ge(edges_float, 3)
                d3 = edge_f[0][0:EP, :].rearrange("p (j e) -> p j e", e=P)
                nc.vector.tensor_reduce(bmm[0:EP, 0, :], d3, AX, ALU.max)
                pad = edge_i[0][0:EP, :].bitcast(F32)
                chain.link(nc.vector.tensor_scalar(pad, edge_f[0][0:EP, :], 0.0, BIG, ALU.is_lt, ALU.mult))
                chain.link(nc.vector.tensor_tensor(pad, pad, edge_f[0][0:EP, :], ALU.add))
                chain.link(nc.vector.tensor_reduce(bmm[0:EP, 1, :], pad.rearrange("p (j e) -> p j e", e=P), AX, ALU.min))
                top = bmm[0:EP, 0, :].unsqueeze(1).to_broadcast([EP, NT, EJ])
                low = bmm[0:EP, 1, :].unsqueeze(1).to_broadcast([EP, NT, EJ])
                nc.vector.tensor_tensor(ov[0:EP], top, wlow[0:EP], ALU.is_ge)
                chain.link(nc.vector.scalar_tensor_tensor(ov2[0:EP], wlow[0:EP], float(P), low, ALU.add, ALU.is_gt))
                chain.link(nc.vector.tensor_tensor(ov[0:EP], ov[0:EP], ov2[0:EP], ALU.mult))
                kb = kmb[0:EP, :].unsqueeze(1).to_broadcast([EP, NT, EJ])
                kp = kidx[0:EP, :].unsqueeze(1).to_broadcast([EP, NT, EJ])
                chain.link(nc.vector.tensor_tensor(ov2[0:EP], ov[0:EP], kb, ALU.mult))
                nc.vector.tensor_reduce(lohi[0:EP, 0, :], ov2[0:EP], AX, ALU.min)
                chain.link(nc.vector.tensor_tensor(ov[0:EP], ov[0:EP], kp, ALU.mult))
                nc.vector.tensor_reduce(lohi[0:EP, 1, :], ov[0:EP], AX, ALU.max).then_inc(lohi_ready, 1)
                for n in range(3):
                    dst = (dstT, srcT, typeT)[n]
                    view = dst[:, 0:CHUNKS].rearrange("p (k j) -> p j k", j=EJ)
                    for half in range(2):
                        dve.wait_ge(edges_turned, 2 * n + half + 1)
                        j0, k = (0, 4) if half == 0 else (4, 3)
                        nc.vector.tensor_copy(
                            view[:, j0:j0 + k, :],
                            bank[2 * n + half][:, 0:k * EP].rearrange("p (j k) -> p j k", k=EP)).then_inc(edges_copied, 1)
                dve.wait_ge(lohi_turned, 1)
                nc.vector.tensor_reduce(col[0:NT, 0:1], bank[6][0:NT, 0:EP], AX, ALU.min)
                chain.link(nc.vector.tensor_reduce(col[0:NT, 1:2], bank[6][0:NT, EP:2 * EP], AX, ALU.max))
                nc.vector.tensor_scalar(col[0:NT, 2:3], col[0:NT, 1:2], 1.0, None, ALU.max)
                chain.link(nc.vector.tensor_scalar(col[0:NT, 3:4], col[0:NT, 0:1], BIG, None, ALU.add))
                chain.link(nc.vector.tensor_scalar(col[0:NT, 4:5], col[0:NT, 2:3], 1.0, None, ALU.subtract))
                chain.link(nc.vector.tensor_tensor(col[0:NT, 5:6], col[0:NT, 3:4], col[0:NT, 4:5], ALU.min))
                chain.link(nc.vector.tensor_tensor(col[0:NT, 6:7], col[0:NT, 2:3], col[0:NT, 5:6], ALU.subtract))
                chain.link(nc.vector.tensor_scalar(coli[0:NT, 0:1], col[0:NT, 6:7], float(U - 1), None, ALU.add))
                chain.link(nc.vector.tensor_single_scalar(coli[0:NT, 1:2], coli[0:NT, 0:1], U.bit_length() - 1,
                                                          ALU.arith_shift_right))
                nc.vector.tensor_copy(col[0:NT, 7:8], coli[0:NT, 1:2]).then_inc(col_ready, 1)
                dve.wait_ge(row_ready, 1)
                chain.link(nc.vector.tensor_copy(windows[0:1, :], bank[7][0:1, 0:3 * NT]))
                chain.link(nc.vector.tensor_scalar(rounds[:, 0:NT], windows[:, 2 * NT:3 * NT], float(M - 1), None,
                                                   ALU.add))
                chain.link(nc.vector.tensor_tensor(rounds[:, NT:NT + 1], rounds[:, NT - 1:NT],
                                                   windows[:, 2 * NT - 1:2 * NT], ALU.add))
                chain.link(nc.vector.tensor_single_scalar(rounds[:, :], rounds[:, :], M.bit_length() - 1,
                                                          ALU.arith_shift_right))
                turned = 0
                for n, (dst, blocks) in enumerate(((wihT, 6), (whhT, 6), (gcnT, 2))):
                    for c in range(C):
                        for j0 in range(0, blocks, 4):
                            k = min(4, blocks - j0)
                            turned += 1
                            dve.wait_ge(raw_turned, turned)
                            nc.vector.tensor_copy(dst[:, c, j0 * P:(j0 + k) * P],
                                                  bank[(turned - 1) % 6][:, 0:k * P]).then_inc(raw_copied, 1)
                dve.wait_ge(loads_done, 16 * weights["loads"])
                chain.link(nc.vector.tensor_tensor(brz[:, :], bih[:, 0:4], bhh[:, 0:4], ALU.add))
                chain.end()

                chain = Chain(dve, "table1_chain", 4)
                dve.wait_ge(x_loaded, 16)
                dve.wait_ge(x_tail_loaded, 16)

                def group(g, w):
                    chain.begin(g)
                    ln_stats(dve, chain, s_var, s_std, g, w)
                    nc.vector.tensor_copy(ln_mean[:, ds(g * GW, w)], mean_var[:, 0:w, 0])
                    nc.vector.tensor_copy(ln_rstd[:, ds(g * GW, w)], rstd[:, 0:w])
                    dve.wait_ge(s_mid, CREDIT + 2 * g)
                    ln_apply(g, w).then_inc(s_h, 1)
                    dve.wait_ge(s_h, g + 1)
                    for half in range((w + 1) // 2):
                        k, lo = min(2, w - 2 * half), 2 * half
                        dve.wait_ge(s_hi, 2 * g + half + 1)
                        dve.wait_ge(s_lo, CREDIT + 2 * g)
                        nc.vector.tensor_tensor(rest[:, half, 0:k, :], h4[:, lo:lo + k, :],
                                                part[:, lo:lo + k, 0:D], ALU.subtract).then_inc(s_r1, 1)
                    for half in range((w + 1) // 2):
                        k, lo = min(2, w - 2 * half), 2 * half
                        dve.wait_ge(s_mid, CREDIT + 2 * g + half + 1)
                        nc.vector.tensor_tensor(rest[:, half, 0:k, :], rest[:, half, 0:k, :],
                                                part[:, lo:lo + k, D:2 * D], ALU.subtract).then_inc(s_r2, 1)
                    chain.end()

                with dve.Fori(0, GROUPS) as g:
                    group(g, GW)
                group(GROUPS, 1)

            @block.tensor
            def _(pe):
                pe.wait_ge(consts_ready, 6)
                for n in range(3):
                    pe.wait_ge(edges_float, n + 1)
                    for half in range(2):
                        j0, k = (0, 4) if half == 0 else (4, 3)
                        for j in range(k):
                            last = nc.tensor.transpose(bank[2 * n + half][:, j * EP:(j + 1) * EP],
                                                       edge_f[n][0:EP, (j0 + j) * P:(j0 + j + 1) * P],
                                                       ident[0:EP, 0:EP])
                        last.then_inc(edges_turned, 1)
                pe.wait_ge(lohi_ready, 1)
                for n in range(2):
                    last = nc.tensor.transpose(bank[6][0:NT, n * EP:(n + 1) * EP], lohi[0:EP, n, :],
                                               ident[0:EP, 0:EP])
                last.then_inc(lohi_turned, 1)
                pe.wait_ge(col_ready, 1)
                for n, (c0, m) in enumerate(((5, ident), (7, ident), (7, ustrict))):
                    last = nc.tensor.matmul(bank[7][0:1, n * NT:(n + 1) * NT], col[0:NT, c0:c0 + 1], m[0:NT, 0:NT],
                                            start=True, stop=True)
                last.then_inc(row_ready, 1)
                pe.wait_ge(loads_done, 16 * weights["loads"])
                pe.wait_ge(edges_copied, 6)
                turned = 0
                for n, blocks in enumerate((6, 6, 2)):
                    for c in range(C):
                        for j0 in range(0, blocks, 4):
                            k = min(4, blocks - j0)
                            if turned >= 6:
                                pe.wait_ge(raw_copied, turned - 5)
                            for j in range(k):
                                last = nc.tensor.transpose(bank[turned % 6][:, j * P:(j + 1) * P],
                                                           wraw[n][:, j0 + j, c * P:(c + 1) * P], ident[:, :])
                            last.then_inc(raw_turned, 1)
                            turned += 1
        setup.close()

        class Gather:
            def __init__(self, name, table, with_types):
                self.table, self.with_types = table, with_types
                self.idx_landed = sem(name + "_idx_landed")
                self.landed = [sem(f"{name}_rows_landed{m}") for m in range(M)]
                self.rows_ready = sem(name + "_rows_ready")
                self.used = sem(name + "_rows_used")
                self.hot = sem(name + "_onehot_ready")
                self.done = sem(name + "_window_done")
                self.evacuated = sem(name + "_window_evacuated")

        def window_values(eng, t):
            first = eng.value_load(windows[0:1, ds(t, 1)], min_val=0, max_val=CHUNKS - 1)
            blocks = eng.value_load(windows[0:1, ds(t + NT, 1)], min_val=1, max_val=CHUNKS // U)
            before = eng.value_load(windows[0:1, ds(t + 2 * NT, 1)], min_val=0, max_val=NT * CHUNKS // U)
            return first, blocks, before

        def ring(eng, n):
            return narrow(eng.snap((n % M) * U), 0, (M - 1) * U)

        def sp_indices(sp, q):
            def block_indices(n, k):
                slot = ring(sp, n)
                sp.wait_ge(q.rows_ready, n + 1)
                sp.dma_start(idx[:, ds(slot, U)], srcT[:, ds(k, U)],
                             allow_slow_non_contiguous=True).then_inc(q.idx_landed, 16)
                sp.wait_ge(q.idx_landed, n * 16 + 16)
                settled(sp)

            with sp.Fori(0, NT) as t:
                first, blocks, before = window_values(sp, t)
                with sp.Fori(0, blocks) as j:
                    block_indices(sp.snap(before + j), narrow(sp.snap(first + j * U), 0, CHUNKS - 1))
            _, blocks, before = window_values(sp, NT - 1)
            with sp.Fori(0, M - 1) as extra:
                block_indices(sp.snap(before + blocks + extra), 0)

        def pool_begin(pool, q, column):
            pool.sem_inc(q.rows_ready, M - 1)
            pool.dma_start(spare[:, column:column + 1], zeros[:, 0:1],
                           allow_slow_non_contiguous=True).then_inc(q.landed[M - 1], 16)

        def pool_rounds(pool, q, r0, r1):
            with pool.Fori(r0, r1) as r:
                for m in range(M):
                    n = pool.snap(r * M + m)
                    pool.wait_ge(q.idx_landed, n * 16 + 16)
                    pool.wait_ge(q.used, n + 1)
                    settled(pool)
                    for s in range(m * U, (m + 1) * U):
                        nc.gpsimd.indirect_dma_start(
                            out=rows[:, s, :], out_offset=None, in_=q.table,
                            in_offset=bass.IndirectOffsetOnAxis(idx[:, s:s + 1], axis=0)).then_inc(q.landed[m], 16)
                    if m == 0:
                        pool.wait_ge(q.landed[M - 1], r * (16 * U) + 16)
                    else:
                        pool.wait_ge(q.landed[m - 1], r * (16 * U) + 16 * U)
                    pool.sem_inc(q.rows_ready, 1)

        def pool_end(pool, q, r):
            pool.wait_ge(q.landed[M - 1], r * (16 * U) + 16)
            pool.sem_inc(q.rows_ready, 1)

        def rounds_value(eng, t, low):
            return eng.value_load(rounds[0:1, ds(t, 1)], min_val=low, max_val=NT * CHUNKS // (U * M) + 1)

        def dve_window(dve, q, t):
            first, blocks, before = window_values(dve, t)
            base = tbase[:, ds(t, 1)]
            with dve.Fori(0, blocks) as j:
                n = dve.snap(before + j)
                k = narrow(dve.snap(first + j * U), 0, CHUNKS - 1)
                slot = ring(dve, n)
                dve.wait_ge(q.used, n + 1)
                last = nc.vector.scalar_tensor_tensor(
                    onehot[:, ds(slot, U), :], iota_row[:, :].unsqueeze(1).to_broadcast([P, U, P]), base,
                    dstT[:, ds(k, U)].unsqueeze(2).to_broadcast([P, U, P]), ALU.add, ALU.is_equal)
                if q.with_types:
                    last = nc.vector.tensor_tensor(
                        typehot[:, ds(slot, U), :], iota_row[:, 0:RELS].unsqueeze(1).to_broadcast([P, U, RELS]),
                        typeT[:, ds(k, U)].unsqueeze(2).to_broadcast([P, U, RELS]), ALU.is_equal)
                last.then_inc(q.hot, 1)

        def pe_window(pe, q, t, acc):
            first, blocks, before = window_values(pe, t)
            width = D + RELS if q.with_types else D
            nc.tensor.matmul(acc[:, 0:width], zlhs, zrhs[:, 0:width], start=True, stop=False, skip_group_check=True)
            with pe.Fori(0, blocks) as j:
                n = pe.snap(before + j)
                slot = ring(pe, n)
                pe.wait_ge(q.hot, n + 1)
                pe.wait_ge(q.rows_ready, n + M + 1)
                for s in range(U):
                    hot = onehot[:, ds(narrow(slot + s, 0, M * U - 1), 1), :].rearrange("p a e -> p (a e)")
                    at = ds(narrow(slot + s, 0, M * U - 1), 1)
                    for part_ in range(PARTS):
                        last = nc.tensor.matmul(acc[:, 0:D], hot,
                                                rows[:, at, part_ * D:(part_ + 1) * D].rearrange("p a d -> p (a d)"),
                                                start=False, stop=False, skip_group_check=True)
                    if q.with_types:
                        last = nc.tensor.matmul(acc[:, D:width], hot, typehot[:, at, :].rearrange("p a d -> p (a d)"),
                                                start=False, stop=False, skip_group_check=True)
                last.then_inc(q.used, 1)
            nc.tensor.matmul(acc[:, 0:width], zlhs, zrhs[:, 0:width], start=False, stop=True,
                             skip_group_check=True).then_inc(q.done, 1)

        def pe_windows(pe, q, g, i):
            if not (isinstance(g, int) and g == 0 and i < 2):
                pe.wait_ge(q.evacuated, g * GW + i - 1)
            pe_window(pe, q, g * GW + i, bank[6 + i % 2])

        def router_buffers(name, where):
            f = {k: sb(f"{name}_{k}", [P, GW, E1], F32, where) for k in ("lg", "ex", "p", "c", "eq1", "eq2", "p2")}
            f.update({k: sb(f"{name}_{k}", [P, GW], F32, where) for k in ("m", "m1", "m2", "i", "s", "w1", "w2", "e")})
            return f

        def router_logits(f, chain, logits, w, experts):
            lg = f["lg"][:, 0:w, 0:experts]
            chain.link(nc.vector.tensor_copy(lg, logits.rearrange("p (t e) -> p t e", e=experts)))
            chain.link(nc.vector.tensor_reduce(f["m"][:, 0:w], lg, AX, ALU.max))
            m = f["m"][:, 0:w].unsqueeze(2).to_broadcast([P, w, experts])
            return nc.vector.tensor_tensor(lg, lg, m, ALU.subtract)

        def router_choice(f, chain, w, experts):
            def wide(v):
                return v[:, 0:w].unsqueeze(2).to_broadcast([P, w, experts])
            ex, p, c, eq1, eq2, p2 = (f[k][:, 0:w, 0:experts] for k in ("ex", "p", "c", "eq1", "eq2", "p2"))
            index = ts_idx[:, 0:w, 0:experts]
            chain.link(nc.vector.tensor_reduce(f["s"][:, 0:w], ex, AX, ALU.add))
            chain.link(nc.vector.reciprocal(f["s"][:, 0:w], f["s"][:, 0:w]))
            chain.link(nc.vector.tensor_tensor(p, ex, wide(f["s"]), ALU.mult))
            for source, m, eq in ((p, f["m1"], eq1), (p2, f["m2"], eq2)):
                chain.link(nc.vector.tensor_reduce(m[:, 0:w], source, AX, ALU.max))
                chain.link(nc.vector.tensor_tensor(c, source, wide(m), ALU.not_equal))
                chain.link(nc.vector.scalar_tensor_tensor(c, c, 16.0, index, ALU.mult, ALU.add))
                chain.link(nc.vector.tensor_reduce(f["i"][:, 0:w], c, AX, ALU.min))
                chain.link(nc.vector.tensor_tensor(eq, index, wide(f["i"]), ALU.is_equal))
                if eq is eq1:
                    chain.link(nc.vector.scalar_tensor_tensor(p2, eq1, -4.0, p, ALU.mult, ALU.add))

        hT = t0
        red4 = sb("red4", [P, GW, D + RELS], F32, layer0)
        ctT = sb("ctT", [RELS, W], F32, layer0)
        redT = sb("redT", [P, C, W], F32, layer0)
        rT = sb("rT", [P, C, W], F32, layer0)
        zT = sb("zT", [P, C, W], F32, layer0)
        tT = sb("tT", [P, C, W], F32, layer0)
        nT = sb("nT", [P, C, W], F32, layer0)
        a1T = sb("a1T", [P, 6, W], F32, layer0)
        a2T = sb("a2T", [P, 3, W], F32, layer0)
        gate5 = sb("gate5", [P, GW, E1], F32, layer0)
        gT = sb("gT", [E0 + 1, W], F32, layer0)
        deg = sb("deg", [P, GW], F32, layer0)
        f0 = router_buffers("f0", layer0)
        q1 = Gather("g1", table1, True)
        names = ("h4_ready hT_ps ct_ps ct_sb redT_ps hT_sb redT_sb r_ps z_ps in_ps hn_ps r_act z_act t1_done t2_done "
                 "n_act hnew back_ps x1_var x1_std h1_ready h1T_ps h1T_sb gate_ps l1_ps l1_act l2_ps l2_act "
                 "lg_ready ex_ready mm_ready em_ready gates_ready gT_ps gT_sb l3_ps comb_done x2_var x2_std "
                 "h2_ready h2T_ps h2T_sb xt_ps hi_done r1_done mid_done r2_done lo_done table2_out").split()
        S = {n: sem("d_" + n) for n in names}
        L3_BANKS = ((1, 5, 2), (3, 4, 0))
        L1_BANKS = (5, 3, 4, 0, 1, 5)
        L2_BANKS = (3, 4, 0)

        def halves(w):
            return [(half, 2 * half, min(2, w - 2 * half)) for half in range((w + 1) // 2)]

        def pe_d1(pe, g, w):
            n = w * P
            pe.wait_ge(S["h4_ready"], g + 1)
            pe.wait_ge(S["hi_done"], CREDIT + 2 * g)
            pe.wait_ge(S["r1_done"], CREDIT + 2 * g)
            for c in range(C):
                for i in range(w):
                    last = nc.tensor.transpose(bank[3 + c][:, i * P:(i + 1) * P], h4[:, i, c * P:(c + 1) * P], ident[:, :])
            last.then_inc(S["hT_ps"], 1)
            pe.wait_ge(q1.evacuated, g * GW + w)
            for i in range(w):
                last = nc.tensor.transpose(bank[2][0:RELS, i * P:(i + 1) * P], red4[:, i, D:D + RELS], ident[:, :])
            last.then_inc(S["ct_ps"], 1)
            for c in range(C):
                for i in range(w):
                    nc.tensor.matmul(bank[c][:, i * P:(i + 1) * P], red4[:, i, c * P:(c + 1) * P], ident[:, :],
                                     start=i == 0, stop=False, skip_group_check=True)
            pe.wait_ge(S["ct_sb"], g + 1)
            for c in range(C):
                last = nc.tensor.matmul(bank[c][:, 0:n], relvec[:, c * P:(c + 1) * P], ctT[:, 0:n],
                                        start=False, stop=True, skip_group_check=True)
            last.then_inc(S["redT_ps"], 1)
            pe.wait_ge(S["hT_sb"], g + 1)
            pe.wait_ge(S["redT_sb"], g + 1)
            for c in range(C):
                b_r, b_z, b_in, b_hn = ((2, 5, 3, 4), (0, 1, 2, 5))[c]
                for gate, b, name in ((0, b_r, "r_ps"), (1, b_z, "z_ps")):
                    o = gate * D + c * P
                    for k in range(C):
                        nc.tensor.matmul(bank[b][:, 0:n], wihT[:, k, o:o + P], redT[:, k, 0:n], start=k == 0, stop=False)
                    for k in range(C):
                        last = nc.tensor.matmul(bank[b][:, 0:n], whhT[:, k, o:o + P], hT[:, k, 0:n],
                                                start=False, stop=k == C - 1)
                    last.then_inc(S[name], 1)
                o = 2 * D + c * P
                if c == 1:
                    pe.wait_ge(S["z_act"], 2 * g + 1)
                for k in range(C):
                    last = nc.tensor.matmul(bank[b_hn][:, 0:n], whhT[:, k, o:o + P], hT[:, k, 0:n],
                                            start=k == 0, stop=k == C - 1)
                last.then_inc(S["hn_ps"], 1)
                for k in range(C):
                    last = nc.tensor.matmul(bank[b_in][:, 0:n], wihT[:, k, o:o + P], redT[:, k, 0:n],
                                            start=k == 0, stop=k == C - 1)
                last.then_inc(S["in_ps"], 1)

        def pe_d2(pe, g, w):
            n = w * P
            pe.wait_ge(S["hnew"], 2 * g + 2)
            for i in range(w):
                for c in range(C):
                    o = (i % 2) * D + c * P
                    last = nc.tensor.transpose(bank[3 + i // 2][:, o:o + P], nT[:, c, i * P:(i + 1) * P], ident[:, :])
            last.then_inc(S["back_ps"], 1)

        def turn(g, w, b0, b1, ready, done, pe):
            pe.wait_ge(S[ready], g + 1)
            for c, b in enumerate((b0, b1)):
                for i in range(w):
                    last = nc.tensor.transpose(bank[b][:, i * P:(i + 1) * P], h4[:, i, c * P:(c + 1) * P], ident[:, :])
            last.then_inc(S[done], 1)

        def pe_d3(pe, g, w):
            n = w * P
            turn(g, w, 0, 1, "h1_ready", "h1T_ps", pe)
            pe.wait_ge(S["h1T_sb"], g + 1)
            for i in range(w):
                o = slice(i * E0, (i + 1) * E0)
                for c in range(C):
                    nc.tensor.matmul(bank[2][:, o], t0[:, c, i * P:(i + 1) * P], gW[:, c, :],
                                     start=i == 0 and c == 0, stop=False, skip_group_check=True)
                last = nc.tensor.matmul(bank[2][:, o], ones[0:1, :], gb[:, :], start=False, stop=True,
                                        skip_group_check=True)
            last.then_inc(S["gate_ps"], 1)
            for j, b in enumerate(L1_BANKS):
                if j == 5:
                    pe.wait_ge(S["l1_act"], 6 * g + 1)
                for c in range(C):
                    w1 = sW1[:, c, j * P:(j + 1) * P] if j < 2 else eW1[:, j - 2, c, :]
                    last = nc.tensor.matmul(bank[b][:, 0:n], w1, t0[:, c, 0:n], start=c == 0, stop=c == C - 1)
                last.then_inc(S["l1_ps"], 1)
            pe.wait_ge(S["l1_act"], 6 * g + 2)
            for c in range(C):
                last = nc.tensor.matmul(bank[3][:, 0:n], sW2[:, c, :], a1T[:, c, 0:n], start=c == 0, stop=c == C - 1)
            last.then_inc(S["l2_ps"], 1)
            for pair in range(2):
                pe.wait_ge(S["l1_act"], 6 * g + 4 + 2 * pair)
                for r in range(2):
                    e = 2 * pair + r
                    last = nc.tensor.matmul(bank[L2_BANKS[1 + pair]][r * 64:(r + 1) * 64, 0:n], eW2[:, e, :],
                                            a1T[:, 2 + e, 0:n], start=True, stop=True)
                last.then_inc(S["l2_ps"], 1)

        def pe_d4(pe, g, w):
            pe.wait_ge(S["gates_ready"], g + 1)
            for i in range(w):
                last = nc.tensor.transpose(bank[2][0:E0 + 1, i * P:(i + 1) * P], gate5[:, i, 0:E0 + 1], ident[:, :])
            last.then_inc(S["gT_ps"], 1)
            pe.wait_ge(S["gT_sb"], g + 1)
            pe.wait_ge(S["l2_act"], 3 * g + 3)
            for i in range(w):
                if i >= 2:
                    pe.wait_ge(S["comb_done"], GW * g + i - 1)
                b_s, b_02, b_13 = (bank[b] for b in L3_BANKS[i % 2])
                o = slice(i * P, (i + 1) * P)
                nc.tensor.matmul(b_s[:, 0:D], a2T[:, 0, o], sW3[:, :], start=True, stop=False)
                nc.tensor.matmul(b_s[:, 0:D], gT[:, o], b_l3[:, :], start=False, stop=True)
                for r, b in enumerate((b_02, b_13)):
                    for pair in range(2):
                        last = nc.tensor.matmul(b[:, pair * D:(pair + 1) * D], a2T[r * 64:(r + 1) * 64, 1 + pair, o],
                                                eW3[r * 64:(r + 1) * 64, pair, :], start=True, stop=True)
                last.then_inc(S["l3_ps"], 1)
            turn(g, w, 1, 5, "h2_ready", "h2T_ps", pe)
            pe.wait_ge(S["h2T_sb"], g + 1)
            for half, lo, k in halves(w):
                for i in range(lo, lo + k):
                    o = slice((i - lo) * D, (i - lo + 1) * D)
                    for c in range(C):
                        nc.tensor.matmul(bank[3 + half][:, o], t0[:, c, i * P:(i + 1) * P], gcnT[:, c, :],
                                         start=c == 0, stop=False)
                    last = nc.tensor.matmul(bank[3 + half][:, o], ones[0:1, :], gcn_b[:, :], start=False, stop=True)
                last.then_inc(S["xt_ps"], 1)

        def act_d1(act, g, w):
            n = w * P
            act.wait_ge(S["hT_ps"], g + 1)
            for c in range(C):
                last = nc.scalar.activation(hT[:, c, 0:n], bank[3 + c][:, 0:n], ACT.Copy)
            last.then_inc(S["hT_sb"], 1)
            act.wait_ge(S["ct_ps"], g + 1)
            nc.scalar.activation(ctT[:, 0:n], bank[2][0:RELS, 0:n], ACT.Copy).then_inc(S["ct_sb"], 1)
            for c in range(C):
                b_r, b_z = ((2, 5), (0, 1))[c]
                act.wait_ge(S["r_ps"], 2 * g + c + 1)
                nc.scalar.activation(rT[:, c, 0:n], bank[b_r][:, 0:n], ACT.Sigmoid,
                                     bias=brz[:, c:c + 1]).then_inc(S["r_act"], 1)
                act.wait_ge(S["z_ps"], 2 * g + c + 1)
                nc.scalar.activation(zT[:, c, 0:n], bank[b_z][:, 0:n], ACT.Sigmoid,
                                     bias=brz[:, 2 + c:3 + c]).then_inc(S["z_act"], 1)
            for c in range(C):
                act.wait_ge(S["t2_done"], 2 * g + c + 1)
                nc.scalar.activation(nT[:, c, 0:n], tT[:, c, 0:n], ACT.Tanh,
                                     bias=bih[:, 4 + c:5 + c]).then_inc(S["n_act"], 1)

        def act_d2(act, g, w):
            ln_sqrt(act, S["x1_var"], S["x1_std"], g, w)

        def act_turned(act, g, w, b0, b1, done_ps, done_sb, credit=0):
            act.wait_ge(S[done_ps], credit + g + 1)
            for c, b in enumerate((b0, b1)):
                last = nc.scalar.activation(t0[:, c, 0:w * P], bank[b][:, 0:w * P], ACT.Copy)
            last.then_inc(S[done_sb], 1)

        def act_d3(act, g, w):
            n = w * P
            act_turned(act, g, w, 0, 1, "h1T_ps", "h1T_sb")
            for j, b in enumerate(L1_BANKS):
                act.wait_ge(S["l1_ps"], 6 * g + j + 1)
                nc.scalar.activation(a1T[:, j, 0:n], bank[b][:, 0:n], ACT.Relu,
                                     bias=b_l1[:, j:j + 1]).then_inc(S["l1_act"], 1)
            for j, b in enumerate(L2_BANKS):
                act.wait_ge(S["l2_ps"], 3 * g + j + 1)
                nc.scalar.activation(a2T[:, j, 0:n], bank[b][:, 0:n], ACT.Relu,
                                     bias=b_l2[:, j:j + 1]).then_inc(S["l2_act"], 1)
            act.wait_ge(S["lg_ready"], g + 1)
            nc.scalar.activation(f0["ex"][:, 0:w, 0:E0], f0["lg"][:, 0:w, 0:E0], ACT.Exp).then_inc(S["ex_ready"], 1)
            act.wait_ge(S["mm_ready"], g + 1)
            nc.scalar.activation(f0["e"][:, 0:w], f0["m"][:, 0:w], ACT.Exp).then_inc(S["em_ready"], 1)

        def act_d4(act, g, w):
            n = w * P
            act.wait_ge(S["gT_ps"], g + 1)
            nc.scalar.activation(gT[:, 0:n], bank[2][0:E0 + 1, 0:n], ACT.Copy).then_inc(S["gT_sb"], 1)
            ln_sqrt(act, S["x2_var"], S["x2_std"], g, w)
            act_turned(act, g, w, 1, 5, "h2T_ps", "h2T_sb", CREDIT)
            act.wait_ge(S["table2_out"], 16 * g + 16)
            for half, lo, k in halves(w):
                act.wait_ge(S["xt_ps"], 2 * g + half + 1)
                nc.scalar.activation(part[:, lo:lo + k, 0:D],
                                     bank[3 + half][:, 0:k * D].rearrange("p (t d) -> p t d", d=D),
                                     ACT.Copy).then_inc(S["hi_done"], 1)
            for half, lo, k in halves(w):
                act.wait_ge(S["r1_done"], CREDIT + 2 * g + half + 1)
                nc.scalar.activation(part[:, lo:lo + k, D:2 * D], rest[:, half, 0:k, :],
                                     ACT.Copy).then_inc(S["mid_done"], 1)
            for half, lo, k in halves(w):
                act.wait_ge(S["r2_done"], 2 * g + half + 1)
                nc.scalar.activation(part[:, lo:lo + k, 2 * D:3 * D], rest[:, half, 0:k, :],
                                     ACT.Copy).then_inc(S["lo_done"], 1)
            act.wait_ge(S["lo_done"], CREDIT + 2 * g + len(halves(w)))
            act.dma_start(table2[ds(g * W, w * P), :].rearrange("(t p) d -> p t d", p=P),
                          part[:, 0:w, :]).then_inc(S["table2_out"], 16)

        def dve_d1(dve, chain, g, w):
            n = w * P
            chain.begin(g)
            dve.wait_ge(S["h2T_ps"], CREDIT + g)
            for i in range(w):
                t = g * GW + i
                last = nc.vector.tensor_scalar(h4[:, i, :], x_cols(t, 1), ln_mean[:, ds(t, 1)], ln_rstd[:, ds(t, 1)],
                                               ALU.subtract, ALU.mult)
            last.then_inc(S["h4_ready"], 1)
            dve.wait_ge(q1.evacuated, g * GW + w)
            chain.link(nc.vector.tensor_reduce(deg[:, 0:w], red4[:, 0:w, D:D + RELS], AX, ALU.add))
            chain.link(nc.vector.tensor_scalar(deg[:, 0:w], deg[:, 0:w], 1.0, None, ALU.add))
            nc.vector.reciprocal(inv_deg[:, ds(g * GW, w)], deg[:, 0:w])
            dve.wait_ge(S["redT_ps"], g + 1)
            for c in range(C):
                last = nc.vector.tensor_copy(redT[:, c, 0:n], bank[c][:, 0:n])
            last.then_inc(S["redT_sb"], 1)
            for c in range(C):
                b_in, b_hn = ((3, 4), (2, 5))[c]
                dve.wait_ge(S["hn_ps"], 2 * g + c + 1)
                dve.wait_ge(S["r_act"], 2 * g + c + 1)
                nc.vector.scalar_tensor_tensor(tT[:, c, 0:n], bank[b_hn][:, 0:n], bhh[:, 4 + c:5 + c], rT[:, c, 0:n],
                                               ALU.add, ALU.mult).then_inc(S["t1_done"], 1)
                dve.wait_ge(S["t1_done"], 2 * g + c + 1)
                dve.wait_ge(S["in_ps"], 2 * g + c + 1)
                nc.vector.tensor_tensor(tT[:, c, 0:n], tT[:, c, 0:n], bank[b_in][:, 0:n],
                                        ALU.add).then_inc(S["t2_done"], 1)
            for c in range(C):
                dve.wait_ge(S["n_act"], 2 * g + c + 1)
                chain.link(nc.vector.tensor_tensor(tT[:, c, 0:n], hT[:, c, 0:n], nT[:, c, 0:n], ALU.subtract))
                chain.link(nc.vector.tensor_tensor(tT[:, c, 0:n], tT[:, c, 0:n], zT[:, c, 0:n], ALU.mult))
                nc.vector.tensor_tensor(nT[:, c, 0:n], nT[:, c, 0:n], tT[:, c, 0:n], ALU.add).then_inc(S["hnew"], 1)

        def dve_d2(dve, chain, g, w):
            dve.wait_ge(S["back_ps"], g + 1)
            for half, lo, k in halves(w):
                xs = x_cols(g * GW + lo, k)
                last = nc.vector.tensor_tensor(xs, xs, bank[3 + half][:, 0:k * D], ALU.add)
            chain.link(last)
            ln_stats(dve, chain, S["x1_var"], S["x1_std"], g, w)
            ln_apply(g, w).then_inc(S["h1_ready"], 1)

        def dve_d3(dve, chain, g, w):
            dve.wait_ge(S["gate_ps"], g + 1)
            router_logits(f0, chain, bank[2][:, 0:w * E0], w, E0).then_inc(S["lg_ready"], 1)
            dve.wait_ge(S["ex_ready"], g + 1)
            router_choice(f0, chain, w, E0)
            m1, m2, w1, w2, e = (f0[k][:, 0:w] for k in ("m1", "m2", "w1", "w2", "e"))
            nc.vector.tensor_tensor(f0["m"][:, 0:w], m2, m1, ALU.subtract).then_inc(S["mm_ready"], 1)
            dve.wait_ge(S["em_ready"], g + 1)
            chain.link(nc.vector.tensor_scalar(w1, e, 1.0, None, ALU.add))
            chain.link(nc.vector.reciprocal(w1, w1))
            chain.link(nc.vector.tensor_tensor(w2, e, w1, ALU.mult))
            eq1, eq2 = (f0[k][:, 0:w, 0:E0] for k in ("eq1", "eq2"))
            wide = [v.unsqueeze(2).to_broadcast([P, w, E0]) for v in (w1, w2)]
            chain.link(nc.vector.tensor_tensor(eq1, eq1, wide[0], ALU.mult))
            chain.link(nc.vector.tensor_tensor(eq2, eq2, wide[1], ALU.mult))
            nc.vector.memset(gate5[:, 0:w, E0:E0 + 1], 1.0)
            chain.link(nc.vector.tensor_tensor(gate5[:, 0:w, 0:E0], eq1, eq2, ALU.add))
            dve.sem_inc(S["gates_ready"], 1)

        def dve_d4(dve, chain, g, w):
            for i in range(w):
                dve.wait_ge(S["l3_ps"], GW * g + i + 1)
                b_s, b_02, b_13 = (bank[b] for b in L3_BANKS[i % 2])
                xs = x_cols(g * GW + i, 1)
                chain.link(nc.vector.tensor_tensor(xs, xs, b_s[:, 0:D], ALU.add))
                for e in range(E0):
                    b = (b_02, b_13)[e % 2][:, (e // 2) * D:(e // 2 + 1) * D]
                    last = nc.vector.scalar_tensor_tensor(xs, b, gate5[:, i, e:e + 1], xs, ALU.mult, ALU.add)
                    if e < E0 - 1:
                        chain.link(last)
                last.then_inc(S["comb_done"], 1)
                if w < GW:
                    dve.sem_inc(S["comb_done"], GW - w)
            dve.wait_ge(S["comb_done"], GW * g + GW)
            ln_stats(dve, chain, S["x2_var"], S["x2_std"], g, w)
            ln_apply(g, w).then_inc(S["h2_ready"], 1)
            for half, lo, k in halves(w):
                dve.wait_ge(S["hi_done"], CREDIT + 2 * g + half + 1)
                dve.wait_ge(S["lo_done"], CREDIT + 2 * g)
                nc.vector.tensor_tensor(rest[:, half, 0:k, :], bank[3 + half][:, 0:k * D].rearrange("p (t d) -> p t d", d=D),
                                        part[:, lo:lo + k, 0:D], ALU.subtract).then_inc(S["r1_done"], 1)
            for half, lo, k in halves(w):
                dve.wait_ge(S["mid_done"], 2 * g + half + 1)
                nc.vector.tensor_tensor(rest[:, half, 0:k, :], rest[:, half, 0:k, :],
                                        part[:, lo:lo + k, D:2 * D], ALU.subtract).then_inc(S["r2_done"], 1)
            chain.end()

        def evacuate1(dve, g, i):
            t = g * GW + i
            if not (isinstance(g, int) and g == 0):
                dve.wait_ge(S["redT_ps"], g)
            dve.wait_ge(q1.done, t + 1)
            nc.vector.tensor_copy(red4[:, i, :], bank[6 + i % 2][:, 0:D + RELS]).then_inc(q1.evacuated, 1)

        def run_graph(eng, gather, steps):
            for i in range(GW):
                gather(0, i)
            with eng.Fori(1, GROUPS) as g:
                for i in range(GW):
                    steps[i](g - 1, GW)
                    gather(g, i)
            for i in range(GW):
                steps[i](GROUPS - 1, GW)
                if i == 0:
                    gather(GROUPS, 0)
            for i in range(GW):
                steps[i](GROUPS, 1)

        with nc.Block() as block:
            @block.gpsimd
            def _(pool):
                pool_begin(pool, q1, 0)
                total_rounds = rounds_value(pool, NT, 1)
                pool_rounds(pool, q1, 0, total_rounds)
                pool_end(pool, q1, total_rounds)

            @block.tensor
            def _(pe):
                pe.sem_inc(q1.used, M)
                pe.sem_inc(S["h2T_ps"], CREDIT)
                run_graph(pe, lambda g, i: pe_windows(pe, q1, g, i),
                          [lambda g, w, f=f: f(pe, g, w) for f in (pe_d1, pe_d2, pe_d3, pe_d4)])

            @block.scalar
            def _(act):
                act.sem_inc(S["hi_done"], CREDIT)
                act.sem_inc(S["lo_done"], CREDIT)
                act.dma_start(spare[:, 1:2], zeros[:, 0:1], allow_slow_non_contiguous=True).then_inc(S["table2_out"], 16)
                run_graph(act, lambda g, i: None,
                          [lambda g, w, f=f: f(act, g, w) for f in (act_d1, act_d2, act_d3, act_d4)])
                act.wait_ge(S["table2_out"], 16 * (GROUPS + 2))

            @block.vector
            def _(dve):
                chain = Chain(dve, "layer0_chain", 64)
                dve.sem_inc(S["r1_done"], CREDIT)

                def gather(g, i):
                    dve_window(dve, q1, g * GW + i)
                    evacuate1(dve, g, i)

                run_graph(dve, gather,
                          [lambda g, w, f=f: f(dve, chain, g, w) for f in (dve_d1, dve_d2, dve_d3, dve_d4)])

            @block.sync
            def _(sp):
                sp_indices(sp, q1)

        f1 = router_buffers("f1", graph)
        chosen = sb("chosen", [P, GW, E1], F32, graph)
        rank = sb("rank", [P, GW, E1], F32, graph)
        total = sb("total", [P, GW, E1], F32, graph)
        region = sb("region", [P, E1], F32, graph)
        count = sb("count", [P, E1], F32, graph)
        pos_f = sb("pos_f", [P, GW, 2], F32, graph)
        pos = sb("pos", [P, 2 * GW], I32, graph)
        xr = sb("xr", [P, GW, 2, RW], F32, graph)
        q2 = Gather("g2", table2, False)
        names = ("var std xn_ready xnT_ps xnT_sb logit_ps lg_ready ex_ready chosen_ready rank_ps pos_ready "
                 "scattered").split()
        R = {n: sem("r_" + n) for n in names}

        def pe_e1(pe, g, w):
            n = w * P
            pe.wait_ge(R["xn_ready"], g + 1)
            for c in range(C):
                for i in range(w):
                    last = nc.tensor.transpose(bank[c][:, i * P:(i + 1) * P], xr[:, i, 0, c * P:(c + 1) * P],
                                               ident[:, :])
            last.then_inc(R["xnT_ps"], 1)
            pe.wait_ge(R["xnT_sb"], g + 1)
            for i in range(w):
                o = slice(i * E1, (i + 1) * E1)
                for c in range(C):
                    nc.tensor.matmul(bank[2][:, o], t0[:, c, i * P:(i + 1) * P], Wr[:, c, :],
                                     start=i == 0 and c == 0, stop=False, skip_group_check=True)
                last = nc.tensor.matmul(bank[2][:, o], ones[0:1, :], br[:, :], start=False, stop=True,
                                        skip_group_check=True)
            last.then_inc(R["logit_ps"], 1)

        def pe_e2(pe, g, w):
            flat = chosen[:, 0:w, :].rearrange("p t e -> p (t e)")
            pe.wait_ge(R["chosen_ready"], g + 1)
            nc.tensor.matmul(bank[3][:, 0:w * E1], ustrict[:, :], flat, start=True, stop=True)
            nc.tensor.matmul(bank[4][:, 0:w * E1], ones[:, :], flat, start=True, stop=True).then_inc(R["rank_ps"], 1)

        def act_e1(act, g, w):
            n = w * P
            ln_sqrt(act, R["var"], R["std"], g, w)
            act.wait_ge(R["xnT_ps"], g + 1)
            for c in range(C):
                last = nc.scalar.activation(t0[:, c, 0:n], bank[c][:, 0:n], ACT.Copy)
            last.then_inc(R["xnT_sb"], 1)
            act.wait_ge(R["lg_ready"], g + 1)
            nc.scalar.activation(f1["ex"][:, 0:w, :], f1["lg"][:, 0:w, :], ACT.Exp).then_inc(R["ex_ready"], 1)

        def dve_e1(dve, chain, g, w):
            chain.begin(g)
            dve.wait_ge(q2.evacuated, g * GW + w)
            ln_stats(dve, chain, R["var"], R["std"], g, w)
            dve.wait_ge(R["scattered"], ROWS_SCATTERED * g + 16)
            for i in range(w):
                t = g * GW + i
                for s_ in range(2):
                    nc.vector.tensor_scalar(xr[:, i, s_, 0:D], x_cols(t, 1), mean_var[:, i, 0:1], rstd[:, i:i + 1],
                                            ALU.subtract, ALU.mult)
            last = nc.vector.tensor_copy(xr[:, 0:w, :, D:RW].bitcast(I32),
                                         place[:, ds(g * GW * 2, w * 2)].rearrange("p (t s a) -> p t s a", s=2, a=1))
            last.then_inc(R["xn_ready"], 1)
            dve.wait_ge(R["logit_ps"], g + 1)
            router_logits(f1, chain, bank[2][:, 0:w * E1], w, E1).then_inc(R["lg_ready"], 1)

        def dve_e2(dve, chain, g, w):
            dve.wait_ge(R["ex_ready"], g + 1)
            router_choice(f1, chain, w, E1)
            m1, m2, s = (f1[k][:, 0:w] for k in ("m1", "m2", "s"))
            chain.link(nc.vector.tensor_tensor(s, m1, m2, ALU.add))
            chain.link(nc.vector.reciprocal(s, s))
            wts = row_wt[:, ds(g * GW * 2, w * 2)].rearrange("p (t s) -> p t s", s=2)
            nc.vector.tensor_tensor(wts[:, :, 0], m1, s, ALU.mult)
            nc.vector.tensor_tensor(wts[:, :, 1], m2, s, ALU.mult)
            eq = [f1[k][:, 0:w, :] for k in ("eq1", "eq2")]
            nc.vector.tensor_tensor(chosen[:, 0:w, :], eq[0], eq[1], ALU.add).then_inc(R["chosen_ready"], 1)
            dve.wait_ge(R["rank_ps"], g + 1)
            nc.vector.tensor_copy(rank[:, 0:w, :], bank[3][:, 0:w * E1].rearrange("p (t e) -> p t e", e=E1))
            chain.link(nc.vector.tensor_copy(total[:, 0:w, :], bank[4][:, 0:w * E1].rearrange("p (t e) -> p t e", e=E1)))
            for i in range(w):
                nc.vector.tensor_tensor(rank[:, i, :], rank[:, i, :], count[:, :], ALU.add)
                chain.link(nc.vector.tensor_tensor(count[:, :], count[:, :], total[:, i, :], ALU.add))
            for s_ in range(2):
                chain.link(nc.vector.tensor_tensor(eq[s_], eq[s_], rank[:, 0:w, :], ALU.mult))
                chain.link(nc.vector.tensor_reduce(pos_f[:, 0:w, s_], eq[s_], AX, ALU.add))
            flat = pos_f[:, 0:w, :].rearrange("p t s -> p (t s)")
            nc.vector.tensor_copy(pos[:, 0:2 * w], flat).then_inc(R["pos_ready"], 1)
            chain.end()

        def evacuate2(dve, g, i):
            t = g * GW + i
            dve.wait_ge(q2.done, t + 1)
            xs = x_cols(t, 1)
            nc.vector.scalar_tensor_tensor(xs, bank[6 + i % 2][:, 0:D], inv_deg[:, ds(t, 1)], xs,
                                           ALU.mult, ALU.add).then_inc(q2.evacuated, 1)

        def scatter(pool, g, w):
            pool.wait_ge(R["pos_ready"], g + 1)
            settled(pool)
            for i in range(w):
                for s_ in range(2):
                    nc.gpsimd.indirect_dma_start(
                        out=routed, out_offset=bass.IndirectOffsetOnAxis(pos[:, 2 * i + s_:2 * i + s_ + 1], axis=0),
                        in_=xr[:, i, s_, :], in_offset=None).then_inc(R["scattered"], 16)

        ROWS_SCATTERED = 16 * 2 * GW

        def nothing(g, w):
            return None

        with nc.Block() as block:
            @block.gpsimd
            def _(pool):
                pool.dma_start(spare[:, 3:4], zeros[:, 0:1], allow_slow_non_contiguous=True).then_inc(R["scattered"], 16)
                pool_begin(pool, q2, 2)
                pool_rounds(pool, q2, 0, rounds_value(pool, GW, 1))
                with pool.Fori(1, GROUPS) as g:
                    pool_rounds(pool, q2, rounds_value(pool, g * GW, 1), rounds_value(pool, g * GW + GW, 2))
                    scatter(pool, g - 1, GW)
                done_rounds = rounds_value(pool, NT - 1, 1)
                total_rounds = rounds_value(pool, NT, 1)
                with pool.If(total_rounds > done_rounds):
                    pool_rounds(pool, q2, done_rounds, total_rounds)
                pool_end(pool, q2, total_rounds)
                scatter(pool, GROUPS - 1, GW)
                scatter(pool, GROUPS, 1)
                pool.wait_ge(R["scattered"], ROWS_SCATTERED * GROUPS + 16 * 3)

            @block.sync
            def _(sp):
                sp_indices(sp, q2)

            @block.tensor
            def _(pe):
                pe.sem_inc(q2.used, M)
                steps = [lambda g, w: pe_e1(pe, g, w), lambda g, w: pe_e2(pe, g, w), nothing, nothing]
                run_graph(pe, lambda g, i: pe_windows(pe, q2, g, i), steps)

            @block.scalar
            def _(act):
                run_graph(act, lambda g, i: None, [lambda g, w: act_e1(act, g, w), nothing, nothing, nothing])

            @block.vector
            def _(dve):
                start = Chain(dve, "count_chain", 32)
                start.begin(0)
                start.link(nc.vector.tensor_scalar(region[:, :], ts_idx[:, 0, :], float(CAP), None, ALU.mult))
                start.link(nc.vector.tensor_copy(count[:, :], region[:, :]))
                chain = Chain(dve, "layer1_chain", 64)

                def gather(g, i):
                    dve_window(dve, q2, g * GW + i)
                    evacuate2(dve, g, i)

                run_graph(dve, gather, [lambda g, w: dve_e1(dve, chain, g, w), lambda g, w: dve_e2(dve, chain, g, w),
                                        nothing, nothing])
                rows_i, tiles_i = lists[0:1, 0:E1], lists[0:1, E1:2 * E1]
                start.link(nc.vector.tensor_tensor(rows_i, count[0:1, :], region[0:1, :], ALU.subtract))
                start.link(nc.vector.tensor_scalar(tiles_i, rows_i, float(TT - 1), float(TT), ALU.add, ALU.max))
                start.link(nc.vector.tensor_single_scalar(tiles_i, tiles_i, TT.bit_length() - 1, ALU.arith_shift_right))
                start.link(nc.vector.memset(lists[0:1, 2 * E1:2 * E1 + 1], 0))
                for e in range(E1):
                    start.link(nc.vector.tensor_tensor(lists[0:1, 2 * E1 + e + 1:2 * E1 + e + 2],
                                                       lists[0:1, 2 * E1 + e:2 * E1 + e + 1],
                                                       lists[0:1, E1 + e:E1 + e + 1], ALU.add))

        graph.close()
        ffn = ctx.enter_context(ExitStack())
        W1 = [sb(f"W1_{b}", [P, C, H], F32, ffn) for b in range(2)]
        W2 = [sb(f"W2_{b}", [P, HC, D], F32, ffn) for b in range(2)]
        b1 = [sb(f"b1_{b}", [P, HC], F32, ffn) for b in range(2)]
        b2 = [sb(f"b2_{b}", [1, D], F32, ffn) for b in range(2)]
        lng = [sb(f"lng_{b}", [P, 2 * C], F32, ffn) for b in range(2)]
        xs = sb("xs", [P, SUB, RW], F32, ffn)
        to = sb("to", [P, SUB], I32, ffn)
        xeT = sb("xeT", [P, C, TT], F32, ffn)
        hidT = sb("hidT", [P, HC, TT], F32, ffn)
        ys = sb("ys", [P, SUB, D], F32, ffn)
        w_loaded = [sem(f"w_loaded{b}") for b in range(2)]
        names = "tail_done to_ready xs_loaded xs_turned xeT_ready g1_ps gelu_done y_ps y_ready y_out expert_done".split()
        X = {n: sem("x_" + n) for n in names}
        WLOADS = 6

        def expert_tiles(eng, body, before_expert=None):
            with eng.Fori(0, E1 // 2) as pair:
                for b in range(2):
                    e = pair * 2 + b
                    if before_expert:
                        before_expert(b, e)
                    tiles = eng.value_load(lists[0:1, ds(e + E1, 1)], min_val=1, max_val=NPAD // TT + 1)
                    first = eng.value_load(lists[0:1, ds(e + 2 * E1, 1)], min_val=0, max_val=E1 * (NPAD // TT + 1))
                    with eng.Fori(0, tiles) as j:
                        body(b, e, j, eng.snap(first + j))

        with nc.Block() as block:
            @block.sync
            def _(sp):
                with sp.Fori(0, E1) as e:
                    rows_ = sp.value_load(lists[0:1, ds(e, 1)], min_val=0, max_val=NPAD)
                    at = narrow(rows_ + e * CAP, 0, E1 * CAP - TT)
                    sp.dma_start(routed[ds(at, TT), :].rearrange("(p s) d -> p s d", p=P),
                                 filler[:, :, :]).then_inc(X["tail_done"], 16)
                sp.wait_ge(X["tail_done"], 16 * E1)

                def load(b, e, j, n):
                    sp.wait_ge(X["xs_turned"], n + CREDIT)
                    sp.wait_ge(X["to_ready"], n + CREDIT)
                    at = narrow(e * CAP + j * TT, 0, E1 * CAP - TT)
                    sp.dma_start(xs[:, :, :],
                                 routed[ds(at, TT), :].rearrange("(p s) d -> p s d", p=P)).then_inc(X["xs_loaded"], 16)

                expert_tiles(sp, load)

            @block.gpsimd
            def _(pool):
                def load_expert(b, e):
                    loads = ((W1[b][:, :, :], a["L1_ffn_W1"][ds(e, 1), :, :].rearrange("a (c p) h -> p (a c) h", p=P)),
                             (W2[b][:, :, :], a["L1_ffn_W2"][ds(e, 1), :, :].rearrange("a (c p) h -> p (a c) h", p=P)),
                             (b1[b][:, :], a["L1_ffn_b1"][ds(e, 1), :].rearrange("a (c p) -> p (a c)", p=P)),
                             (b2[b][:, :], a["L1_ffn_b2"][ds(e, 1), :]),
                             (lng[b][:, 0:C], a["L1_ffn_ln_g"][ds(e, 1), :].rearrange("a (c p) -> p (a c)", p=P)),
                             (lng[b][:, C:2 * C], a["L1_ffn_ln_b"][ds(e, 1), :].rearrange("a (c p) -> p (a c)", p=P)))
                    assert len(loads) == WLOADS
                    for dst, src in loads:
                        pool.dma_start(dst, src, allow_slow_non_contiguous=True).then_inc(w_loaded[b], 16)

                load_expert(0, 0)
                load_expert(1, 1)
                for s in range(SUB):
                    pool.dma_start(results[2 * NPAD + s * P:2 * NPAD + (s + 1) * P, :],
                                   filler[:, s, 0:D]).then_inc(X["y_out"], 16)

                def next_expert(b, e):
                    pool.wait_ge(X["expert_done"], e + CREDIT)
                    settled(pool)
                    if b == 0:
                        with pool.If(e > 0):
                            load_expert(1, narrow(e + 1, 1, E1 - 1))
                    else:
                        with pool.If(e < E1 - 1):
                            load_expert(0, narrow(e + 1, 1, E1 - 1))

                def store(b, e, j, n):
                    for s in range(SUB):
                        pool.wait_ge(X["y_ready"], CREDIT + SUB * n + s + 1)
                        settled(pool)
                        nc.gpsimd.indirect_dma_start(
                            out=results, out_offset=bass.IndirectOffsetOnAxis(to[:, s:s + 1], axis=0),
                            in_=ys[:, s, :], in_offset=None).then_inc(X["y_out"], 16)

                expert_tiles(pool, store, next_expert)
                tiles = pool.value_load(lists[0:1, 3 * E1:3 * E1 + 1], min_val=E1, max_val=E1 * (NPAD // TT + 1))
                pool.wait_ge(X["y_out"], tiles * (16 * SUB) + 16 * SUB)

            @block.tensor
            def _(pe):
                def weights_here(b, e):
                    pe.wait_ge(w_loaded[b], (e - b) * (8 * WLOADS) + 16 * WLOADS)

                def tile(b, e, j, n):
                    pe.wait_ge(X["xs_loaded"], n * 16 + 16)
                    pe.wait_ge(X["xeT_ready"], n + CREDIT)
                    for c in range(C):
                        for s in range(SUB):
                            o = c * TT + s * P
                            last = nc.tensor.transpose(bank[0][:, o:o + P], xs[:, s, c * P:(c + 1) * P],
                                                       ident[:, :])
                    last.then_inc(X["xs_turned"], 1)
                    pe.wait_ge(X["xeT_ready"], CREDIT + n + 1)
                    for hc in range(HC):
                        if hc % 2 == 0:
                            pe.wait_ge(X["gelu_done"], n * HC + hc + 2)
                        o = (hc % 2) * TT
                        for c in range(C):
                            last = nc.tensor.matmul(bank[1 + hc // 2][:, o:o + TT], W1[b][:, c, hc * P:(hc + 1) * P],
                                                    xeT[:, c, :], start=c == 0, stop=c == C - 1)
                        if hc % 2 == 1:
                            last.then_inc(X["g1_ps"], 1)
                    for s in range(SUB):
                        pe.wait_ge(X["y_ready"], n * SUB + s + CREDIT)
                        for hc in range(HC):
                            if s == 0:
                                pe.wait_ge(X["gelu_done"], n * HC + HC + hc + 1)
                            nc.tensor.matmul(bank[5 + s][:, 0:D], hidT[:, hc, s * P:(s + 1) * P], W2[b][:, hc, :],
                                             start=hc == 0, stop=False)
                        nc.tensor.matmul(bank[5 + s][:, 0:D], ones[0:1, :], b2[b][:, :], start=False,
                                         stop=True).then_inc(X["y_ps"], 1)

                pe.sem_inc(X["xs_turned"], CREDIT)
                pe.sem_inc(X["expert_done"], CREDIT)
                with pe.Fori(0, E1 // 2) as pair:
                    for b in range(2):
                        e = pair * 2 + b
                        weights_here(b, e)
                        tiles = pe.value_load(lists[0:1, ds(e + E1, 1)], min_val=1, max_val=NPAD // TT + 1)
                        first = pe.value_load(lists[0:1, ds(e + 2 * E1, 1)], min_val=0, max_val=E1 * (NPAD // TT + 1))
                        with pe.Fori(0, tiles) as j:
                            tile(b, e, j, pe.snap(first + j))
                        nc.tensor.matmul(bank[7][:, 0:P], zeros[:, 0:P], zeros[:, 0:P], start=True,
                                         stop=True).then_inc(X["expert_done"], 1)

            @block.scalar
            def _(act):
                act.sem_inc(X["gelu_done"], HC)

                def tile(b, e, j, n):
                    for hc in range(HC):
                        if hc % 2 == 0:
                            act.wait_ge(X["g1_ps"], n * (HC // 2) + hc // 2 + 1)
                        o = (hc % 2) * TT
                        nc.scalar.activation(hidT[:, hc, :], bank[1 + hc // 2][:, o:o + TT], ACT.Gelu,
                                             bias=b1[b][:, hc:hc + 1]).then_inc(X["gelu_done"], 1)

                expert_tiles(act, tile, lambda b, e: act.wait_ge(w_loaded[b], (e - b) * (8 * WLOADS) + 16 * WLOADS))

            @block.vector
            def _(dve):
                def tile(b, e, j, n):
                    dve.wait_ge(X["xs_turned"], CREDIT + n + 1)
                    for c in range(C):
                        last = nc.vector.tensor_scalar(xeT[:, c, :], bank[0][:, c * TT:(c + 1) * TT], lng[b][:, c:c + 1],
                                                       lng[b][:, C + c:C + c + 1], ALU.mult, ALU.add)
                    last.then_inc(X["xeT_ready"], 1)
                    dve.wait_ge(X["y_out"], n * (16 * SUB) + 16 * SUB)
                    dve.wait_ge(X["xs_loaded"], n * 16 + 16)
                    nc.vector.tensor_copy(to[:, :], xs[:, :, D].bitcast(I32)).then_inc(X["to_ready"], 1)
                    for s in range(SUB):
                        dve.wait_ge(X["y_ps"], n * 2 + s + 1)
                        nc.vector.tensor_copy(ys[:, s, :], bank[5 + s][:, 0:D]).then_inc(X["y_ready"], 1)

                for name in ("xeT_ready", "to_ready", "y_ready"):
                    dve.sem_inc(X[name], CREDIT)
                expert_tiles(dve, tile, lambda b, e: dve.wait_ge(w_loaded[b], (e - b) * (8 * WLOADS) + 16 * WLOADS))
        ffn.close()

        comb = ctx.enter_context(ExitStack())
        y = [sb(f"y{b}", [P, GW, 2 * D], F32, comb) for b in range(2)]
        y_landed = [sem(f"y_landed{b}") for b in range(2)]
        c_half, c_used, c_out = (sem("c_" + n) for n in ("half", "used", "out"))

        def all_groups(eng, body):
            with eng.Fori(0, GROUPS // 2) as pair:
                for b in range(2):
                    body(pair * 2 + b, b, pair, GW)
            body(GROUPS, 0, GROUPS // 2, 1)

        assert GROUPS % 2 == 0

        with nc.Block() as block:
            @block.scalar
            def _(act):
                def load(g, b, pair, w):
                    act.wait_ge(c_used, g * GW + GW)
                    act.dma_start(y[b][:, 0:w, :],
                                  results[ds(g * (2 * W), w * 2 * P), :].rearrange("(t p s) d -> p t (s d)", p=P, s=2)
                                  ).then_inc(y_landed[b], 16)

                all_groups(act, load)

            @block.vector
            def _(dve):
                dve.sem_inc(c_used, 2 * GW)

                def group(g, b, pair, w):
                    dve.wait_ge(y_landed[b], pair * 16 + 16)
                    for s in range(2):
                        for i in range(w):
                            t = g * GW + i
                            if s == 1 and i == 0:
                                dve.wait_ge(c_half, g + 1)
                            last = nc.vector.scalar_tensor_tensor(
                                x_cols(t, 1), y[b][:, i, s * D:(s + 1) * D], row_wt[:, ds(t * 2 + s, 1)], x_cols(t, 1),
                                ALU.mult, ALU.add)
                            if s == 1:
                                last.then_inc(c_used, 1)
                        if s == 0:
                            last.then_inc(c_half, 1)

                all_groups(dve, group)

            @block.sync
            def _(sp):
                with sp.Fori(0, GROUPS) as g:
                    sp.wait_ge(c_used, g * GW + 3 * GW)
                    sp.dma_start(out[ds(g * W, W), :].rearrange("(t p) d -> p t d", p=P),
                                 x_cols(g * GW, GW).rearrange("p (t d) -> p t d", d=D)).then_inc(c_out, 16)
                sp.wait_ge(c_used, NT + 2 * GW)
                sp.dma_start(out[GROUPS * W:N, :], x_res[0:N - GROUPS * W, (NT - 1) * D:NT * D]).then_inc(c_out, 16)
                sp.wait_ge(c_out, 16 * (GROUPS + 1))


_INS = ["x", "src", "dst", "edge_type_16", "L0_gnn_relvectors", "L0_gnn_w_ih", "L0_gnn_w_hh", "L0_gnn_b_ih",
        "L0_gnn_b_hh", "L0_ffn_sW1", "L0_ffn_sb1", "L0_ffn_sW2", "L0_ffn_sb2", "L0_ffn_sW3", "L0_ffn_sb3",
        "L0_ffn_eW1", "L0_ffn_eb1", "L0_ffn_eW2", "L0_ffn_eb2", "L0_ffn_eW3", "L0_ffn_eb3", "L0_ffn_gW",
        "L0_ffn_gb", "L1_gnn_W", "L1_gnn_b", "L1_ffn_Wr", "L1_ffn_br", "L1_ffn_ln_g", "L1_ffn_ln_b",
        "L1_ffn_W1", "L1_ffn_b1", "L1_ffn_W2", "L1_ffn_b2"]


def kernel(**inputs):
    import numpy as _np
    import concourse.bacc as _bacc
    from concourse import mybir as _mybir
    from concourse.bass_utils import run_bass_kernel_spmd as _run

    nc = _bacc.Bacc("TRN2", target_bir_lowering=False, num_devices=1)
    arrays, args = {}, {}
    for name in _INS:
        v = _np.ascontiguousarray(inputs[name])
        arrays[f"in_{name}_dram"] = v
        args[name] = nc.dram_tensor(f"in_{name}_dram", v.shape, _mybir.dt.from_np(v.dtype), kind="ExternalInput").ap()
    out = nc.dram_tensor("out_0_dram", (N, D), _mybir.dt.float32, kind="ExternalOutput").ap()
    program(nc, args, out)
    r = _run(nc, [arrays], core_ids=[0])
    return r.results[0]["out_0_dram"]
```

```python
from contextlib import ExitStack

import concourse.bass as bass
from concourse import mybir

F32 = mybir.dt.float32
BF16 = mybir.dt.bfloat16
FR = mybir.dt.float32r
I32 = mybir.dt.int32
ALU = mybir.AluOpType
ACT = mybir.ActivationFunctionType
AX = mybir.AxisListType.X
ds = bass.ds

P = 128
N = 6250
D = 256
C = D // P
NE = 100000
RELS = 16
NT = (N + P - 1) // P
NPAD = NT * P
GW = 4
GROUPS = NT // GW
W = GW * P
EP, EJ = 112, 7
CHUNKS = EP * EJ
U = 4
M = 4
MH = 8
KCOLS = CHUNKS + U
PARTS = 3
BIG = float(1 << 20)
EPS = 1e-5
H = 1024
HC = H // P
E0 = 4
E1 = 8
TT = 256
SUB = TT // P
CAP = NPAD + TT
RW = D + 1
CREDIT = 1
LOOP = "the loop's bounds and the edge windows keep it inside"


def program(nc, a, out):
    assert NT == GROUPS * GW + 1 and EP * EJ * P >= NE

    def narrow(value, low, high):
        return nc.s_assert_within(value, low, high, skip_runtime_bounds_check_because=LOOP)

    with ExitStack() as ctx:
        def sem(name):
            return ctx.enter_context(nc.semaphore(name))

        def sb(name, shape, dt, where=None):
            return (where or ctx).enter_context(nc.sbuf_tensor(name, shape, dt))

        bank = [ctx.enter_context(nc.psum_tensor(f"bank{i}", [P, 512], F32)) for i in range(8)]

        table1 = nc.dram_tensor("table1", (NPAD, PARTS * D), BF16).ap()
        table2 = nc.dram_tensor("table2", (NPAD, PARTS * D), BF16).ap()
        routed = nc.dram_tensor("routed", (E1 * CAP, RW), F32).ap()
        results = nc.dram_tensor("results", (2 * NPAD + TT, D), F32).ap()

        x_res = sb("x_res", [P, NT * D], F32)
        ident = sb("ident", [P, P], F32)
        ustrict = sb("ustrict", [P, P], F32)
        ones = sb("ones", [P, P], F32)
        eps = sb("eps", [P, 1], F32)
        zeros = sb("zeros", [P, W], F32)
        inv_deg = sb("inv_deg", [P, NT], F32)
        row_wt = sb("row_wt", [P, NT * 2], F32)
        place = sb("place", [P, NT * 2], I32)
        filler = sb("filler", [P, SUB, RW], F32)
        lists = sb("lists", [1, 3 * E1 + 1], I32)
        ts_idx = sb("ts_idx", [P, GW, E1], F32)

        def x_cols(first, count):
            return x_res[:, ds(first * D, count * D)]

        graph = ctx.enter_context(ExitStack())
        dstT = sb("dstT", [P, KCOLS], F32, graph)
        typeT = sb("typeT", [P, KCOLS], F32, graph)
        srcT = sb("srcT", [P, KCOLS], I32, graph)
        windows = sb("windows", [1, 3 * NT], I32, graph)
        rounds = sb("rounds", [1, NT + 1], I32, graph)
        early = sb("early", [1, NT], I32, graph)
        tbase = sb("tbase", [P, NT], F32, graph)
        iota_row = sb("iota_row", [P, P], BF16, graph)
        zlhs = zeros[:, 0:P // 2].bitcast(BF16)
        zrhs = zeros[:, 0:2 * D // 2].bitcast(BF16)
        rows = sb("rows", [P, M * U, PARTS * D], BF16, graph)
        onehot = sb("onehot", [P, MH * U, P], BF16, graph)
        typehot = sb("typehot", [P, MH * U, RELS], BF16, graph)
        idx = sb("idx", [P, M * U], I32, graph)
        spare = sb("spare", [P, 4], F32, graph)
        h4 = sb("h4", [P, GW, D], F32, graph)
        stats = sb("stats", [P, GW, 6], F32, graph)
        mean_var = sb("mean_var", [P, GW, 2], F32, graph)
        stdev = sb("stdev", [P, GW], F32, graph)
        rstd = sb("rstd", [P, GW], F32, graph)
        part = sb("part", [P, GW, PARTS * D], BF16, graph)
        rest = sb("rest", [P, 2, 2, D], F32, graph)
        ln_mean = sb("ln_mean", [P, NT], F32, graph)
        ln_rstd = sb("ln_rstd", [P, NT], F32, graph)
        t0 = sb("t0", [P, C, W], F32, graph)

        consts_ready = sem("consts_ready")
        filler_clear = sem("filler_clear")
        loads_done = sem("loads_done")
        x_loaded = sem("x_loaded")
        x_tail_loaded = sem("x_tail_loaded")

        waits_passed = sem("waits_passed")

        def settled(eng):
            eng.sem_inc(waits_passed, 1)

        class Chain:

            def __init__(self, eng, name, per):
                self.eng, self.sem, self.per = eng, sem(name), per

            def begin(self, round_):
                base = round_ * self.per
                self.base, self.n = base if isinstance(base, int) else self.eng.snap(base), 0

            def link(self, instruction):
                self.n += 1
                instruction.then_inc(self.sem, 1)
                self.eng.wait_ge(self.sem, self.base + self.n)

            def end(self):
                assert self.n <= self.per, self.n
                if self.n < self.per:
                    self.eng.sem_inc(self.sem, self.per - self.n)

        def first_window(g):
            return 0 if isinstance(g, int) and g == 0 else g * GW - (GW - 1)

        def ln_stats(dve, chain, var_ready, std_ready, g, w, w0):
            settled(dve)
            for i in range(w):
                last = nc.vector.bn_stats(stats[:, i, :], x_cols(w0 + i, 1))
            chain.link(last)
            settled(dve)
            for i in range(w):
                last = nc.vector.bn_aggr(mean_var[:, i, :], stats[:, i, :])
            last.then_inc(var_ready, 1)
            dve.wait_ge(std_ready, g + 1)
            chain.link(nc.vector.reciprocal(rstd[:, 0:w], stdev[:, 0:w]))

        def ln_apply(w0, w):
            for i in range(w):
                last = nc.vector.tensor_scalar(h4[:, i, :], x_cols(w0 + i, 1), mean_var[:, i, 0:1],
                                               rstd[:, i:i + 1], ALU.subtract, ALU.mult)
            return last

        def ln_sqrt(act, var_ready, std_ready, g, w):
            act.wait_ge(var_ready, g + 1)
            nc.scalar.activation(stdev[:, 0:w], mean_var[:, 0:w, 1], ACT.Sqrt,
                                 bias=eps[:, 0:1]).then_inc(std_ready, 1)

        setup = ctx.enter_context(ExitStack())
        weights = {}

        layer0 = graph.enter_context(ExitStack())

        def wt(name, shape):
            weights[name] = sb(name, shape, F32, layer0)
            return weights[name]

        wihT = wt("wihT", [P, C, 3 * D])
        whhT = wt("whhT", [P, C, 3 * D])
        gcnT = wt("gcnT", [P, C, D])
        relvec = wt("relvec", [RELS, D])
        sW1 = wt("sW1", [P, C, D])
        sW2 = wt("sW2", [P, C, P])
        sW3 = wt("sW3", [P, D])
        eW1 = wt("eW1", [P, E0, C, P])
        eW2 = wt("eW2", [P, E0, 64])
        eW3 = wt("eW3", [P, 2, D])
        sel = wt("sel", [E0, E0 * 64])
        gW = wt("gW", [P, C, E0])
        Wr = wt("Wr", [P, C, E1])
        bih = wt("bih", [P, 6])
        bhh = wt("bhh", [P, 6])
        brz = wt("brz", [P, 4])
        b_l1 = wt("b_l1", [P, 6])
        b_l2 = wt("b_l2", [P, 3])
        b_l3 = wt("b_l3", [E0 + 1, D])
        gb = wt("gb", [1, E0])
        gcn_b = wt("gcn_b", [1, D])
        br = wt("br", [1, E1])

        edge_i = [sb(f"edge_i{n}", [P, EJ * P], I32, setup) for n in range(3)]
        edge_f = [sb(f"edge_f{n}", [P, EJ * P], F32, setup) for n in range(3)]
        iw = [sb(f"iw{n}", [P, n_], I32, setup) for n, n_ in enumerate((P, NT, NT * EJ, EJ, GW * E1))]
        wlow = sb("wlow", [P, NT, EJ], F32, setup)
        kidx = sb("kidx", [P, EJ], F32, setup)
        kmb = sb("kmb", [P, EJ], F32, setup)
        ov = sb("ov", [P, NT, EJ], F32, setup)
        ov2 = sb("ov2", [P, NT, EJ], F32, setup)
        bmm = sb("bmm", [P, 2, EJ], F32, setup)
        lohi = sb("lohi", [P, 2, NT], F32, setup)
        col = sb("col", [64, 8], F32, setup)
        coli = sb("coli", [64, 2], I32, setup)
        wraw = [sb(f"wraw{n}", [P, 6 if n < 2 else 2, D], F32, setup) for n in range(3)]

        edges_clear = sem("edges_clear")
        edges_loaded = sem("edges_loaded")
        edges_float = sem("edges_float")
        edges_turned = sem("edges_turned")
        edges_copied = sem("edges_copied")
        lohi_ready = sem("lohi_ready")
        lohi_turned = sem("lohi_turned")
        col_ready = sem("col_ready")
        row_ready = sem("row_ready")
        raw_turned = sem("raw_turned")
        raw_copied = sem("raw_copied")
        iotas = sem("iotas")
        s_var = sem("s_var")
        s_std = sem("s_std")
        s_h = sem("s_h")
        s_hi = sem("s_hi")
        s_r1 = sem("s_r1")
        s_mid = sem("s_mid")
        s_r2 = sem("s_r2")
        s_lo = sem("s_lo")
        s_out = sem("s_out")
        s_left = sem("s_left")
        WEIGHT_LOADS = 30

        with nc.Block() as block:
            @block.sync
            def _(sp):
                sp.dma_start(x_res[:, 0:(NT - 1) * D].rearrange("p (t d) -> p t d", d=D),
                             a["x"][0:(NT - 1) * P, :].rearrange("(t p) d -> p t d", p=P)).then_inc(x_loaded, 16)
                sp.wait_ge(edges_clear, 1)
                full = NE // (EJ * P)
                left = NE - full * EJ * P
                for n, name in enumerate(("dst", "src", "edge_type_16")):
                    e = a[name]
                    sp.dma_start(edge_i[n][0:full, :],
                                 e[0:full * EJ * P].rearrange("(p c) -> p c", p=full)).then_inc(edges_loaded, 16)
                    sp.dma_start(edge_i[n][full:full + 1, 0:left],
                                 e[full * EJ * P:NE].rearrange("(p c) -> p c", p=1)).then_inc(edges_loaded, 16)
                sp.dma_start(x_res[0:N - (NT - 1) * P, (NT - 1) * D:NT * D],
                             a["x"][(NT - 1) * P:N, :]).then_inc(x_tail_loaded, 16)
                sp.sem_inc(s_left, CREDIT)
                def store(g, w):
                    sp.wait_ge(s_lo, CREDIT + 2 * g + (2 if w > 1 else 1))
                    sp.dma_start(table1[ds(g * W, w * P), :].rearrange("(t p) d -> p t d", p=P),
                                 part[:, 0:w, :]).then_inc(s_out, 16)
                    sp.wait_ge(s_out, 16 * g + 16)
                    sp.sem_inc(s_left, 1)
                with sp.Fori(0, GROUPS) as g:
                    store(g, GW)
                store(GROUPS, 1)

            @block.gpsimd
            def _(pool):
                nc.gpsimd.iota(iw[0][:, :], pattern=[[1, P]], base=0, channel_multiplier=0).then_inc(iotas, 1)
                nc.gpsimd.iota(iw[1][:, :], pattern=[[P, NT]], base=0, channel_multiplier=0).then_inc(iotas, 1)
                nc.gpsimd.iota(iw[2][:, :], pattern=[[P, NT], [0, EJ]], base=0, channel_multiplier=0).then_inc(iotas, 1)
                nc.gpsimd.iota(iw[3][:, :], pattern=[[1, EJ]], base=0, channel_multiplier=EJ).then_inc(iotas, 1)
                nc.gpsimd.iota(iw[4][:, :], pattern=[[0, GW], [1, E1]], base=0, channel_multiplier=0).then_inc(iotas, 1)
                nc.gpsimd.iota(place[:, :], pattern=[[2 * P, NT], [1, 2]], base=0, channel_multiplier=2)
                nc.gpsimd.memset(filler[:, :, :], 0.0).then_inc(filler_clear, 1)
                pool.wait_ge(filler_clear, 1)
                nc.gpsimd.iota(filler[:, :, D:RW].bitcast(I32), pattern=[[1, SUB], [1, 1]], base=2 * NPAD,
                               channel_multiplier=SUB)
                nc.gpsimd.memset(ident[:, :], 0.0).then_inc(consts_ready, 1)
                nc.gpsimd.memset(ones[:, :], 1.0).then_inc(consts_ready, 1)
                nc.gpsimd.memset(zeros[:, :], 0.0).then_inc(consts_ready, 1)
                nc.gpsimd.memset(eps[:, :], EPS).then_inc(consts_ready, 1)
                pool.wait_ge(consts_ready, 4)
                nc.gpsimd.affine_select(out=ident[:, :], in_=ident[:, :], compare_op=ALU.not_equal, fill=1.0,
                                        base=0, pattern=[[-1, P]], channel_multiplier=1).then_inc(consts_ready, 1)
                nc.gpsimd.affine_select(out=ustrict[:, :], in_=ones[:, :], compare_op=ALU.is_gt, fill=0.0,
                                        base=0, pattern=[[1, P]], channel_multiplier=-1).then_inc(consts_ready, 1)

            @block.scalar
            def _(act):
                n = 0

                def load(dst, src):
                    nonlocal n
                    n += 1
                    act.dma_start(dst, src, allow_slow_non_contiguous=True).then_inc(loads_done, 16)

                load(wraw[0][:, :, :], a["L0_gnn_w_ih"].rearrange("(j p) i -> p j i", p=P))
                load(wraw[1][:, :, :], a["L0_gnn_w_hh"].rearrange("(j p) i -> p j i", p=P))
                load(wraw[2][:, :, :], a["L1_gnn_W"].rearrange("(j p) i -> p j i", p=P))
                load(relvec[:, :], a["L0_gnn_relvectors"])
                load(bih[:, :], a["L0_gnn_b_ih"].rearrange("(j p) -> p j", p=P))
                load(bhh[:, :], a["L0_gnn_b_hh"].rearrange("(j p) -> p j", p=P))
                load(sW1[:, :, :], a["L0_ffn_sW1"].rearrange("(c p) o -> p c o", p=P))
                load(sW2[:, :, :], a["L0_ffn_sW2"].rearrange("(c p) o -> p c o", p=P))
                load(sW3[:, :], a["L0_ffn_sW3"])
                for e in range(E0):
                    load(eW1[:, e, :, :], a["L0_ffn_eW1"][e].rearrange("(c p) o -> p c o", p=P))
                load(eW2[:, :, :], a["L0_ffn_eW2"].rearrange("e p o -> p e o"))
                load(eW3[:, :, :], a["L0_ffn_eW3"].rearrange("(q r) k o -> (r k) q o", r=2))
                load(gW[:, :, :], a["L0_ffn_gW"].rearrange("(c p) o -> p c o", p=P))
                load(Wr[:, :, :], a["L1_ffn_Wr"].rearrange("(c p) o -> p c o", p=P))
                load(b_l1[:, 0:2], a["L0_ffn_sb1"].rearrange("(j p) -> p j", p=P))
                load(b_l1[:, 2:6], a["L0_ffn_eb1"].rearrange("e p -> p e"))
                load(b_l2[:, 0:1], a["L0_ffn_sb2"].rearrange("(p j) -> p j", j=1))
                load(b_l2[:, 1:3], a["L0_ffn_eb2"].rearrange("(q r) k -> (r k) q", r=2))
                load(b_l3[0:E0, :], a["L0_ffn_eb3"])
                load(b_l3[E0:E0 + 1, :], a["L0_ffn_sb3"].rearrange("(j p) -> j p", j=1))
                load(gb[:, :], a["L0_ffn_gb"].rearrange("(j p) -> j p", j=1))
                load(gcn_b[:, :], a["L1_gnn_b"].rearrange("(j p) -> j p", j=1))
                load(br[:, :], a["L1_ffn_br"].rearrange("(j p) -> j p", j=1))
                weights["loads"] = n

                def group(g, w):
                    ln_sqrt(act, s_var, s_std, g, w)
                    for half in range((w + 1) // 2):
                        k = min(2, w - 2 * half)
                        lo = 2 * half
                        act.wait_ge(s_h, g + 1)
                        act.wait_ge(s_left, g + CREDIT)
                        nc.scalar.activation(part[:, lo:lo + k, 0:D], h4[:, lo:lo + k, :],
                                             ACT.Copy).then_inc(s_hi, 1)
                    for half in range((w + 1) // 2):
                        k = min(2, w - 2 * half)
                        lo = 2 * half
                        act.wait_ge(s_r1, 2 * g + half + 1)
                        nc.scalar.activation(part[:, lo:lo + k, D:2 * D], rest[:, half, 0:k, :],
                                             ACT.Copy).then_inc(s_mid, 1)
                    for half in range((w + 1) // 2):
                        k = min(2, w - 2 * half)
                        lo = 2 * half
                        act.wait_ge(s_r2, 2 * g + half + 1)
                        nc.scalar.activation(part[:, lo:lo + k, 2 * D:3 * D], rest[:, half, 0:k, :],
                                             ACT.Copy).then_inc(s_lo, 1)

                act.wait_ge(consts_ready, 4)
                act.sem_inc(s_mid, CREDIT)
                act.sem_inc(s_lo, CREDIT)
                with act.Fori(0, GROUPS) as g:
                    group(g, GW)
                group(GROUPS, 1)
                act.wait_ge(loads_done, 16 * n)

            @block.vector
            def _(dve):
                chain = Chain(dve, "setup_chain", 64)
                chain.begin(0)
                nc.vector.memset(edge_i[0][:, :], -1)
                nc.vector.memset(edge_i[1][:, :], 0)
                nc.vector.memset(edge_i[2][:, :], 0)
                nc.vector.memset(x_res[:, (NT - 1) * D:NT * D], 0.0).then_inc(edges_clear, 1)
                nc.vector.memset(dstT[:, CHUNKS:KCOLS], -1.0)
                nc.vector.memset(typeT[:, CHUNKS:KCOLS], 0.0)
                nc.vector.memset(srcT[:, CHUNKS:KCOLS], 0)
                dve.wait_ge(iotas, 5)
                nc.vector.tensor_copy(iota_row[:, :], iw[0][:, :])
                nc.vector.tensor_copy(tbase[:, :], iw[1][:, :])
                nc.vector.tensor_copy(wlow[:, :, :], iw[2][:, :].rearrange("p (t j) -> p t j", j=EJ))
                nc.vector.tensor_copy(ts_idx[:, :, :], iw[4][:, :].rearrange("p (t j) -> p t j", j=E1))
                nc.vector.tensor_scalar(kmb[:, :], iw[3][:, :], BIG, None, ALU.subtract)
                chain.link(nc.vector.tensor_scalar(kidx[:, :], iw[3][:, :], 1.0, None, ALU.add))
                dve.wait_ge(edges_loaded, 6 * 16)
                for n in range(3):
                    nc.vector.tensor_copy(edge_f[n][0:EP, :], edge_i[n][0:EP, :]).then_inc(edges_float, 1)
                dve.wait_ge(edges_float, 3)
                d3 = edge_f[0][0:EP, :].rearrange("p (j e) -> p j e", e=P)
                nc.vector.tensor_reduce(bmm[0:EP, 0, :], d3, AX, ALU.max)
                pad = edge_i[0][0:EP, :].bitcast(F32)
                chain.link(nc.vector.tensor_scalar(pad, edge_f[0][0:EP, :], 0.0, BIG, ALU.is_lt, ALU.mult))
                chain.link(nc.vector.tensor_tensor(pad, pad, edge_f[0][0:EP, :], ALU.add))
                chain.link(nc.vector.tensor_reduce(bmm[0:EP, 1, :], pad.rearrange("p (j e) -> p j e", e=P), AX, ALU.min))
                top = bmm[0:EP, 0, :].unsqueeze(1).to_broadcast([EP, NT, EJ])
                low = bmm[0:EP, 1, :].unsqueeze(1).to_broadcast([EP, NT, EJ])
                nc.vector.tensor_tensor(ov[0:EP], top, wlow[0:EP], ALU.is_ge)
                chain.link(nc.vector.scalar_tensor_tensor(ov2[0:EP], wlow[0:EP], float(P), low, ALU.add, ALU.is_gt))
                chain.link(nc.vector.tensor_tensor(ov[0:EP], ov[0:EP], ov2[0:EP], ALU.mult))
                kb = kmb[0:EP, :].unsqueeze(1).to_broadcast([EP, NT, EJ])
                kp = kidx[0:EP, :].unsqueeze(1).to_broadcast([EP, NT, EJ])
                chain.link(nc.vector.tensor_tensor(ov2[0:EP], ov[0:EP], kb, ALU.mult))
                nc.vector.tensor_reduce(lohi[0:EP, 0, :], ov2[0:EP], AX, ALU.min)
                chain.link(nc.vector.tensor_tensor(ov[0:EP], ov[0:EP], kp, ALU.mult))
                nc.vector.tensor_reduce(lohi[0:EP, 1, :], ov[0:EP], AX, ALU.max).then_inc(lohi_ready, 1)
                for n in range(3):
                    dst = (dstT, srcT, typeT)[n]
                    view = dst[:, 0:CHUNKS].rearrange("p (k j) -> p j k", j=EJ)
                    for half in range(2):
                        dve.wait_ge(edges_turned, 2 * n + half + 1)
                        j0, k = (0, 4) if half == 0 else (4, 3)
                        nc.vector.tensor_copy(
                            view[:, j0:j0 + k, :],
                            bank[2 * n + half][:, 0:k * EP].rearrange("p (j k) -> p j k", k=EP)).then_inc(edges_copied, 1)
                dve.wait_ge(lohi_turned, 1)
                nc.vector.tensor_reduce(col[0:NT, 0:1], bank[6][0:NT, 0:EP], AX, ALU.min)
                chain.link(nc.vector.tensor_reduce(col[0:NT, 1:2], bank[6][0:NT, EP:2 * EP], AX, ALU.max))
                nc.vector.tensor_scalar(col[0:NT, 2:3], col[0:NT, 1:2], 1.0, None, ALU.max)
                chain.link(nc.vector.tensor_scalar(col[0:NT, 3:4], col[0:NT, 0:1], BIG, None, ALU.add))
                chain.link(nc.vector.tensor_scalar(col[0:NT, 4:5], col[0:NT, 2:3], 1.0, None, ALU.subtract))
                chain.link(nc.vector.tensor_tensor(col[0:NT, 5:6], col[0:NT, 3:4], col[0:NT, 4:5], ALU.min))
                chain.link(nc.vector.tensor_tensor(col[0:NT, 6:7], col[0:NT, 2:3], col[0:NT, 5:6], ALU.subtract))
                chain.link(nc.vector.tensor_scalar(coli[0:NT, 0:1], col[0:NT, 6:7], float(U - 1), None, ALU.add))
                chain.link(nc.vector.tensor_single_scalar(coli[0:NT, 1:2], coli[0:NT, 0:1], U.bit_length() - 1,
                                                          ALU.arith_shift_right))
                nc.vector.tensor_copy(col[0:NT, 7:8], coli[0:NT, 1:2]).then_inc(col_ready, 1)
                dve.wait_ge(row_ready, 1)
                chain.link(nc.vector.tensor_copy(windows[0:1, :], bank[7][0:1, 0:3 * NT]))
                nc.vector.tensor_scalar(early[:, :], windows[:, NT:2 * NT], float(MH), None, ALU.min)
                chain.link(nc.vector.tensor_scalar(rounds[:, 0:NT], windows[:, 2 * NT:3 * NT], float(M - 1), None,
                                                   ALU.add))
                chain.link(nc.vector.tensor_tensor(rounds[:, NT:NT + 1], rounds[:, NT - 1:NT],
                                                   windows[:, 2 * NT - 1:2 * NT], ALU.add))
                chain.link(nc.vector.tensor_single_scalar(rounds[:, :], rounds[:, :], M.bit_length() - 1,
                                                          ALU.arith_shift_right))
                dve.wait_ge(consts_ready, 6)
                nc.vector.tensor_copy(sel[:, :].rearrange("p (e k) -> p e k", k=64),
                                      ident[0:E0, 0:E0].unsqueeze(2).to_broadcast([E0, E0, 64]))
                turned = 0
                for n, (dst, blocks) in enumerate(((wihT, 6), (whhT, 6), (gcnT, 2))):
                    for c in range(C):
                        for j0 in range(0, blocks, 4):
                            k = min(4, blocks - j0)
                            turned += 1
                            dve.wait_ge(raw_turned, turned)
                            nc.vector.tensor_copy(dst[:, c, j0 * P:(j0 + k) * P],
                                                  bank[(turned - 1) % 6][:, 0:k * P]).then_inc(raw_copied, 1)
                dve.wait_ge(loads_done, 16 * weights["loads"])
                chain.link(nc.vector.tensor_tensor(brz[:, :], bih[:, 0:4], bhh[:, 0:4], ALU.add))
                chain.end()

                chain = Chain(dve, "table1_chain", 4)
                dve.wait_ge(x_loaded, 16)
                dve.wait_ge(x_tail_loaded, 16)

                def group(g, w):
                    chain.begin(g)
                    ln_stats(dve, chain, s_var, s_std, g, w, g * GW)
                    nc.vector.tensor_copy(ln_mean[:, ds(g * GW, w)], mean_var[:, 0:w, 0])
                    nc.vector.tensor_copy(ln_rstd[:, ds(g * GW, w)], rstd[:, 0:w])
                    dve.wait_ge(s_mid, CREDIT + 2 * g)
                    ln_apply(g * GW, w).then_inc(s_h, 1)
                    dve.wait_ge(s_h, g + 1)
                    for half in range((w + 1) // 2):
                        k, lo = min(2, w - 2 * half), 2 * half
                        dve.wait_ge(s_hi, 2 * g + half + 1)
                        dve.wait_ge(s_lo, CREDIT + 2 * g)
                        nc.vector.tensor_tensor(rest[:, half, 0:k, :], h4[:, lo:lo + k, :],
                                                part[:, lo:lo + k, 0:D], ALU.subtract).then_inc(s_r1, 1)
                    for half in range((w + 1) // 2):
                        k, lo = min(2, w - 2 * half), 2 * half
                        dve.wait_ge(s_mid, CREDIT + 2 * g + half + 1)
                        nc.vector.tensor_tensor(rest[:, half, 0:k, :], rest[:, half, 0:k, :],
                                                part[:, lo:lo + k, D:2 * D], ALU.subtract).then_inc(s_r2, 1)
                    chain.end()

                with dve.Fori(0, GROUPS) as g:
                    group(g, GW)
                group(GROUPS, 1)

            @block.tensor
            def _(pe):
                pe.wait_ge(consts_ready, 6)
                for n in range(3):
                    pe.wait_ge(edges_float, n + 1)
                    for half in range(2):
                        j0, k = (0, 4) if half == 0 else (4, 3)
                        for j in range(k):
                            last = nc.tensor.transpose(bank[2 * n + half][:, j * EP:(j + 1) * EP],
                                                       edge_f[n][0:EP, (j0 + j) * P:(j0 + j + 1) * P],
                                                       ident[0:EP, 0:EP])
                        last.then_inc(edges_turned, 1)
                pe.wait_ge(lohi_ready, 1)
                for n in range(2):
                    last = nc.tensor.transpose(bank[6][0:NT, n * EP:(n + 1) * EP], lohi[0:EP, n, :],
                                               ident[0:EP, 0:EP])
                last.then_inc(lohi_turned, 1)
                pe.wait_ge(col_ready, 1)
                for n, (c0, m) in enumerate(((5, ident), (7, ident), (7, ustrict))):
                    last = nc.tensor.matmul(bank[7][0:1, n * NT:(n + 1) * NT], col[0:NT, c0:c0 + 1], m[0:NT, 0:NT],
                                            start=True, stop=True)
                last.then_inc(row_ready, 1)
                pe.wait_ge(loads_done, 16 * weights["loads"])
                pe.wait_ge(edges_copied, 6)
                turned = 0
                for n, blocks in enumerate((6, 6, 2)):
                    for c in range(C):
                        for j0 in range(0, blocks, 4):
                            k = min(4, blocks - j0)
                            if turned >= 6:
                                pe.wait_ge(raw_copied, turned - 5)
                            for j in range(k):
                                last = nc.tensor.transpose(bank[turned % 6][:, j * P:(j + 1) * P],
                                                           wraw[n][:, j0 + j, c * P:(c + 1) * P], ident[:, :])
                            last.then_inc(raw_turned, 1)
                            turned += 1
        setup.close()

        class Gather:
            def __init__(self, name, table, with_types):
                self.table, self.with_types = table, with_types
                self.idx_landed = sem(name + "_idx_landed")
                self.landed = [sem(f"{name}_rows_landed{m}") for m in range(M)]
                self.rows_ready = sem(name + "_rows_ready")
                self.used = sem(name + "_rows_used")
                self.hot = sem(name + "_onehot_ready")
                self.done = sem(name + "_window_done")
                self.evacuated = sem(name + "_window_evacuated")

        def window_values(eng, t):
            first = eng.value_load(windows[0:1, ds(t, 1)], min_val=0, max_val=CHUNKS - 1)
            blocks = eng.value_load(windows[0:1, ds(t + NT, 1)], min_val=1, max_val=CHUNKS // U)
            before = eng.value_load(windows[0:1, ds(t + 2 * NT, 1)], min_val=0, max_val=NT * CHUNKS // U)
            return first, blocks, before

        def ring(eng, n, blocks):
            return narrow(eng.snap((n % blocks) * U), 0, (blocks - 1) * U)

        def sp_indices(sp, q):
            def block_indices(n, k):
                slot = ring(sp, n, M)
                sp.wait_ge(q.rows_ready, n + 1)
                sp.dma_start(idx[:, ds(slot, U)], srcT[:, ds(k, U)],
                             allow_slow_non_contiguous=True).then_inc(q.idx_landed, 16)
                sp.wait_ge(q.idx_landed, n * 16 + 16)
                settled(sp)

            with sp.Fori(0, NT) as t:
                first, blocks, before = window_values(sp, t)
                with sp.Fori(0, blocks) as j:
                    block_indices(sp.snap(before + j), narrow(sp.snap(first + j * U), 0, CHUNKS - 1))
            _, blocks, before = window_values(sp, NT - 1)
            with sp.Fori(0, M - 1) as extra:
                block_indices(sp.snap(before + blocks + extra), 0)

        def pool_begin(pool, q, column):
            pool.sem_inc(q.rows_ready, M - 1)
            pool.dma_start(spare[:, column:column + 1], zeros[:, 0:1],
                           allow_slow_non_contiguous=True).then_inc(q.landed[M - 1], 16)

        def pool_rounds(pool, q, r0, r1):
            with pool.Fori(r0, r1) as r:
                for m in range(M):
                    n = pool.snap(r * M + m)
                    pool.wait_ge(q.idx_landed, n * 16 + 16)
                    pool.wait_ge(q.used, n + 1 + MH - M)
                    settled(pool)
                    for s in range(m * U, (m + 1) * U):
                        nc.gpsimd.indirect_dma_start(
                            out=rows[:, s, :], out_offset=None, in_=q.table,
                            in_offset=bass.IndirectOffsetOnAxis(idx[:, s:s + 1], axis=0)).then_inc(q.landed[m], 16)
                    if m == 0:
                        pool.wait_ge(q.landed[M - 1], r * (16 * U) + 16)
                    else:
                        pool.wait_ge(q.landed[m - 1], r * (16 * U) + 16 * U)
                    pool.sem_inc(q.rows_ready, 1)

        def pool_end(pool, q, r):
            pool.wait_ge(q.landed[M - 1], r * (16 * U) + 16)
            pool.sem_inc(q.rows_ready, 1)

        def rounds_value(eng, t, low):
            return eng.value_load(rounds[0:1, ds(t, 1)], min_val=low, max_val=NT * CHUNKS // (U * M) + 1)

        def dve_onehots(dve, q, t, late):
            first, blocks, before = window_values(dve, t)
            first_blocks = dve.value_load(early[0:1, ds(t, 1)], min_val=1, max_val=MH)
            base = tbase[:, ds(t, 1)]

            def block_onehots(j):
                n = dve.snap(before + j)
                k = narrow(dve.snap(first + j * U), 0, CHUNKS - 1)
                slot = ring(dve, n, MH)
                dve.wait_ge(q.used, n + 1)
                last = nc.vector.scalar_tensor_tensor(
                    onehot[:, ds(slot, U), :], iota_row[:, :].unsqueeze(1).to_broadcast([P, U, P]), base,
                    dstT[:, ds(k, U)].unsqueeze(2).to_broadcast([P, U, P]), ALU.add, ALU.is_equal)
                if q.with_types:
                    last = nc.vector.tensor_tensor(
                        typehot[:, ds(slot, U), :], iota_row[:, 0:RELS].unsqueeze(1).to_broadcast([P, U, RELS]),
                        typeT[:, ds(k, U)].unsqueeze(2).to_broadcast([P, U, RELS]), ALU.is_equal)
                last.then_inc(q.hot, 1)

            if late:
                with dve.If(blocks > first_blocks):
                    with dve.Fori(first_blocks, blocks) as j:
                        block_onehots(j)
            else:
                with dve.Fori(0, first_blocks) as j:
                    block_onehots(j)

        def pe_window(pe, q, t, acc):
            first, blocks, before = window_values(pe, t)
            wide, low = acc
            width = D + RELS if q.with_types else D
            nc.tensor.matmul(wide[:, 0:2 * D], zlhs, zrhs[:, 0:2 * D], start=True, stop=False, skip_group_check=True)
            nc.tensor.matmul(low[:, 0:width], zlhs, zrhs[:, 0:width], start=True, stop=False, skip_group_check=True)
            with pe.Fori(0, blocks) as j:
                n = pe.snap(before + j)
                slot, hot_slot = ring(pe, n, M), ring(pe, n, MH)
                pe.wait_ge(q.hot, n + 1)
                pe.wait_ge(q.rows_ready, n + M + 1)
                for s in range(U):
                    at, hot_at = ds(narrow(slot + s, 0, M * U - 1), 1), ds(narrow(hot_slot + s, 0, MH * U - 1), 1)
                    hot = onehot[:, hot_at, :].rearrange("p a e -> p (a e)")
                    nc.tensor.matmul(wide[:, 0:2 * D], hot, rows[:, at, 0:2 * D].rearrange("p a d -> p (a d)"),
                                     start=False, stop=False, skip_group_check=True)
                    last = nc.tensor.matmul(low[:, 0:D], hot, rows[:, at, 2 * D:3 * D].rearrange("p a d -> p (a d)"),
                                            start=False, stop=False, skip_group_check=True)
                    if q.with_types:
                        last = nc.tensor.matmul(low[:, D:width], hot, typehot[:, hot_at, :].rearrange("p a d -> p (a d)"),
                                                start=False, stop=False, skip_group_check=True)
                last.then_inc(q.used, 1)
            nc.tensor.matmul(wide[:, 0:2 * D], zlhs, zrhs[:, 0:2 * D], start=False, stop=True, skip_group_check=True)
            nc.tensor.matmul(low[:, 0:width], zlhs, zrhs[:, 0:width], start=False, stop=True,
                             skip_group_check=True).then_inc(q.done, 1)

        def pe_windows(pe, q, g, i, banks):
            t = first_window(g) + i
            back = next(k for k in range(1, GW + 1) if banks[(i - k) % GW] == banks[i])
            if isinstance(t, int) and t == 0:
                i = GW - 1
            elif not (isinstance(t, int) and t < back):
                pe.wait_ge(q.evacuated, t + 1 - back)
            pe_window(pe, q, t, banks[i])

        def router_buffers(name, where):
            f = {k: sb(f"{name}_{k}", [P, GW, E1], F32, where) for k in ("lg", "ex", "p", "c", "eq1", "eq2", "p2")}
            f.update({k: sb(f"{name}_{k}", [P, GW], F32, where) for k in ("m", "m1", "m2", "i", "s", "w1", "w2", "e")})
            return f

        def router_logits(f, chain, logits, w, experts):
            lg = f["lg"][:, 0:w, 0:experts]
            chain.link(nc.vector.tensor_copy(lg, logits.rearrange("p (t e) -> p t e", e=experts)))
            chain.link(nc.vector.tensor_reduce(f["m"][:, 0:w], lg, AX, ALU.max))
            m = f["m"][:, 0:w].unsqueeze(2).to_broadcast([P, w, experts])
            return nc.vector.tensor_tensor(lg, lg, m, ALU.subtract)

        def router_choice(f, chain, w, experts):
            def wide(v):
                return v[:, 0:w].unsqueeze(2).to_broadcast([P, w, experts])
            ex, p, c, eq1, eq2, p2 = (f[k][:, 0:w, 0:experts] for k in ("ex", "p", "c", "eq1", "eq2", "p2"))
            index = ts_idx[:, 0:w, 0:experts]
            chain.link(nc.vector.tensor_reduce(f["s"][:, 0:w], ex, AX, ALU.add))
            chain.link(nc.vector.reciprocal(f["s"][:, 0:w], f["s"][:, 0:w]))
            chain.link(nc.vector.tensor_tensor(p, ex, wide(f["s"]), ALU.mult))
            for source, m, eq in ((p, f["m1"], eq1), (p2, f["m2"], eq2)):
                chain.link(nc.vector.tensor_reduce(m[:, 0:w], source, AX, ALU.max))
                chain.link(nc.vector.tensor_tensor(c, source, wide(m), ALU.not_equal))
                chain.link(nc.vector.scalar_tensor_tensor(c, c, 16.0, index, ALU.mult, ALU.add))
                chain.link(nc.vector.tensor_reduce(f["i"][:, 0:w], c, AX, ALU.min))
                chain.link(nc.vector.tensor_tensor(eq, index, wide(f["i"]), ALU.is_equal))
                if eq is eq1:
                    chain.link(nc.vector.scalar_tensor_tensor(p2, eq1, -4.0, p, ALU.mult, ALU.add))

        hT = t0
        red4 = sb("red4", [P, GW, D + RELS], F32, layer0)
        ctT = sb("ctT", [RELS, W], F32, layer0)
        redT = sb("redT", [P, C, W], F32, layer0)
        rT = sb("rT", [P, C, W], F32, layer0)
        zT = sb("zT", [P, C, W], F32, layer0)
        tT = sb("tT", [P, C, W], F32, layer0)
        nT = sb("nT", [P, C, W], F32, layer0)
        a1T = sb("a1T", [P, 6, W], F32, layer0)
        a2T = sb("a2T", [P, 3, W], F32, layer0)
        gate5 = sb("gate5", [P, GW, E1], F32, layer0)
        gT = sb("gT", [E0 + 1, W], F32, layer0)
        deg = sb("deg", [P, GW], F32, layer0)
        f0 = router_buffers("f0", layer0)
        q1 = Gather("g1", table1, True)
        names = ("h4_ready hT_ps ct_ps ct_sb redT_ps hT_sb redT_sb r_ps z_ps in_ps hn_ps r_act z_act t1_done t2_done "
                 "n_act hnew back_ps x1_var x1_std h1_ready h1T_ps h1T_sb gate_ps l1_ps l1_act l2_ps l2_act "
                 "lg_ready ex_ready mm_ready em_ready gates_ready gT_ps gT_sb spread_ps gated l3_ps x2_var x2_std "
                 "h2_ready h2T_ps h2T_sb xt_ps hi_done r1_done mid_done r2_done lo_done table2_out").split()
        S = {n: sem("d_" + n) for n in names}
        BANKS1 = ((bank[6], bank[7]), (bank[5], bank[1]), (bank[6], bank[7]), (bank[6], bank[7]))
        BANKS2 = ((bank[4], bank[5]), (bank[6], bank[7])) * 2
        L1_BANKS = (4, 0, 3, 1, 5, 4)
        L2_BANKS = (0, 3, 4)

        def halves(w):
            return [(half, 2 * half, min(2, w - 2 * half)) for half in range((w + 1) // 2)]

        def per_half(w):
            return 1 if w > 2 else 2

        def pe_d1(pe, g, w):
            n = w * P
            pe.wait_ge(S["h4_ready"], g + 1)
            for c in range(C):
                for i in range(w):
                    last = nc.tensor.transpose(bank[c][:, i * P:(i + 1) * P], h4[:, i, c * P:(c + 1) * P], ident[:, :])
            last.then_inc(S["hT_ps"], 1)
            pe.wait_ge(q1.evacuated, first_window(g) + w)
            for i in range(w):
                last = nc.tensor.transpose(bank[2][0:RELS, i * P:(i + 1) * P], red4[:, i, D:D + RELS], ident[:, :])
            last.then_inc(S["ct_ps"], 1)
            pe.wait_ge(S["hi_done"], CREDIT + 2 * g)
            pe.wait_ge(S["r1_done"], CREDIT + 2 * g)
            for c in range(C):
                for i in range(w):
                    nc.tensor.matmul(bank[3 + c][:, i * P:(i + 1) * P], red4[:, i, c * P:(c + 1) * P], ident[:, :],
                                     start=i == 0, stop=False, skip_group_check=True)
            pe.wait_ge(S["ct_sb"], g + 1)
            for c in range(C):
                last = nc.tensor.matmul(bank[3 + c][:, 0:n], relvec[:, c * P:(c + 1) * P], ctT[:, 0:n],
                                        start=False, stop=True, skip_group_check=True)
            last.then_inc(S["redT_ps"], 1)
            pe.wait_ge(S["hT_sb"], g + 1)
            pe.wait_ge(S["redT_sb"], g + 1)
            for c in range(C):
                b_r, b_z, b_in, b_hn = ((2, 5, 3, 4), (0, 1, 2, 5))[c]
                for gate, b, name in ((0, b_r, "r_ps"), (1, b_z, "z_ps")):
                    o = gate * D + c * P
                    for k in range(C):
                        nc.tensor.matmul(bank[b][:, 0:n], wihT[:, k, o:o + P], redT[:, k, 0:n], start=k == 0, stop=False)
                    for k in range(C):
                        last = nc.tensor.matmul(bank[b][:, 0:n], whhT[:, k, o:o + P], hT[:, k, 0:n],
                                                start=False, stop=k == C - 1)
                    last.then_inc(S[name], 1)
                o = 2 * D + c * P
                if c == 1:
                    pe.wait_ge(S["z_act"], 2 * g + 1)
                for k in range(C):
                    last = nc.tensor.matmul(bank[b_hn][:, 0:n], whhT[:, k, o:o + P], hT[:, k, 0:n],
                                            start=k == 0, stop=k == C - 1)
                last.then_inc(S["hn_ps"], 1)
                for k in range(C):
                    last = nc.tensor.matmul(bank[b_in][:, 0:n], wihT[:, k, o:o + P], redT[:, k, 0:n],
                                            start=k == 0, stop=k == C - 1)
                last.then_inc(S["in_ps"], 1)

        def pe_d2(pe, g, w):
            n = w * P
            pe.wait_ge(S["hnew"], 2 * g + 2)
            for i in range(w):
                for c in range(C):
                    o = (i % 2) * D + c * P
                    last = nc.tensor.transpose(bank[3 + i // 2][:, o:o + P], nT[:, c, i * P:(i + 1) * P], ident[:, :])
            last.then_inc(S["back_ps"], 1)

        def turn(g, w, b0, b1, ready, done, pe):
            pe.wait_ge(S[ready], g + 1)
            for c, b in enumerate((b0, b1)):
                for i in range(w):
                    last = nc.tensor.transpose(bank[b][:, i * P:(i + 1) * P], h4[:, i, c * P:(c + 1) * P], ident[:, :])
            last.then_inc(S[done], 1)

        def pe_d3(pe, g, w):
            n = w * P
            turn(g, w, 0, 3, "h1_ready", "h1T_ps", pe)
            pe.wait_ge(S["h1T_sb"], g + 1)
            for i in range(w):
                o = slice(i * E0, (i + 1) * E0)
                for c in range(C):
                    nc.tensor.matmul(bank[2][:, o], t0[:, c, i * P:(i + 1) * P], gW[:, c, :],
                                     start=i == 0 and c == 0, stop=False, skip_group_check=True)
                last = nc.tensor.matmul(bank[2][:, o], ones[0:1, :], gb[:, :], start=False, stop=True,
                                        skip_group_check=True)
            last.then_inc(S["gate_ps"], 1)
            for j, b in enumerate(L1_BANKS):
                if j == 3 and not isinstance(g, int) or j == 3 and g < GROUPS:
                    pe.wait_ge(q1.evacuated, first_window(g + 1) + 2)
                if j == 5:
                    pe.wait_ge(S["l1_act"], 6 * g + 1)
                for c in range(C):
                    w1 = sW1[:, c, j * P:(j + 1) * P] if j < 2 else eW1[:, j - 2, c, :]
                    last = nc.tensor.matmul(bank[b][:, 0:n], w1, t0[:, c, 0:n], start=c == 0, stop=c == C - 1)
                last.then_inc(S["l1_ps"], 1)
            pe.wait_ge(S["l1_act"], 6 * g + 2)
            for c in range(C):
                last = nc.tensor.matmul(bank[L2_BANKS[0]][:, 0:n], sW2[:, c, :], a1T[:, c, 0:n], start=c == 0, stop=c == C - 1)
            last.then_inc(S["l2_ps"], 1)
            for pair in range(2):
                pe.wait_ge(S["l1_act"], 6 * g + 4 + 2 * pair)
                for r in range(2):
                    e = 2 * pair + r
                    last = nc.tensor.matmul(bank[L2_BANKS[1 + pair]][r * 64:(r + 1) * 64, 0:n], eW2[:, e, :],
                                            a1T[:, 2 + e, 0:n], start=True, stop=True)
                last.then_inc(S["l2_ps"], 1)

        def pe_d4(pe, g, w):
            n = w * P
            pe.wait_ge(S["gates_ready"], g + 1)
            for i in range(w):
                last = nc.tensor.transpose(bank[2][0:E0 + 1, i * P:(i + 1) * P], gate5[:, i, 0:E0 + 1], ident[:, :])
            last.then_inc(S["gT_ps"], 1)
            pe.wait_ge(S["gT_sb"], g + 1)
            pe.wait_ge(S["l2_act"], 3 * g + 3)
            for pair, b in enumerate((1, 5)):
                nc.tensor.matmul(bank[b][:, 0:n], sel[:, pair * P:(pair + 1) * P], gT[0:E0, 0:n],
                                 start=True, stop=True).then_inc(S["spread_ps"], 1)
            for half, lo, k in halves(w):
                for i in range(lo, lo + k):
                    acc = bank[3 + half][:, (i - lo) * D:(i - lo + 1) * D]
                    nc.tensor.matmul(acc, a2T[:, 0, i * P:(i + 1) * P], sW3[:, :], start=i == lo, stop=False,
                                     skip_group_check=True)
                    nc.tensor.matmul(acc, gT[:, i * P:(i + 1) * P], b_l3[:, :], start=False, stop=False,
                                     skip_group_check=True)
            pe.wait_ge(S["gated"], 2 * g + 2)
            for half, lo, k in halves(w):
                for i in range(lo, lo + k):
                    acc = bank[3 + half][:, (i - lo) * D:(i - lo + 1) * D]
                    for pair in range(2):
                        last = nc.tensor.matmul(acc, a2T[:, 1 + pair, i * P:(i + 1) * P], eW3[:, pair, :],
                                                start=False, stop=pair == 1, skip_group_check=True)
                last.then_inc(S["l3_ps"], per_half(w))

        def pe_d5(pe, g, w):
            turn(g, w, 1, 5, "h2_ready", "h2T_ps", pe)
            pe.wait_ge(S["h2T_sb"], g + 1)
            for half, lo, k in halves(w):
                for i in range(lo, lo + k):
                    o = slice((i - lo) * D, (i - lo + 1) * D)
                    for c in range(C):
                        nc.tensor.matmul(bank[3 + half][:, o], t0[:, c, i * P:(i + 1) * P], gcnT[:, c, :],
                                         start=c == 0, stop=False)
                    last = nc.tensor.matmul(bank[3 + half][:, o], ones[0:1, :], gcn_b[:, :], start=False, stop=True)
                last.then_inc(S["xt_ps"], per_half(w))

        def act_d1(act, g, w):
            n = w * P
            act.wait_ge(S["hT_ps"], g + 1)
            for c in range(C):
                last = nc.scalar.activation(hT[:, c, 0:n], bank[c][:, 0:n], ACT.Copy)
            last.then_inc(S["hT_sb"], 1)
            act.wait_ge(S["ct_ps"], g + 1)
            nc.scalar.activation(ctT[:, 0:n], bank[2][0:RELS, 0:n], ACT.Copy).then_inc(S["ct_sb"], 1)
            for c in range(C):
                b_r, b_z = ((2, 5), (0, 1))[c]
                act.wait_ge(S["r_ps"], 2 * g + c + 1)
                nc.scalar.activation(rT[:, c, 0:n], bank[b_r][:, 0:n], ACT.Sigmoid,
                                     bias=brz[:, c:c + 1]).then_inc(S["r_act"], 1)
                act.wait_ge(S["z_ps"], 2 * g + c + 1)
                nc.scalar.activation(zT[:, c, 0:n], bank[b_z][:, 0:n], ACT.Sigmoid,
                                     bias=brz[:, 2 + c:3 + c]).then_inc(S["z_act"], 1)
            for c in range(C):
                act.wait_ge(S["t2_done"], 2 * g + c + 1)
                nc.scalar.activation(nT[:, c, 0:n], tT[:, c, 0:n], ACT.Tanh,
                                     bias=bih[:, 4 + c:5 + c]).then_inc(S["n_act"], 1)

        def act_d2(act, g, w):
            ln_sqrt(act, S["x1_var"], S["x1_std"], g, w)

        def act_turned(act, g, w, b0, b1, done_ps, done_sb, credit=0):
            act.wait_ge(S[done_ps], credit + g + 1)
            for c, b in enumerate((b0, b1)):
                last = nc.scalar.activation(t0[:, c, 0:w * P], bank[b][:, 0:w * P], ACT.Copy)
            last.then_inc(S[done_sb], 1)

        def act_d3(act, g, w):
            n = w * P
            act_turned(act, g, w, 0, 3, "h1T_ps", "h1T_sb")
            for j, b in enumerate(L1_BANKS):
                act.wait_ge(S["l1_ps"], 6 * g + j + 1)
                nc.scalar.activation(a1T[:, j, 0:n], bank[b][:, 0:n], ACT.Relu,
                                     bias=b_l1[:, j:j + 1]).then_inc(S["l1_act"], 1)
            for j, b in enumerate(L2_BANKS):
                act.wait_ge(S["l2_ps"], 3 * g + j + 1)
                nc.scalar.activation(a2T[:, j, 0:n], bank[b][:, 0:n], ACT.Relu,
                                     bias=b_l2[:, j:j + 1]).then_inc(S["l2_act"], 1)
            act.wait_ge(S["lg_ready"], g + 1)
            nc.scalar.activation(f0["ex"][:, 0:w, 0:E0], f0["lg"][:, 0:w, 0:E0], ACT.Exp).then_inc(S["ex_ready"], 1)
            act.wait_ge(S["mm_ready"], g + 1)
            nc.scalar.activation(f0["e"][:, 0:w], f0["m"][:, 0:w], ACT.Exp).then_inc(S["em_ready"], 1)

        def act_d4(act, g, w):
            n = w * P
            act.wait_ge(S["gT_ps"], g + 1)
            nc.scalar.activation(gT[:, 0:n], bank[2][0:E0 + 1, 0:n], ACT.Copy).then_inc(S["gT_sb"], 1)
            ln_sqrt(act, S["x2_var"], S["x2_std"], g, w)

        def act_d5(act, g, w):
            act_turned(act, g, w, 1, 5, "h2T_ps", "h2T_sb", CREDIT)
            act.wait_ge(S["table2_out"], 16 * g + 16)
            for half, lo, k in halves(w):
                act.wait_ge(S["xt_ps"], 2 * g + half + 1)
                nc.scalar.activation(part[:, lo:lo + k, 0:D],
                                     bank[3 + half][:, 0:k * D].rearrange("p (t d) -> p t d", d=D),
                                     ACT.Copy).then_inc(S["hi_done"], per_half(w))
            for half, lo, k in halves(w):
                act.wait_ge(S["r1_done"], CREDIT + 2 * g + half + 1)
                nc.scalar.activation(part[:, lo:lo + k, D:2 * D], rest[:, half, 0:k, :],
                                     ACT.Copy).then_inc(S["mid_done"], per_half(w))
            for half, lo, k in halves(w):
                act.wait_ge(S["r2_done"], 2 * g + half + 1)
                nc.scalar.activation(part[:, lo:lo + k, 2 * D:3 * D], rest[:, half, 0:k, :],
                                     ACT.Copy).then_inc(S["lo_done"], per_half(w))
            act.wait_ge(S["lo_done"], CREDIT + 2 * g + 2)
            act.dma_start(table2[ds(first_window(g) * P, w * P), :].rearrange("(t p) d -> p t d", p=P),
                          part[:, 0:w, :]).then_inc(S["table2_out"], 16)

        def normalised(dve, g, w):
            dve.wait_ge(S["h2T_ps"], CREDIT + g)
            for i in range(w):
                t = first_window(g) + i
                last = nc.vector.tensor_scalar(h4[:, i, :], x_cols(t, 1), ln_mean[:, ds(t, 1)], ln_rstd[:, ds(t, 1)],
                                               ALU.subtract, ALU.mult)
            last.then_inc(S["h4_ready"], 1)

        def dve_d1(dve, chain, g, w):
            n = w * P
            chain.begin(g)
            dve.wait_ge(q1.evacuated, first_window(g) + w)
            chain.link(nc.vector.tensor_reduce(deg[:, 0:w], red4[:, 0:w, D:D + RELS], AX, ALU.add))
            chain.link(nc.vector.tensor_scalar(deg[:, 0:w], deg[:, 0:w], 1.0, None, ALU.add))
            nc.vector.reciprocal(inv_deg[:, ds(first_window(g), w)], deg[:, 0:w])
            dve.wait_ge(S["redT_ps"], g + 1)
            for c in range(C):
                last = nc.vector.tensor_copy(redT[:, c, 0:n], bank[3 + c][:, 0:n])
            last.then_inc(S["redT_sb"], 1)
            for c in range(C):
                b_in, b_hn = ((3, 4), (2, 5))[c]
                dve.wait_ge(S["hn_ps"], 2 * g + c + 1)
                dve.wait_ge(S["r_act"], 2 * g + c + 1)
                nc.vector.scalar_tensor_tensor(tT[:, c, 0:n], bank[b_hn][:, 0:n], bhh[:, 4 + c:5 + c], rT[:, c, 0:n],
                                               ALU.add, ALU.mult).then_inc(S["t1_done"], 1)
                dve.wait_ge(S["t1_done"], 2 * g + c + 1)
                dve.wait_ge(S["in_ps"], 2 * g + c + 1)
                nc.vector.tensor_tensor(tT[:, c, 0:n], tT[:, c, 0:n], bank[b_in][:, 0:n],
                                        ALU.add).then_inc(S["t2_done"], 1)
            for c in range(C):
                dve.wait_ge(S["n_act"], 2 * g + c + 1)
                chain.link(nc.vector.tensor_tensor(tT[:, c, 0:n], hT[:, c, 0:n], nT[:, c, 0:n], ALU.subtract))
                chain.link(nc.vector.tensor_tensor(tT[:, c, 0:n], tT[:, c, 0:n], zT[:, c, 0:n], ALU.mult))
                nc.vector.tensor_tensor(nT[:, c, 0:n], nT[:, c, 0:n], tT[:, c, 0:n], ALU.add).then_inc(S["hnew"], 1)

        def dve_d2(dve, chain, g, w):
            dve.wait_ge(S["back_ps"], g + 1)
            for half, lo, k in halves(w):
                xs = x_cols(first_window(g) + lo, k)
                last = nc.vector.tensor_tensor(xs, xs, bank[3 + half][:, 0:k * D], ALU.add)
            chain.link(last)
            ln_stats(dve, chain, S["x1_var"], S["x1_std"], g, w, first_window(g))
            ln_apply(first_window(g), w).then_inc(S["h1_ready"], 1)

        def dve_d3(dve, chain, g, w):
            dve.wait_ge(S["gate_ps"], g + 1)
            router_logits(f0, chain, bank[2][:, 0:w * E0], w, E0).then_inc(S["lg_ready"], 1)
            dve.wait_ge(S["ex_ready"], g + 1)
            router_choice(f0, chain, w, E0)
            m1, m2, w1, w2, e = (f0[k][:, 0:w] for k in ("m1", "m2", "w1", "w2", "e"))
            nc.vector.tensor_tensor(f0["m"][:, 0:w], m2, m1, ALU.subtract).then_inc(S["mm_ready"], 1)
            dve.wait_ge(S["em_ready"], g + 1)
            chain.link(nc.vector.tensor_scalar(w1, e, 1.0, None, ALU.add))
            chain.link(nc.vector.reciprocal(w1, w1))
            chain.link(nc.vector.tensor_tensor(w2, e, w1, ALU.mult))
            eq1, eq2 = (f0[k][:, 0:w, 0:E0] for k in ("eq1", "eq2"))
            wide = [v.unsqueeze(2).to_broadcast([P, w, E0]) for v in (w1, w2)]
            chain.link(nc.vector.tensor_tensor(eq1, eq1, wide[0], ALU.mult))
            chain.link(nc.vector.tensor_tensor(eq2, eq2, wide[1], ALU.mult))
            nc.vector.memset(gate5[:, 0:w, E0:E0 + 1], 1.0)
            chain.link(nc.vector.tensor_tensor(gate5[:, 0:w, 0:E0], eq1, eq2, ALU.add))
            dve.sem_inc(S["gates_ready"], 1)

        def dve_d4(dve, chain, g, w):
            dve.wait_ge(S["l2_act"], 3 * g + 3)
            for pair, b in enumerate((1, 5)):
                dve.wait_ge(S["spread_ps"], 2 * g + pair + 1)
                hidden = a2T[:, 1 + pair, 0:w * P]
                nc.vector.tensor_tensor(hidden, hidden, bank[b][:, 0:w * P], ALU.mult).then_inc(S["gated"], 1)
            for half, lo, k in halves(w):
                dve.wait_ge(S["l3_ps"], 2 * g + half + 1)
                xs = x_cols(first_window(g) + lo, k)
                last = nc.vector.tensor_tensor(xs, xs, bank[3 + half][:, 0:k * D], ALU.add)
            chain.link(last)
            ln_stats(dve, chain, S["x2_var"], S["x2_std"], g, w, first_window(g))
            ln_apply(first_window(g), w).then_inc(S["h2_ready"], 1)

        def dve_d5(dve, chain, g, w):
            if not (isinstance(g, int) and g == GROUPS):
                normalised(dve, g + 1, GW)
            for half, lo, k in halves(w):
                dve.wait_ge(S["hi_done"], CREDIT + 2 * g + half + 1)
                dve.wait_ge(S["lo_done"], CREDIT + 2 * g)
                nc.vector.tensor_tensor(rest[:, half, 0:k, :], bank[3 + half][:, 0:k * D].rearrange("p (t d) -> p t d", d=D),
                                        part[:, lo:lo + k, 0:D], ALU.subtract).then_inc(S["r1_done"], per_half(w))
            for half, lo, k in halves(w):
                dve.wait_ge(S["mid_done"], 2 * g + half + 1)
                nc.vector.tensor_tensor(rest[:, half, 0:k, :], rest[:, half, 0:k, :],
                                        part[:, lo:lo + k, D:2 * D], ALU.subtract).then_inc(S["r2_done"], per_half(w))
            chain.end()

        sum_chain = [None, None]

        def evacuate1(dve, g, i):
            t = first_window(g) + i
            sums = sum_chain[0]
            sums.begin(t)
            wide, low = BANKS1[i] if not (isinstance(t, int) and t == 0) else BANKS1[GW - 1]
            if not (isinstance(g, int) and g == 0):
                dve.wait_ge(S["redT_ps"], g)
            dve.wait_ge(q1.done, t + 1)
            sums.link(nc.vector.tensor_copy(red4[:, i, :], low[:, 0:D + RELS]))
            for part_ in range(2):
                last = nc.vector.tensor_tensor(red4[:, i, 0:D], red4[:, i, 0:D], wide[:, part_ * D:(part_ + 1) * D],
                                               ALU.add)
                if part_ == 0:
                    sums.link(last)
            last.then_inc(q1.evacuated, 1)

        def run_graph(gather, steps, eng):
            gather(0, 0)
            for i in range(GW):
                steps[i](0, 1)
                gather(1, i)
            steps[GW](0, 1)
            with eng.Fori(2, GROUPS + 1) as g:
                for i in range(GW):
                    steps[i](g - 1, GW)
                    gather(g, i)
                steps[GW](g - 1, GW)
            for i in range(GW + 1):
                steps[i](GROUPS, GW)

        def dve_gather(dve, q, evacuate):
            def gather(g, i):
                t = first_window(g) + i
                if isinstance(t, int) and t == 0:
                    dve_onehots(dve, q, 0, False)
                dve_onehots(dve, q, t, True)
                if i < GW - 1 or isinstance(t, int):
                    dve_onehots(dve, q, t + 1, False)
                else:
                    with dve.If(t + 1 < NT):
                        dve_onehots(dve, q, narrow(t + 1, 0, NT - 1), False)
                evacuate(dve, g, i)
            return gather

        with nc.Block() as block:
            @block.gpsimd
            def _(pool):
                pool_begin(pool, q1, 0)
                total_rounds = rounds_value(pool, NT, 1)
                pool_rounds(pool, q1, 0, total_rounds)
                pool_end(pool, q1, total_rounds)

            @block.tensor
            def _(pe):
                pe.sem_inc(q1.used, MH)
                pe.sem_inc(S["h2T_ps"], CREDIT)
                run_graph(lambda g, i: pe_windows(pe, q1, g, i, BANKS1),
                          [lambda g, w, f=f: f(pe, g, w) for f in (pe_d1, pe_d2, pe_d3, pe_d4, pe_d5)], pe)

            @block.scalar
            def _(act):
                act.sem_inc(S["hi_done"], CREDIT)
                act.sem_inc(S["lo_done"], CREDIT)
                act.dma_start(spare[:, 1:2], zeros[:, 0:1], allow_slow_non_contiguous=True).then_inc(S["table2_out"], 16)
                run_graph(lambda g, i: None,
                          [lambda g, w, f=f: f(act, g, w) for f in (act_d1, act_d2, act_d3, act_d4, act_d5)], act)
                act.wait_ge(S["table2_out"], 16 * (GROUPS + 2))

            @block.vector
            def _(dve):
                chain = Chain(dve, "layer0_chain", 64)
                sum_chain[0] = Chain(dve, "g1_sum_chain", 2)
                dve.sem_inc(S["r1_done"], CREDIT)

                normalised(dve, 0, 1)
                run_graph(dve_gather(dve, q1, evacuate1),
                          [lambda g, w, f=f: f(dve, chain, g, w) for f in (dve_d1, dve_d2, dve_d3, dve_d4, dve_d5)], dve)

            @block.sync
            def _(sp):
                sp_indices(sp, q1)

        f1 = router_buffers("f1", graph)
        chosen = sb("chosen", [P, GW, E1], F32, graph)
        rank = sb("rank", [P, GW, E1], F32, graph)
        total = sb("total", [P, GW, E1], F32, graph)
        region = sb("region", [P, E1], F32, graph)
        count = sb("count", [P, E1], F32, graph)
        pos_f = sb("pos_f", [P, GW, 2], F32, graph)
        pos = sb("pos", [P, 2 * GW], I32, graph)
        xr = sb("xr", [P, GW, 2, RW], F32, graph)
        q2 = Gather("g2", table2, False)
        names = ("var std xn_ready xnT_ps xnT_sb logit_ps lg_ready ex_ready chosen_ready rank_ps pos_ready "
                 "scattered").split()
        R = {n: sem("r_" + n) for n in names}

        def pe_e1(pe, g, w):
            n = w * P
            pe.wait_ge(R["xn_ready"], g + 1)
            for c in range(C):
                for i in range(w):
                    last = nc.tensor.transpose(bank[c][:, i * P:(i + 1) * P], xr[:, i, 0, c * P:(c + 1) * P],
                                               ident[:, :])
            last.then_inc(R["xnT_ps"], 1)
            pe.wait_ge(R["xnT_sb"], g + 1)
            for i in range(w):
                o = slice(i * E1, (i + 1) * E1)
                for c in range(C):
                    nc.tensor.matmul(bank[2][:, o], t0[:, c, i * P:(i + 1) * P], Wr[:, c, :],
                                     start=i == 0 and c == 0, stop=False, skip_group_check=True)
                last = nc.tensor.matmul(bank[2][:, o], ones[0:1, :], br[:, :], start=False, stop=True,
                                        skip_group_check=True)
            last.then_inc(R["logit_ps"], 1)

        def pe_e2(pe, g, w):
            flat = chosen[:, 0:w, :].rearrange("p t e -> p (t e)")
            pe.wait_ge(R["chosen_ready"], g + 1)
            nc.tensor.matmul(bank[3][:, 0:w * E1], ustrict[:, :], flat, start=True, stop=True)
            nc.tensor.matmul(bank[2][:, W // 2:W // 2 + w * E1], ones[:, :], flat, start=True, stop=True).then_inc(R["rank_ps"], 1)

        def act_e1(act, g, w):
            n = w * P
            act.wait_ge(R["xnT_ps"], g + 1)
            for c in range(C):
                last = nc.scalar.activation(t0[:, c, 0:n], bank[c][:, 0:n], ACT.Copy)
            last.then_inc(R["xnT_sb"], 1)
            act.wait_ge(R["lg_ready"], g + 1)
            nc.scalar.activation(f1["ex"][:, 0:w, :], f1["lg"][:, 0:w, :], ACT.Exp).then_inc(R["ex_ready"], 1)

        def dve_e1(dve, chain, g, w):
            chain.begin(g)
            dve.wait_ge(q2.evacuated, first_window(g) + w)
            ln_stats(dve, chain, R["var"], R["std"], g, w, first_window(g))
            dve.wait_ge(R["scattered"], 16 * 2 * first_window(g) + 16)
            for i in range(w):
                t = first_window(g) + i
                for s_ in range(2):
                    nc.vector.tensor_scalar(xr[:, i, s_, 0:D], x_cols(t, 1), mean_var[:, i, 0:1], rstd[:, i:i + 1],
                                            ALU.subtract, ALU.mult)
            last = nc.vector.tensor_copy(xr[:, 0:w, :, D:RW].bitcast(I32),
                                         place[:, ds(first_window(g) * 2, w * 2)].rearrange("p (t s a) -> p t s a", s=2, a=1))
            last.then_inc(R["xn_ready"], 1)

        def dve_e2(dve, chain, g, w):
            dve.wait_ge(R["logit_ps"], g + 1)
            router_logits(f1, chain, bank[2][:, 0:w * E1], w, E1).then_inc(R["lg_ready"], 1)

            dve.wait_ge(R["ex_ready"], g + 1)
            router_choice(f1, chain, w, E1)
            m1, m2, s = (f1[k][:, 0:w] for k in ("m1", "m2", "s"))
            chain.link(nc.vector.tensor_tensor(s, m1, m2, ALU.add))
            chain.link(nc.vector.reciprocal(s, s))
            wts = row_wt[:, ds(first_window(g) * 2, w * 2)].rearrange("p (t s) -> p t s", s=2)
            nc.vector.tensor_tensor(wts[:, :, 0], m1, s, ALU.mult)
            nc.vector.tensor_tensor(wts[:, :, 1], m2, s, ALU.mult)
            eq = [f1[k][:, 0:w, :] for k in ("eq1", "eq2")]
            nc.vector.tensor_tensor(chosen[:, 0:w, :], eq[0], eq[1], ALU.add).then_inc(R["chosen_ready"], 1)

        def dve_e3(dve, chain, g, w):
            eq = [f1[k][:, 0:w, :] for k in ("eq1", "eq2")]
            dve.wait_ge(R["rank_ps"], g + 1)
            nc.vector.tensor_copy(rank[:, 0:w, :], bank[3][:, 0:w * E1].rearrange("p (t e) -> p t e", e=E1))
            chain.link(nc.vector.tensor_copy(total[:, 0:w, :], bank[2][:, W // 2:W // 2 + w * E1].rearrange("p (t e) -> p t e", e=E1)))
            for i in range(w):
                nc.vector.tensor_tensor(rank[:, i, :], rank[:, i, :], count[:, :], ALU.add)
                chain.link(nc.vector.tensor_tensor(count[:, :], count[:, :], total[:, i, :], ALU.add))
            for s_ in range(2):
                chain.link(nc.vector.tensor_tensor(eq[s_], eq[s_], rank[:, 0:w, :], ALU.mult))
                chain.link(nc.vector.tensor_reduce(pos_f[:, 0:w, s_], eq[s_], AX, ALU.add))
            flat = pos_f[:, 0:w, :].rearrange("p t s -> p (t s)")
            nc.vector.tensor_copy(pos[:, 0:2 * w], flat).then_inc(R["pos_ready"], 1)
            chain.end()

        window_sum = sb("window_sum", [P, D], F32, graph)

        def evacuate2(dve, g, i):
            t = first_window(g) + i
            sums = sum_chain[1]
            sums.begin(t)
            wide, low = BANKS2[i] if not (isinstance(t, int) and t == 0) else BANKS2[GW - 1]
            dve.wait_ge(q2.done, t + 1)
            if not (isinstance(t, int) and t == 0):
                dve.wait_ge(q2.evacuated, t)
            sums.link(nc.vector.tensor_copy(window_sum[:, :], low[:, 0:D]))
            for part_ in range(2):
                sums.link(nc.vector.tensor_tensor(window_sum[:, :], window_sum[:, :], wide[:, part_ * D:(part_ + 1) * D],
                                                  ALU.add))
            xs = x_cols(t, 1)
            nc.vector.scalar_tensor_tensor(xs, window_sum[:, :], inv_deg[:, ds(t, 1)], xs,
                                           ALU.mult, ALU.add).then_inc(q2.evacuated, 1)

        def scatter(pool, g, w):
            pool.wait_ge(R["pos_ready"], g + 1)
            settled(pool)
            for i in range(w):
                for s_ in range(2):
                    nc.gpsimd.indirect_dma_start(
                        out=routed, out_offset=bass.IndirectOffsetOnAxis(pos[:, 2 * i + s_:2 * i + s_ + 1], axis=0),
                        in_=xr[:, i, s_, :], in_offset=None).then_inc(R["scattered"], 16)

        def nothing(g, w):
            return None

        with nc.Block() as block:
            @block.gpsimd
            def _(pool):
                pool.dma_start(spare[:, 3:4], zeros[:, 0:1], allow_slow_non_contiguous=True).then_inc(R["scattered"], 16)
                pool_begin(pool, q2, 2)
                pool_rounds(pool, q2, 0, rounds_value(pool, 1, 1))

                def rounds_between(t0_, t1):
                    r0, r1 = rounds_value(pool, t0_, 1), rounds_value(pool, t1, 1)
                    with pool.If(r1 > r0):
                        pool_rounds(pool, q2, r0, r1)

                def group(g, w):
                    t = first_window(g)
                    rounds_between(t, t + GW)
                    scatter(pool, g - 1, w)

                group(1, 1)
                with pool.Fori(2, GROUPS + 1) as g:
                    group(g, GW)
                pool_end(pool, q2, rounds_value(pool, NT, 1))
                scatter(pool, GROUPS, GW)
                pool.wait_ge(R["scattered"], 16 * 2 * NT + 16)

            @block.sync
            def _(sp):
                sp_indices(sp, q2)

            @block.tensor
            def _(pe):
                pe.sem_inc(q2.used, MH)
                steps = [nothing, lambda g, w: pe_e1(pe, g, w), lambda g, w: pe_e2(pe, g, w), nothing, nothing]
                run_graph(lambda g, i: pe_windows(pe, q2, g, i, BANKS2), steps, pe)

            @block.scalar
            def _(act):
                run_graph(lambda g, i: None, [lambda g, w: ln_sqrt(act, R["var"], R["std"], g, w), lambda g, w: act_e1(act, g, w),
                                              nothing, nothing, nothing], act)

            @block.vector
            def _(dve):
                start = Chain(dve, "count_chain", 32)
                start.begin(0)
                start.link(nc.vector.tensor_scalar(region[:, :], ts_idx[:, 0, :], float(CAP), None, ALU.mult))
                start.link(nc.vector.tensor_copy(count[:, :], region[:, :]))
                chain = Chain(dve, "layer1_chain", 64)
                sum_chain[1] = Chain(dve, "g2_sum_chain", 3)

                run_graph(dve_gather(dve, q2, evacuate2),
                          [lambda g, w, f=f: f(dve, chain, g, w) for f in (dve_e1, dve_e2, dve_e3)] + [nothing, nothing], dve)
                rows_i, tiles_i = lists[0:1, 0:E1], lists[0:1, E1:2 * E1]
                start.link(nc.vector.tensor_tensor(rows_i, count[0:1, :], region[0:1, :], ALU.subtract))
                start.link(nc.vector.tensor_scalar(tiles_i, rows_i, float(TT - 1), float(TT), ALU.add, ALU.max))
                start.link(nc.vector.tensor_single_scalar(tiles_i, tiles_i, TT.bit_length() - 1, ALU.arith_shift_right))
                start.link(nc.vector.memset(lists[0:1, 2 * E1:2 * E1 + 1], 0))
                for e in range(E1):
                    start.link(nc.vector.tensor_tensor(lists[0:1, 2 * E1 + e + 1:2 * E1 + e + 2],
                                                       lists[0:1, 2 * E1 + e:2 * E1 + e + 1],
                                                       lists[0:1, E1 + e:E1 + e + 1], ALU.add))

        graph.close()
        ffn = ctx.enter_context(ExitStack())
        W1 = sb("W1", [P, C, H], F32, ffn)
        W2 = sb("W2", [P, HC, D], F32, ffn)
        W1_high, W1_low = ([sb(f"W1_{n}{b}", [P, C, H], FR, ffn) for b in range(2)] for n in ("high", "low"))
        W2_high, W2_low = ([sb(f"W2_{n}{b}", [P, HC, D], FR, ffn) for b in range(2)] for n in ("high", "low"))
        b2 = sb("b2", [1, D], F32, ffn)
        b2_high, b2_low = ([sb(f"b2_{n}{b}", [1, D], FR, ffn) for b in range(2)] for n in ("high", "low"))
        b1 = [sb(f"b1_{b}", [P, HC], F32, ffn) for b in range(2)]
        lng = [sb(f"lng_{b}", [P, 2 * C], F32, ffn) for b in range(2)]
        one_row = sb("one_row", [1, P], FR, ffn)
        xs = sb("xs", [P, SUB, RW], F32, ffn)
        to = sb("to", [P, SUB], I32, ffn)
        to_next = sb("to_next", [P, SUB], I32, ffn)
        xe = sb("xe", [P, C, TT], F32, ffn)
        xe_high, xe_low = (sb(f"xe_{n}", [P, C, TT], FR, ffn) for n in ("high", "low"))
        hid = sb("hid", [P, HC, TT], F32, ffn)
        hid_high, hid_low = (sb(f"hid_{n}", [P, HC, TT], FR, ffn) for n in ("high", "low"))
        ys = sb("ys", [P, SUB, D], F32, ffn)
        names = ("tail_done raw_loaded small_loaded high_ready b2_split weights_ready one_ready xs_loaded xs_turned xs_read xe_high "
                 "xe_ready g1_ps gelu_done hid_high hid_ready y_ps y_ready y_out expert_done").split()
        X = {n: sem("x_" + n) for n in names}
        SMALL = 4
        PAIRS = HC // 2

        def expert_tiles(eng, body, before_expert=None, after_expert=None):
            with eng.Fori(0, E1 // 2) as pair:
                for b in range(2):
                    e = pair * 2 + b
                    if before_expert:
                        before_expert(b, e, pair)
                    tiles = eng.value_load(lists[0:1, ds(e + E1, 1)], min_val=1, max_val=NPAD // TT + 1)
                    first = eng.value_load(lists[0:1, ds(e + 2 * E1, 1)], min_val=0, max_val=E1 * (NPAD // TT + 1))
                    with eng.Fori(0, tiles) as j:
                        body(b, e, j, eng.snap(first + j))
                    if after_expert:
                        after_expert(b, e, pair)

        def all_tiles(eng):
            return eng.value_load(lists[0:1, 3 * E1:3 * E1 + 1], min_val=E1, max_val=E1 * (NPAD // TT + 1))

        def weights_ready(eng):
            return lambda b, e, pair: eng.wait_ge(X["weights_ready"], e * 3 + 3)

        def unless_last(eng, b, pair, step):
            if b == 0:
                step()
            else:
                with eng.If(pair < E1 // 2 - 1):
                    step()

        with nc.Block() as block:
            @block.sync
            def _(sp):
                with sp.Fori(0, E1) as e:
                    rows_ = sp.value_load(lists[0:1, ds(e, 1)], min_val=0, max_val=NPAD)
                    at = narrow(rows_ + e * CAP, 0, E1 * CAP - TT)
                    sp.dma_start(routed[ds(at, TT), :].rearrange("(p s) d -> p s d", p=P),
                                 filler[:, :, :]).then_inc(X["tail_done"], 16)
                sp.wait_ge(X["tail_done"], 16 * E1)

                def load(b, e, j, n):
                    at = narrow(sp.snap(e * CAP + j * TT), 0, E1 * CAP - TT)
                    sp.wait_ge(X["xs_turned"], n + CREDIT)
                    sp.wait_ge(X["xs_read"], n + CREDIT)
                    sp.dma_start(xs[:, :, :],
                                 routed[ds(at, TT), :].rearrange("(p s) d -> p s d", p=P)).then_inc(X["xs_loaded"], 16)

                expert_tiles(sp, load)
                n = all_tiles(sp)
                sp.wait_ge(X["xs_turned"], n + CREDIT)
                sp.wait_ge(X["xs_read"], n + CREDIT)
                sp.dma_start(xs[:, :, :], routed[0:TT, :].rearrange("(p s) d -> p s d", p=P)).then_inc(X["xs_loaded"], 16)
                sp.wait_ge(X["xs_loaded"], n * 16 + 16)
                settled(sp)

            @block.gpsimd
            def _(pool):
                def load_raw(e):
                    pool.dma_start(W1[:, :, :], a["L1_ffn_W1"][ds(e, 1), :, :].rearrange("a (c p) h -> p (a c) h", p=P)
                                   ).then_inc(X["raw_loaded"], 16)
                    pool.dma_start(W2[:, :, :], a["L1_ffn_W2"][ds(e, 1), :, :].rearrange("a (c p) h -> p (a c) h", p=P)
                                   ).then_inc(X["raw_loaded"], 16)

                def load_small(b, e):
                    small = ((b1[b][:, :], a["L1_ffn_b1"][ds(e, 1), :].rearrange("a (c p) -> p (a c)", p=P)),
                             (b2[:, :], a["L1_ffn_b2"][ds(e, 1), :]),
                             (lng[b][:, 0:C], a["L1_ffn_ln_g"][ds(e, 1), :].rearrange("a (c p) -> p (a c)", p=P)),
                             (lng[b][:, C:2 * C], a["L1_ffn_ln_b"][ds(e, 1), :].rearrange("a (c p) -> p (a c)", p=P)))
                    assert len(small) == SMALL
                    for dst, src in small:
                        pool.dma_start(dst, src, allow_slow_non_contiguous=True).then_inc(X["small_loaded"], 16)

                load_raw(0)
                load_small(0, 0)
                nc.gpsimd.tensor_copy(one_row[:, :], ones[0:1, :]).then_inc(X["one_ready"], 1)
                for s in range(SUB):
                    pool.dma_start(results[2 * NPAD + s * P:2 * NPAD + (s + 1) * P, :],
                                   filler[:, s, 0:D]).then_inc(X["y_out"], 16)

                def next_expert(b, e, pair):
                    pool.wait_ge(X["weights_ready"], e * 3 + 3)
                    pool.wait_ge(X["expert_done"], e + CREDIT)
                    settled(pool)

                    def load():
                        load_raw(narrow(e + 1, 1, E1 - 1))
                        load_small(1 - b, narrow(e + 1, 1, E1 - 1))

                    unless_last(pool, b, pair, load)

                def store(b, e, j, n):
                    for s in range(SUB):
                        pool.wait_ge(X["y_ready"], n * SUB + s + 1)
                        settled(pool)
                        nc.gpsimd.indirect_dma_start(
                            out=results, out_offset=bass.IndirectOffsetOnAxis(to[:, s:s + 1], axis=0),
                            in_=ys[:, s, :], in_offset=None).then_inc(X["y_out"], 16)

                expert_tiles(pool, store, next_expert)
                n = all_tiles(pool)
                store(0, 0, 0, n)
                pool.wait_ge(X["y_out"], n * (16 * SUB) + 2 * 16 * SUB)

            @block.tensor
            def _(pe):
                def turn_tile(n):
                    pe.wait_ge(X["xs_loaded"], n * 16 + 16)
                    for c in range(C):
                        for s in range(SUB):
                            o = c * TT + s * P
                            last = nc.tensor.transpose(bank[0][:, o:o + P], xs[:, s, c * P:(c + 1) * P],
                                                       ident[:, :])
                    last.then_inc(X["xs_turned"], 1)

                def halves_product(acc, weights_, moving, start, stop):
                    w_high, w_low = weights_
                    m_high, m_low = moving
                    nc.tensor.matmul(acc, w_high, m_high, start=start, stop=False)
                    nc.tensor.matmul(acc, w_high, m_low, start=False, stop=False)
                    return nc.tensor.matmul(acc, w_low, m_high, start=False, stop=stop)

                def tile(b, e, j, n):
                    pe.wait_ge(X["xe_ready"], n + 1)
                    for hc in range(HC):
                        if hc % 2 == 0:
                            pe.wait_ge(X["gelu_done"], n * HC + hc + 2)
                        o = (hc % 2) * TT
                        for c in range(C):
                            block_ = slice(hc * P, (hc + 1) * P)
                            last = halves_product(bank[1 + hc // 2][:, o:o + TT],
                                                  (W1_high[b][:, c, block_], W1_low[b][:, c, block_]),
                                                  (xe_high[:, c, :], xe_low[:, c, :]), c == 0, c == C - 1)
                        if hc % 2 == 1:
                            last.then_inc(X["g1_ps"], 1)
                    turn_tile(n + 1)
                    pe.wait_ge(X["y_ready"], n * SUB + SUB)
                    for s in range(SUB):
                        for b2_half in (b2_high, b2_low):
                            nc.tensor.matmul(bank[5 + s][:, 0:D], one_row[:, :], b2_half[b][:, :],
                                             start=b2_half is b2_high, stop=False)
                    for hc in range(HC):
                        if hc % 2 == 0:
                            pe.wait_ge(X["hid_ready"], n * PAIRS + hc // 2 + 1)
                        for s in range(SUB):
                            tokens = slice(s * P, (s + 1) * P)
                            last = halves_product(bank[5 + s][:, 0:D], (hid_high[:, hc, tokens], hid_low[:, hc, tokens]),
                                                  (W2_high[b][:, hc, :], W2_low[b][:, hc, :]), False, hc == HC - 1)
                    last.then_inc(X["y_ps"], 1)

                def expert_end(b, e, pair):
                    nc.tensor.matmul(bank[7][:, 0:P], zeros[:, 0:P], zeros[:, 0:P], start=True,
                                     stop=True).then_inc(X["expert_done"], 1)

                for s in range(SUB):
                    last = nc.tensor.matmul(bank[5 + s][:, 0:D], zeros[:, 0:P], zeros[:, 0:D], start=True, stop=True)
                last.then_inc(X["y_ps"], 1)
                pe.sem_inc(X["xs_turned"], CREDIT)
                pe.sem_inc(X["expert_done"], CREDIT)
                pe.wait_ge(X["one_ready"], 1)
                turn_tile(0)
                expert_tiles(pe, tile, weights_ready(pe), expert_end)

            @block.scalar
            def _(act):
                act.sem_inc(X["gelu_done"], HC)

                def tile(b, e, j, n):
                    for pair in range(PAIRS):
                        act.wait_ge(X["g1_ps"], n * PAIRS + pair + 1)
                        for hc in (2 * pair, 2 * pair + 1):
                            o = (hc % 2) * TT
                            nc.scalar.activation(hid[:, hc, :], bank[1 + pair][:, o:o + TT], ACT.Gelu,
                                                 bias=b1[b][:, hc:hc + 1]).then_inc(X["gelu_done"], 1)
                        act.wait_ge(X["gelu_done"], n * HC + HC + 2 * pair + 2)
                        both = slice(2 * pair, 2 * pair + 2)
                        nc.scalar.activation(hid_high[:, both, :], hid[:, both, :], ACT.Copy).then_inc(X["hid_high"], 1)

                def split(b, e):
                    act.wait_ge(X["raw_loaded"], e * 32 + 32)
                    nc.scalar.activation(W1_high[b][:, :, :], W1[:, :, :], ACT.Copy).then_inc(X["high_ready"], 1)
                    nc.scalar.activation(W2_high[b][:, :, :], W2[:, :, :], ACT.Copy).then_inc(X["high_ready"], 1)

                split(0, 0)
                expert_tiles(act, tile, weights_ready(act), lambda b, e, pair: unless_last(
                    act, b, pair, lambda: split(1 - b, e + 1)))

            @block.vector
            def _(dve):
                chain = Chain(dve, "tile_chain", 1)

                def leave(n):
                    dve.wait_ge(X["y_out"], n * (16 * SUB) + 16 * SUB)
                    chain.begin(n)
                    chain.link(nc.vector.tensor_copy(to[:, :], to_next[:, :]))

                def results_out(n):
                    dve.wait_ge(X["y_ps"], n + 1)
                    for s in range(SUB):
                        nc.vector.tensor_copy(ys[:, s, :], bank[5 + s][:, 0:D]).then_inc(X["y_ready"], 1)

                def tile(b, e, j, n):
                    dve.wait_ge(X["xs_turned"], CREDIT + n + 1)
                    for c in range(C):
                        last = nc.vector.tensor_scalar(xe[:, c, :], bank[0][:, c * TT:(c + 1) * TT], lng[b][:, c:c + 1],
                                                       lng[b][:, C + c:C + c + 1], ALU.mult, ALU.add)
                    last.then_inc(X["xe_high"], 1)
                    dve.wait_ge(X["xe_high"], 2 * n + 1)
                    nc.vector.tensor_copy(xe_high[:, :, :], xe[:, :, :]).then_inc(X["xe_high"], 1)
                    dve.wait_ge(X["xe_high"], 2 * n + 2)
                    nc.vector.tensor_tensor(xe_low[:, :, :], xe[:, :, :], xe_high[:, :, :].bitcast(F32),
                                            ALU.subtract).then_inc(X["xe_ready"], 1)
                    leave(n)
                    dve.wait_ge(X["xs_loaded"], n * 16 + 16)
                    nc.vector.tensor_copy(to_next[:, :], xs[:, :, D].bitcast(I32)).then_inc(X["xs_read"], 1)
                    dve.wait_ge(X["xs_read"], CREDIT + n + 1)
                    results_out(n)
                    for pair in range(PAIRS):
                        dve.wait_ge(X["hid_high"], n * PAIRS + pair + 1)
                        both = slice(2 * pair, 2 * pair + 2)
                        nc.vector.tensor_tensor(hid_low[:, both, :], hid[:, both, :], hid_high[:, both, :].bitcast(F32),
                                                ALU.subtract).then_inc(X["hid_ready"], 1)

                nc.vector.tensor_copy(to_next[:, :], filler[:, :, D].bitcast(I32)).then_inc(X["xs_read"], CREDIT)
                dve.wait_ge(X["xs_read"], CREDIT)
                def split(b, e):
                    dve.wait_ge(X["high_ready"], e * 2 + 1)
                    nc.vector.tensor_tensor(W1_low[b][:, :, :], W1[:, :, :], W1_high[b][:, :, :].bitcast(F32),
                                            ALU.subtract).then_inc(X["weights_ready"], 1)
                    dve.wait_ge(X["small_loaded"], e * (16 * SMALL) + 16 * SMALL)
                    nc.vector.tensor_copy(b2_high[b][:, :], b2[:, :]).then_inc(X["b2_split"], 1)
                    dve.wait_ge(X["high_ready"], e * 2 + 2)
                    nc.vector.tensor_tensor(W2_low[b][:, :, :], W2[:, :, :], W2_high[b][:, :, :].bitcast(F32),
                                            ALU.subtract).then_inc(X["weights_ready"], 1)
                    dve.wait_ge(X["b2_split"], e + 1)
                    nc.vector.tensor_tensor(b2_low[b][:, :], b2[:, :], b2_high[b][:, :].bitcast(F32),
                                            ALU.subtract).then_inc(X["weights_ready"], 1)

                split(0, 0)
                expert_tiles(dve, tile, weights_ready(dve), lambda b, e, pair: unless_last(
                    dve, b, pair, lambda: split(1 - b, e + 1)))
                n = all_tiles(dve)
                leave(n)
                results_out(n)
        ffn.close()

        comb = ctx.enter_context(ExitStack())
        y = [sb(f"y{b}", [P, GW, 2 * D], F32, comb) for b in range(2)]
        y_landed = [sem(f"y_landed{b}") for b in range(2)]
        c_half, c_used, c_out = (sem("c_" + n) for n in ("half", "used", "out"))

        def all_groups(eng, body):
            with eng.Fori(0, GROUPS // 2) as pair:
                for b in range(2):
                    body(pair * 2 + b, b, pair, GW)
            body(GROUPS, 0, GROUPS // 2, 1)

        assert GROUPS % 2 == 0

        with nc.Block() as block:
            @block.scalar
            def _(act):
                def load(g, b, pair, w):
                    act.wait_ge(c_used, g * GW + GW)
                    act.dma_start(y[b][:, 0:w, :],
                                  results[ds(g * (2 * W), w * 2 * P), :].rearrange("(t p s) d -> p t (s d)", p=P, s=2)
                                  ).then_inc(y_landed[b], 16)

                all_groups(act, load)

            @block.vector
            def _(dve):
                dve.sem_inc(c_used, 2 * GW)

                def group(g, b, pair, w):
                    dve.wait_ge(y_landed[b], pair * 16 + 16)
                    for s in range(2):
                        for i in range(w):
                            t = g * GW + i
                            if s == 1 and i == 0:
                                dve.wait_ge(c_half, g + 1)
                            last = nc.vector.scalar_tensor_tensor(
                                x_cols(t, 1), y[b][:, i, s * D:(s + 1) * D], row_wt[:, ds(t * 2 + s, 1)], x_cols(t, 1),
                                ALU.mult, ALU.add)
                            if s == 1:
                                last.then_inc(c_used, 1)
                        if s == 0:
                            last.then_inc(c_half, 1)

                all_groups(dve, group)

            @block.sync
            def _(sp):
                with sp.Fori(0, GROUPS) as g:
                    sp.wait_ge(c_used, g * GW + 3 * GW)
                    sp.dma_start(out[ds(g * W, W), :].rearrange("(t p) d -> p t d", p=P),
                                 x_cols(g * GW, GW).rearrange("p (t d) -> p t d", d=D)).then_inc(c_out, 16)
                sp.wait_ge(c_used, NT + 2 * GW)
                sp.dma_start(out[GROUPS * W:N, :], x_res[0:N - GROUPS * W, (NT - 1) * D:NT * D]).then_inc(c_out, 16)
                sp.wait_ge(c_out, 16 * (GROUPS + 1))


_INS = ["x", "src", "dst", "edge_type_16", "L0_gnn_relvectors", "L0_gnn_w_ih", "L0_gnn_w_hh", "L0_gnn_b_ih",
        "L0_gnn_b_hh", "L0_ffn_sW1", "L0_ffn_sb1", "L0_ffn_sW2", "L0_ffn_sb2", "L0_ffn_sW3", "L0_ffn_sb3",
        "L0_ffn_eW1", "L0_ffn_eb1", "L0_ffn_eW2", "L0_ffn_eb2", "L0_ffn_eW3", "L0_ffn_eb3", "L0_ffn_gW",
        "L0_ffn_gb", "L1_gnn_W", "L1_gnn_b", "L1_ffn_Wr", "L1_ffn_br", "L1_ffn_ln_g", "L1_ffn_ln_b",
        "L1_ffn_W1", "L1_ffn_b1", "L1_ffn_W2", "L1_ffn_b2"]


def kernel(**inputs):
    import numpy as _np
    import concourse.bacc as _bacc
    from concourse import mybir as _mybir
    from concourse.bass_utils import run_bass_kernel_spmd as _run

    nc = _bacc.Bacc("TRN2", target_bir_lowering=False, num_devices=1)
    arrays, args = {}, {}
    for name in _INS:
        v = _np.ascontiguousarray(inputs[name])
        arrays[f"in_{name}_dram"] = v
        args[name] = nc.dram_tensor(f"in_{name}_dram", v.shape, _mybir.dt.from_np(v.dtype), kind="ExternalInput").ap()
    out = nc.dram_tensor("out_0_dram", (N, D), _mybir.dt.float32, kind="ExternalOutput").ap()
    program(nc, args, out)
    r = _run(nc, [arrays], core_ids=[0])
    return r.results[0]["out_0_dram"]
```

```python
from contextlib import ExitStack

import concourse.bass as bass
from concourse import mybir

F32 = mybir.dt.float32
BF16 = mybir.dt.bfloat16
FR = mybir.dt.float32r
I32 = mybir.dt.int32
ALU = mybir.AluOpType
ACT = mybir.ActivationFunctionType
AX = mybir.AxisListType.X
ds = bass.ds

P = 128
N = 6250
D = 256
C = D // P
NE = 100000
RELS = 16
NT = (N + P - 1) // P
NPAD = NT * P
GW = 4
GROUPS = NT // GW
W = GW * P
EP, EJ = 112, 7
CHUNKS = EP * EJ
U = 4
M = 4
MH = 8
KCOLS = CHUNKS + U
PARTS = 3
BIG = float(1 << 20)
EPS = 1e-5
H = 1024
HC = H // P
E0 = 4
E1 = 8
TT = 256
SUB = TT // P
CAP = NPAD + TT
YB = 4
RW = D + 1
TURN_CREDIT = 3
CREDIT = 1
LOOP = "the loop's bounds and the edge windows keep it inside"


def program(nc, a, out):
    assert NT == GROUPS * GW + 1 and EP * EJ * P >= NE

    def narrow(value, low, high):
        return nc.s_assert_within(value, low, high, skip_runtime_bounds_check_because=LOOP)

    with ExitStack() as ctx:
        def sem(name):
            return ctx.enter_context(nc.semaphore(name))

        def sb(name, shape, dt, where=None):
            return (where or ctx).enter_context(nc.sbuf_tensor(name, shape, dt))

        bank = [ctx.enter_context(nc.psum_tensor(f"bank{i}", [P, 512], F32)) for i in range(8)]

        table1 = nc.dram_tensor("table1", (NPAD, PARTS * D), BF16).ap()
        table2 = nc.dram_tensor("table2", (NPAD, PARTS * D), BF16).ap()
        routed = nc.dram_tensor("routed", (E1 * CAP, RW), F32).ap()
        results = nc.dram_tensor("results", (2 * NPAD + TT, D), F32).ap()

        x_res = sb("x_res", [P, NT * D], F32)
        ident = sb("ident", [P, P], F32)
        ustrict = sb("ustrict", [P, P], F32)
        ones = sb("ones", [P, P], F32)
        eps = sb("eps", [P, 1], F32)
        zeros = sb("zeros", [P, D], F32)
        inv_deg = sb("inv_deg", [P, NT], F32)
        row_wt = sb("row_wt", [P, NT * 2], F32)
        place = sb("place", [P, NT * 2], I32)
        filler = sb("filler", [P, SUB, RW], F32)
        lists = sb("lists", [1, 3 * E1 + 1], I32)
        ts_idx = sb("ts_idx", [P, GW, E1], F32)

        def x_cols(first, count):
            return x_res[:, ds(first * D, count * D)]

        graph = ctx.enter_context(ExitStack())
        dstT = sb("dstT", [P, KCOLS], F32, graph)
        typeT = sb("typeT", [P, KCOLS], F32, graph)
        srcT = sb("srcT", [P, KCOLS], I32, graph)
        windows = sb("windows", [1, 3 * NT], I32, graph)
        rounds = sb("rounds", [1, NT + 1], I32, graph)
        early = sb("early", [1, NT], I32, graph)
        tbase = sb("tbase", [P, NT], F32, graph)
        iota_row = sb("iota_row", [P, P], BF16, graph)
        zlhs = zeros[:, 0:P // 2].bitcast(BF16)
        zrhs = zeros[:, 0:2 * D // 2].bitcast(BF16)
        ln_mean = sb("ln_mean", [P, NT], F32, graph)
        ln_rstd = sb("ln_rstd", [P, NT], F32, graph)

        consts_ready = sem("consts_ready")
        filler_clear = sem("filler_clear")
        loads_done = sem("loads_done")
        x_loaded = sem("x_loaded")
        x_tail_loaded = sem("x_tail_loaded")

        waits_passed = sem("waits_passed")

        def settled(eng):
            eng.sem_inc(waits_passed, 1)

        def halves(w):
            return [(half, 2 * half, min(2, w - 2 * half)) for half in range((w + 1) // 2)]

        class Chain:

            def __init__(self, eng, name, per):
                self.eng, self.sem, self.per = eng, sem(name), per

            def begin(self, round_):
                base = round_ * self.per
                self.base, self.n = base if isinstance(base, int) else self.eng.snap(base), 0

            def link(self, instruction):
                self.n += 1
                instruction.then_inc(self.sem, 1)
                self.eng.wait_ge(self.sem, self.base + self.n)

            def end(self):
                assert self.n <= self.per, self.n
                if self.n < self.per:
                    self.eng.sem_inc(self.sem, self.per - self.n)

        def first_window(g):
            return 0 if isinstance(g, int) and g == 0 else g * GW - (GW - 1)

        def ln_stats(dve, chain, var_ready, std_ready, g, w, w0):
            ln_variance(dve, chain, var_ready, w, w0, stats, mean_var)
            ln_rstd_(dve, chain, std_ready, g, w, stdev, rstd)

        def ln_variance(dve, chain, var_ready, w, w0, stats_, mean_var_):
            settled(dve)
            for i in range(w):
                last = nc.vector.bn_stats(stats_[:, i, :], x_cols(w0 + i, 1))
            chain.link(last)
            settled(dve)
            for i in range(w):
                last = nc.vector.bn_aggr(mean_var_[:, i, :], stats_[:, i, :])
            last.then_inc(var_ready, 1)

        def ln_rstd_(dve, chain, std_ready, g, w, stdev_, rstd_):
            dve.wait_ge(std_ready, g + 1)
            chain.link(nc.vector.reciprocal(rstd_[:, 0:w], stdev_[:, 0:w]))

        def ln_apply(w0, w, out_=None, mean_var_=None, rstd_=None):
            out_, mean_var_, rstd_ = out_ or h4, mean_var_ or mean_var, rstd_ or rstd
            for i in range(w):
                last = nc.vector.tensor_scalar(out_[:, i, :], x_cols(w0 + i, 1), mean_var_[:, i, 0:1],
                                               rstd_[:, i:i + 1], ALU.subtract, ALU.mult)
            return last

        def ln_sqrt(act, var_ready, std_ready, g, w, mean_var_=None, stdev_=None):
            mean_var_, stdev_ = mean_var_ or mean_var, stdev_ or stdev
            act.wait_ge(var_ready, g + 1)
            nc.scalar.activation(stdev_[:, 0:w], mean_var_[:, 0:w, 1], ACT.Sqrt,
                                 bias=eps[:, 0:1]).then_inc(std_ready, 1)

        setup = ctx.enter_context(ExitStack())
        weights = {}

        Wr = sb("Wr", [P, C, E1], F32, graph)
        br = sb("br", [1, E1], F32, graph)
        layer0 = graph.enter_context(ExitStack())

        def layer_buffers(n, where):
            return (sb(f"rows{n}", [P, M * U, PARTS * D], BF16, where), sb(f"idx{n}", [P, M * U], I32, where),
                    sb(f"onehot{n}", [P, MH * U, P], BF16, where), sb(f"spare{n}", [P, 4], F32, where),
                    sb(f"stats{n}", [P, GW, 6], F32, where), sb(f"mean_var{n}", [P, GW, 2], F32, where),
                    sb(f"stdev{n}", [P, GW], F32, where), sb(f"rstd{n}", [P, GW], F32, where))

        rows, idx, onehot, spare, stats, mean_var, stdev, rstd = layer_buffers(0, layer0)
        typehot = sb("typehot", [P, MH * U, RELS], BF16, layer0)
        h4 = sb("h4", [P, GW, D], F32, layer0)
        part = sb("part", [P, GW, PARTS * D], BF16, layer0)
        rest = sb("rest", [P, 2, 2, D], F32, layer0)

        def wt(name, shape):
            weights[name] = sb(name, shape, F32, layer0)
            return weights[name]

        def split_wt(name, shape):
            return tuple(sb(f"{name}_{half}", shape, FR, layer0) for half in ("high", "low"))

        wihT = split_wt("wihT", [P, C, 3 * D])
        whhT = split_wt("whhT", [P, C, 3 * D])
        gcnT = wt("gcnT", [P, C, D])
        sW1 = wt("sW1", [P, C, D])
        eW1 = wt("eW1", [P, E0, C, P])
        gW = wt("gW", [P, C, E0])
        gcn_b = wt("gcn_b", [1, D])
        relvec = wt("relvec", [RELS, D])
        sW2 = wt("sW2", [P, C, P])
        sW3 = wt("sW3", [P, D])
        eW2 = wt("eW2", [P, E0, 64])
        eW3 = wt("eW3", [P, 2, D])
        sel = wt("sel", [E0, E0 * 64])
        bih = wt("bih", [P, 6])
        bhh = wt("bhh", [P, 6])
        brz = wt("brz", [P, 4])
        b_l1 = wt("b_l1", [P, 6])
        b_l2 = wt("b_l2", [P, 3])
        b_l3 = wt("b_l3", [E0 + 1, D])
        gb = wt("gb", [1, E0])

        edge_i = [sb(f"edge_i{n}", [P, EJ * P], I32, setup) for n in range(3)]
        edge_f = [sb(f"edge_f{n}", [P, EJ * P], F32, setup) for n in range(3)]
        iw = [sb(f"iw{n}", [P, n_], I32, setup) for n, n_ in enumerate((P, NT, NT * EJ, EJ, GW * E1))]
        wlow = sb("wlow", [P, NT, EJ], F32, setup)
        kidx = sb("kidx", [P, EJ], F32, setup)
        kmb = sb("kmb", [P, EJ], F32, setup)
        ov = sb("ov", [P, NT, EJ], F32, setup)
        ov2 = sb("ov2", [P, NT, EJ], F32, setup)
        bmm = sb("bmm", [P, 2, EJ], F32, setup)
        lohi = sb("lohi", [P, 2, NT], F32, setup)
        col = sb("col", [64, 8], F32, setup)
        coli = sb("coli", [64, 2], I32, setup)
        ring_words = rows[:, :, :].rearrange("p s d -> p (s d)").bitcast(F32)
        wraw = [ring_words[:, j0 * D:j1 * D].rearrange("p (j i) -> p j i", i=D) for j0, j1 in ((0, 6), (6, 12), (12, 14))]

        turns = [(stats, mean_var, stdev, rstd, h4, part, rest),
                 (sb("stats_b", [P, GW, 6], F32, setup), sb("mean_var_b", [P, GW, 2], F32, setup),
                  sb("stdev_b", [P, GW], F32, setup), sb("rstd_b", [P, GW], F32, setup),
                  sb("h4_b", [P, GW, D], F32, setup), sb("part_b", [P, GW, PARTS * D], BF16, setup),
                  sb("rest_b", [P, 2, 2, D], F32, setup))]

        def table1_groups(eng, stages):
            with eng.Fori(0, GROUPS // 2) as pair:
                both = [stages(pair * 2 + turn_, GW, turns[turn_]) for turn_ in range(2)]
                for steps in zip(*both):
                    for step in steps:
                        step()
            for step in stages(GROUPS, 1, turns[0]):
                step()

        assert GROUPS % 2 == 0

        edges_clear = sem("edges_clear")
        edges_loaded = sem("edges_loaded")
        edges_float = sem("edges_float")
        edges_turned = sem("edges_turned")
        edges_copied = sem("edges_copied")
        lohi_ready = sem("lohi_ready")
        lohi_turned = sem("lohi_turned")
        col_ready = sem("col_ready")
        row_ready = sem("row_ready")
        raw_turned = sem("raw_turned")
        raw_copied = sem("raw_copied")
        raw_high = sem("raw_high")
        iotas = sem("iotas")
        s_var = sem("s_var")
        s_std = sem("s_std")
        s_h = sem("s_h")
        s_hi = sem("s_hi")
        s_r1 = sem("s_r1")
        s_mid = sem("s_mid")
        s_r2 = sem("s_r2")
        s_lo = sem("s_lo")
        s_out = sem("s_out")
        s_left = sem("s_left")
        WEIGHT_LOADS = 30

        with nc.Block() as block:
            @block.sync
            def _(sp):
                sp.wait_ge(edges_clear, 1)
                full = NE // (EJ * P)
                left = NE - full * EJ * P
                for n, name in enumerate(("dst", "src", "edge_type_16")):
                    e = a[name]
                    sp.dma_start(edge_i[n][0:full, :],
                                 e[0:full * EJ * P].rearrange("(p c) -> p c", p=full)).then_inc(edges_loaded, 16)
                    sp.dma_start(edge_i[n][full:full + 1, 0:left],
                                 e[full * EJ * P:NE].rearrange("(p c) -> p c", p=1)).then_inc(edges_loaded, 16)
                sp.dma_start(x_res[:, 0:(NT - 1) * D].rearrange("p (t d) -> p t d", d=D),
                             a["x"][0:(NT - 1) * P, :].rearrange("(t p) d -> p t d", p=P)).then_inc(x_loaded, 16)
                sp.dma_start(x_res[0:N - (NT - 1) * P, (NT - 1) * D:NT * D],
                             a["x"][(NT - 1) * P:N, :]).then_inc(x_tail_loaded, 16)
                sp.sem_inc(s_left, CREDIT + 1)

                def store(g, w, buffers):
                    part_ = buffers[5]
                    sp.wait_ge(s_lo, TURN_CREDIT + 2 * g + (2 if w > 1 else 1))
                    sp.dma_start(table1[ds(g * W, w * P), :].rearrange("(t p) d -> p t d", p=P),
                                 part_[:, 0:w, :]).then_inc(s_out, 16)
                    sp.wait_ge(s_out, 16 * g + 16)
                    sp.sem_inc(s_left, 1)

                table1_groups(sp, lambda g, w, buffers: [lambda: store(g, w, buffers)])

            @block.gpsimd
            def _(pool):
                nc.gpsimd.iota(iw[0][:, :], pattern=[[1, P]], base=0, channel_multiplier=0).then_inc(iotas, 1)
                nc.gpsimd.iota(iw[1][:, :], pattern=[[P, NT]], base=0, channel_multiplier=0).then_inc(iotas, 1)
                nc.gpsimd.iota(iw[2][:, :], pattern=[[P, NT], [0, EJ]], base=0, channel_multiplier=0).then_inc(iotas, 1)
                nc.gpsimd.iota(iw[3][:, :], pattern=[[1, EJ]], base=0, channel_multiplier=EJ).then_inc(iotas, 1)
                nc.gpsimd.iota(iw[4][:, :], pattern=[[0, GW], [1, E1]], base=0, channel_multiplier=0).then_inc(iotas, 1)
                nc.gpsimd.iota(place[:, :], pattern=[[2 * P, NT], [1, 2]], base=0, channel_multiplier=2)
                nc.gpsimd.memset(filler[:, :, :], 0.0).then_inc(filler_clear, 1)
                pool.wait_ge(filler_clear, 1)
                nc.gpsimd.iota(filler[:, :, D:RW].bitcast(I32), pattern=[[1, SUB], [1, 1]], base=2 * NPAD,
                               channel_multiplier=SUB)
                nc.gpsimd.memset(ident[:, :], 0.0).then_inc(consts_ready, 1)
                nc.gpsimd.memset(ones[:, :], 1.0).then_inc(consts_ready, 1)
                nc.gpsimd.memset(zeros[:, :], 0.0).then_inc(consts_ready, 1)
                nc.gpsimd.memset(eps[:, :], EPS).then_inc(consts_ready, 1)
                pool.wait_ge(consts_ready, 4)
                nc.gpsimd.affine_select(out=ident[:, :], in_=ident[:, :], compare_op=ALU.not_equal, fill=1.0,
                                        base=0, pattern=[[-1, P]], channel_multiplier=1).then_inc(consts_ready, 1)
                nc.gpsimd.affine_select(out=ustrict[:, :], in_=ones[:, :], compare_op=ALU.is_gt, fill=0.0,
                                        base=0, pattern=[[1, P]], channel_multiplier=-1).then_inc(consts_ready, 1)

            @block.scalar
            def _(act):
                n = 0

                def load(dst, src):
                    nonlocal n
                    n += 1
                    act.dma_start(dst, src, allow_slow_non_contiguous=True).then_inc(loads_done, 16)

                load(wraw[0][:, :, :], a["L0_gnn_w_ih"].rearrange("(j p) i -> p j i", p=P))
                load(wraw[1][:, :, :], a["L0_gnn_w_hh"].rearrange("(j p) i -> p j i", p=P))
                load(wraw[2][:, :, :], a["L1_gnn_W"].rearrange("(j p) i -> p j i", p=P))
                load(relvec[:, :], a["L0_gnn_relvectors"])
                load(bih[:, :], a["L0_gnn_b_ih"].rearrange("(j p) -> p j", p=P))
                load(bhh[:, :], a["L0_gnn_b_hh"].rearrange("(j p) -> p j", p=P))
                load(sW1[:, :, :], a["L0_ffn_sW1"].rearrange("(c p) o -> p c o", p=P))
                load(sW2[:, :, :], a["L0_ffn_sW2"].rearrange("(c p) o -> p c o", p=P))
                load(sW3[:, :], a["L0_ffn_sW3"])
                for e in range(E0):
                    load(eW1[:, e, :, :], a["L0_ffn_eW1"][e].rearrange("(c p) o -> p c o", p=P))
                load(eW2[:, :, :], a["L0_ffn_eW2"].rearrange("e p o -> p e o"))
                load(eW3[:, :, :], a["L0_ffn_eW3"].rearrange("(q r) k o -> (r k) q o", r=2))
                load(gW[:, :, :], a["L0_ffn_gW"].rearrange("(c p) o -> p c o", p=P))
                load(Wr[:, :, :], a["L1_ffn_Wr"].rearrange("(c p) o -> p c o", p=P))
                load(b_l1[:, 0:2], a["L0_ffn_sb1"].rearrange("(j p) -> p j", p=P))
                load(b_l1[:, 2:6], a["L0_ffn_eb1"].rearrange("e p -> p e"))
                load(b_l2[:, 0:1], a["L0_ffn_sb2"].rearrange("(p j) -> p j", j=1))
                load(b_l2[:, 1:3], a["L0_ffn_eb2"].rearrange("(q r) k -> (r k) q", r=2))
                load(b_l3[0:E0, :], a["L0_ffn_eb3"])
                load(b_l3[E0:E0 + 1, :], a["L0_ffn_sb3"].rearrange("(j p) -> j p", j=1))
                load(gb[:, :], a["L0_ffn_gb"].rearrange("(j p) -> j p", j=1))
                load(gcn_b[:, :], a["L1_gnn_b"].rearrange("(j p) -> j p", j=1))
                load(br[:, :], a["L1_ffn_br"].rearrange("(j p) -> j p", j=1))
                weights["loads"] = n

                def stages(g, w, buffers):
                    _, mean_var_, stdev_, _, h4_, part_, rest_ = buffers

                    def high():
                        for half, lo, k in halves(w):
                            act.wait_ge(s_h, g + 1)
                            act.wait_ge(s_left, g + CREDIT)
                            nc.scalar.activation(part_[:, lo:lo + k, 0:D], h4_[:, lo:lo + k, :],
                                                 ACT.Copy).then_inc(s_hi, 1)

                    def further(column, remainders, done):
                        for half, lo, k in halves(w):
                            act.wait_ge(remainders, 2 * g + half + 1)
                            nc.scalar.activation(part_[:, lo:lo + k, column * D:(column + 1) * D], rest_[:, half, 0:k, :],
                                                 ACT.Copy).then_inc(done, 1)

                    return [lambda: ln_sqrt(act, s_var, s_std, g, w, mean_var_, stdev_), high,
                            lambda: further(1, s_r1, s_mid), lambda: further(2, s_r2, s_lo)]

                turned = 0
                for dst, blocks in ((wihT, 6), (whhT, 6)):
                    for c in range(C):
                        for j0 in range(0, blocks, 4):
                            k = min(4, blocks - j0)
                            turned += 1
                            act.wait_ge(raw_turned, turned)
                            nc.scalar.activation(dst[0][:, c, j0 * P:(j0 + k) * P], bank[(turned - 1) % 6][:, 0:k * P],
                                                 ACT.Copy).then_inc(raw_high, 1)
                act.wait_ge(consts_ready, 4)
                act.sem_inc(s_mid, TURN_CREDIT)
                act.sem_inc(s_lo, TURN_CREDIT)
                table1_groups(act, stages)
                act.wait_ge(loads_done, 16 * n)

            @block.vector
            def _(dve):
                chain = Chain(dve, "setup_chain", 64)
                chain.begin(0)
                nc.vector.memset(edge_i[0][:, :], -1)
                nc.vector.memset(edge_i[1][:, :], 0)
                nc.vector.memset(edge_i[2][:, :], 0)
                nc.vector.memset(x_res[:, (NT - 1) * D:NT * D], 0.0).then_inc(edges_clear, 1)
                nc.vector.memset(dstT[:, CHUNKS:KCOLS], -1.0)
                nc.vector.memset(typeT[:, CHUNKS:KCOLS], 0.0)
                nc.vector.memset(srcT[:, CHUNKS:KCOLS], 0)
                dve.wait_ge(iotas, 5)
                nc.vector.tensor_copy(iota_row[:, :], iw[0][:, :])
                nc.vector.tensor_copy(tbase[:, :], iw[1][:, :])
                nc.vector.tensor_copy(wlow[:, :, :], iw[2][:, :].rearrange("p (t j) -> p t j", j=EJ))
                nc.vector.tensor_copy(ts_idx[:, :, :], iw[4][:, :].rearrange("p (t j) -> p t j", j=E1))
                nc.vector.tensor_scalar(kmb[:, :], iw[3][:, :], BIG, None, ALU.subtract)
                chain.link(nc.vector.tensor_scalar(kidx[:, :], iw[3][:, :], 1.0, None, ALU.add))
                dve.wait_ge(edges_loaded, 6 * 16)
                for n in range(3):
                    nc.vector.tensor_copy(edge_f[n][0:EP, :], edge_i[n][0:EP, :]).then_inc(edges_float, 1)
                dve.wait_ge(edges_float, 3)
                d3 = edge_f[0][0:EP, :].rearrange("p (j e) -> p j e", e=P)
                nc.vector.tensor_reduce(bmm[0:EP, 0, :], d3, AX, ALU.max)
                pad = edge_i[0][0:EP, :].bitcast(F32)
                chain.link(nc.vector.tensor_scalar(pad, edge_f[0][0:EP, :], 0.0, BIG, ALU.is_lt, ALU.mult))
                chain.link(nc.vector.tensor_tensor(pad, pad, edge_f[0][0:EP, :], ALU.add))
                chain.link(nc.vector.tensor_reduce(bmm[0:EP, 1, :], pad.rearrange("p (j e) -> p j e", e=P), AX, ALU.min))
                top = bmm[0:EP, 0, :].unsqueeze(1).to_broadcast([EP, NT, EJ])
                low = bmm[0:EP, 1, :].unsqueeze(1).to_broadcast([EP, NT, EJ])
                nc.vector.tensor_tensor(ov[0:EP], top, wlow[0:EP], ALU.is_ge)
                chain.link(nc.vector.scalar_tensor_tensor(ov2[0:EP], wlow[0:EP], float(P), low, ALU.add, ALU.is_gt))
                chain.link(nc.vector.tensor_tensor(ov[0:EP], ov[0:EP], ov2[0:EP], ALU.mult))
                kb = kmb[0:EP, :].unsqueeze(1).to_broadcast([EP, NT, EJ])
                kp = kidx[0:EP, :].unsqueeze(1).to_broadcast([EP, NT, EJ])
                chain.link(nc.vector.tensor_tensor(ov2[0:EP], ov[0:EP], kb, ALU.mult))
                nc.vector.tensor_reduce(lohi[0:EP, 0, :], ov2[0:EP], AX, ALU.min)
                chain.link(nc.vector.tensor_tensor(ov[0:EP], ov[0:EP], kp, ALU.mult))
                nc.vector.tensor_reduce(lohi[0:EP, 1, :], ov[0:EP], AX, ALU.max).then_inc(lohi_ready, 1)
                for n in range(3):
                    dst = (dstT, srcT, typeT)[n]
                    view = dst[:, 0:CHUNKS].rearrange("p (k j) -> p j k", j=EJ)
                    for half in range(2):
                        dve.wait_ge(edges_turned, 2 * n + half + 1)
                        j0, k = (0, 4) if half == 0 else (4, 3)
                        nc.vector.tensor_copy(
                            view[:, j0:j0 + k, :],
                            bank[2 * n + half][:, 0:k * EP].rearrange("p (j k) -> p j k", k=EP)).then_inc(edges_copied, 1)
                dve.wait_ge(lohi_turned, 1)
                nc.vector.tensor_reduce(col[0:NT, 0:1], bank[6][0:NT, 0:EP], AX, ALU.min)
                chain.link(nc.vector.tensor_reduce(col[0:NT, 1:2], bank[6][0:NT, EP:2 * EP], AX, ALU.max))
                nc.vector.tensor_scalar(col[0:NT, 2:3], col[0:NT, 1:2], 1.0, None, ALU.max)
                chain.link(nc.vector.tensor_scalar(col[0:NT, 3:4], col[0:NT, 0:1], BIG, None, ALU.add))
                chain.link(nc.vector.tensor_scalar(col[0:NT, 4:5], col[0:NT, 2:3], 1.0, None, ALU.subtract))
                chain.link(nc.vector.tensor_tensor(col[0:NT, 5:6], col[0:NT, 3:4], col[0:NT, 4:5], ALU.min))
                chain.link(nc.vector.tensor_tensor(col[0:NT, 6:7], col[0:NT, 2:3], col[0:NT, 5:6], ALU.subtract))
                chain.link(nc.vector.tensor_scalar(coli[0:NT, 0:1], col[0:NT, 6:7], float(U - 1), None, ALU.add))
                chain.link(nc.vector.tensor_single_scalar(coli[0:NT, 1:2], coli[0:NT, 0:1], U.bit_length() - 1,
                                                          ALU.arith_shift_right))
                nc.vector.tensor_copy(col[0:NT, 7:8], coli[0:NT, 1:2]).then_inc(col_ready, 1)
                dve.wait_ge(row_ready, 1)
                chain.link(nc.vector.tensor_copy(windows[0:1, :], bank[7][0:1, 0:3 * NT]))
                nc.vector.tensor_scalar(early[:, :], windows[:, NT:2 * NT], float(MH), None, ALU.min)
                chain.link(nc.vector.tensor_scalar(rounds[:, 0:NT], windows[:, 2 * NT:3 * NT], float(M - 1), None,
                                                   ALU.add))
                chain.link(nc.vector.tensor_tensor(rounds[:, NT:NT + 1], rounds[:, NT - 1:NT],
                                                   windows[:, 2 * NT - 1:2 * NT], ALU.add))
                chain.link(nc.vector.tensor_single_scalar(rounds[:, :], rounds[:, :], M.bit_length() - 1,
                                                          ALU.arith_shift_right))
                dve.wait_ge(consts_ready, 6)
                nc.vector.tensor_copy(sel[:, :].rearrange("p (e k) -> p e k", k=64),
                                      ident[0:E0, 0:E0].unsqueeze(2).to_broadcast([E0, E0, 64]))
                turned = 0
                for dst, blocks in ((wihT, 6), (whhT, 6)):
                    for c in range(C):
                        for j0 in range(0, blocks, 4):
                            k = min(4, blocks - j0)
                            turned += 1
                            dve.wait_ge(raw_high, turned)
                            o = slice(j0 * P, (j0 + k) * P)
                            nc.vector.tensor_tensor(dst[1][:, c, o], bank[(turned - 1) % 6][:, 0:k * P],
                                                    dst[0][:, c, o].bitcast(F32), ALU.subtract).then_inc(raw_copied, 1)
                for c in range(C):
                    turned += 1
                    dve.wait_ge(raw_turned, turned)
                    nc.vector.tensor_copy(gcnT[:, c, :], bank[(turned - 1) % 6][:, 0:D]).then_inc(raw_copied, 1)
                dve.wait_ge(loads_done, 16 * weights["loads"])
                chain.link(nc.vector.tensor_tensor(brz[:, :], bih[:, 0:4], bhh[:, 0:4], ALU.add))
                chain.end()

                variance_chain, rstd_chain = Chain(dve, "variance_chain", 1), Chain(dve, "rstd_chain", 1)
                dve.wait_ge(x_loaded, 16)
                dve.wait_ge(x_tail_loaded, 16)

                def stages(g, w, buffers):
                    stats_, mean_var_, stdev_, rstd_, h4_, part_, rest_ = buffers

                    def variance():
                        variance_chain.begin(g)
                        ln_variance(dve, variance_chain, s_var, w, g * GW, stats_, mean_var_)

                    def normalise():
                        rstd_chain.begin(g)
                        ln_rstd_(dve, rstd_chain, s_std, g, w, stdev_, rstd_)
                        nc.vector.tensor_copy(ln_mean[:, ds(g * GW, w)], mean_var_[:, 0:w, 0])
                        nc.vector.tensor_copy(ln_rstd[:, ds(g * GW, w)], rstd_[:, 0:w])
                        dve.wait_ge(s_mid, TURN_CREDIT + 2 * g - 2)
                        ln_apply(g * GW, w, h4_, mean_var_, rstd_).then_inc(s_h, 1)

                    def first_rest():
                        dve.wait_ge(s_h, g + 1)
                        for half, lo, k in halves(w):
                            dve.wait_ge(s_hi, 2 * g + half + 1)
                            dve.wait_ge(s_lo, TURN_CREDIT + 2 * g - 2)
                            nc.vector.tensor_tensor(rest_[:, half, 0:k, :], h4_[:, lo:lo + k, :],
                                                    part_[:, lo:lo + k, 0:D], ALU.subtract).then_inc(s_r1, 1)

                    def second_rest():
                        for half, lo, k in halves(w):
                            dve.wait_ge(s_mid, TURN_CREDIT + 2 * g + half + 1)
                            nc.vector.tensor_tensor(rest_[:, half, 0:k, :], rest_[:, half, 0:k, :],
                                                    part_[:, lo:lo + k, D:2 * D], ALU.subtract).then_inc(s_r2, 1)

                    return [variance, normalise, first_rest, second_rest]

                table1_groups(dve, stages)

            @block.tensor
            def _(pe):
                pe.wait_ge(consts_ready, 6)
                for n in range(3):
                    pe.wait_ge(edges_float, n + 1)
                    for half in range(2):
                        j0, k = (0, 4) if half == 0 else (4, 3)
                        for j in range(k):
                            last = nc.tensor.transpose(bank[2 * n + half][:, j * EP:(j + 1) * EP],
                                                       edge_f[n][0:EP, (j0 + j) * P:(j0 + j + 1) * P],
                                                       ident[0:EP, 0:EP])
                        last.then_inc(edges_turned, 1)
                pe.wait_ge(lohi_ready, 1)
                for n in range(2):
                    last = nc.tensor.transpose(bank[6][0:NT, n * EP:(n + 1) * EP], lohi[0:EP, n, :],
                                               ident[0:EP, 0:EP])
                last.then_inc(lohi_turned, 1)
                pe.wait_ge(col_ready, 1)
                for n, (c0, m) in enumerate(((5, ident), (7, ident), (7, ustrict))):
                    last = nc.tensor.matmul(bank[7][0:1, n * NT:(n + 1) * NT], col[0:NT, c0:c0 + 1], m[0:NT, 0:NT],
                                            start=True, stop=True)
                last.then_inc(row_ready, 1)
                pe.wait_ge(loads_done, 16 * weights["loads"])
                pe.wait_ge(edges_copied, 6)
                turned = 0
                for n, blocks in enumerate((6, 6, 2)):
                    for c in range(C):
                        for j0 in range(0, blocks, 4):
                            k = min(4, blocks - j0)
                            if turned >= 6:
                                pe.wait_ge(raw_copied, turned - 5)
                            for j in range(k):
                                last = nc.tensor.transpose(bank[turned % 6][:, j * P:(j + 1) * P],
                                                           wraw[n][:, j0 + j, c * P:(c + 1) * P], ident[:, :])
                            last.then_inc(raw_turned, 1)
                            turned += 1
        setup.close()

        class Gather:
            def __init__(self, name, table, with_types):
                self.table, self.with_types = table, with_types
                self.idx_landed = sem(name + "_idx_landed")
                self.landed = [sem(f"{name}_rows_landed{m}") for m in range(M)]
                self.rows_ready = sem(name + "_rows_ready")
                self.used = sem(name + "_rows_used")
                self.hot = sem(name + "_onehot_ready")
                self.done = sem(name + "_window_done")
                self.evacuated = sem(name + "_window_evacuated")

        def window_values(eng, t):
            first = eng.value_load(windows[0:1, ds(t, 1)], min_val=0, max_val=CHUNKS - 1)
            blocks = eng.value_load(windows[0:1, ds(t + NT, 1)], min_val=1, max_val=CHUNKS // U)
            before = eng.value_load(windows[0:1, ds(t + 2 * NT, 1)], min_val=0, max_val=NT * CHUNKS // U)
            return first, blocks, before

        def ring(eng, n, blocks):
            return narrow(eng.snap((n % blocks) * U), 0, (blocks - 1) * U)

        def sp_indices(sp, q):
            def block_indices(n, k):
                slot = ring(sp, n, M)
                sp.wait_ge(q.rows_ready, n + 1)
                sp.dma_start(idx[:, ds(slot, U)], srcT[:, ds(k, U)],
                             allow_slow_non_contiguous=True).then_inc(q.idx_landed, 16)
                sp.wait_ge(q.idx_landed, n * 16 + 16)
                settled(sp)

            with sp.Fori(0, NT) as t:
                first, blocks, before = window_values(sp, t)
                with sp.Fori(0, blocks) as j:
                    block_indices(sp.snap(before + j), narrow(sp.snap(first + j * U), 0, CHUNKS - 1))
            _, blocks, before = window_values(sp, NT - 1)
            with sp.Fori(0, M - 1) as extra:
                block_indices(sp.snap(before + blocks + extra), 0)

        def pool_begin(pool, q, column):
            pool.sem_inc(q.rows_ready, M - 1)
            pool.dma_start(spare[:, column:column + 1], zeros[:, 0:1],
                           allow_slow_non_contiguous=True).then_inc(q.landed[M - 1], 16)

        def pool_rounds(pool, q, r0, r1):
            with pool.Fori(r0, r1) as r:
                for m in range(M):
                    n = pool.snap(r * M + m)
                    pool.wait_ge(q.idx_landed, n * 16 + 16)
                    pool.wait_ge(q.used, n + 1 + MH - M)
                    settled(pool)
                    for s in range(m * U, (m + 1) * U):
                        nc.gpsimd.indirect_dma_start(
                            out=rows[:, s, :], out_offset=None, in_=q.table,
                            in_offset=bass.IndirectOffsetOnAxis(idx[:, s:s + 1], axis=0)).then_inc(q.landed[m], 16)
                    if m == 0:
                        pool.wait_ge(q.landed[M - 1], r * (16 * U) + 16)
                    else:
                        pool.wait_ge(q.landed[m - 1], r * (16 * U) + 16 * U)
                    pool.sem_inc(q.rows_ready, 1)

        def pool_end(pool, q, r):
            pool.wait_ge(q.landed[M - 1], r * (16 * U) + 16)
            pool.sem_inc(q.rows_ready, 1)

        def rounds_value(eng, t, low):
            return eng.value_load(rounds[0:1, ds(t, 1)], min_val=low, max_val=NT * CHUNKS // (U * M) + 1)

        def dve_onehots(dve, q, t, late):
            if late:
                blocks = dve.value_load(windows[0:1, ds(t + NT, 1)], min_val=1, max_val=CHUNKS // U)
                with dve.If(blocks > MH):
                    dve_onehots_of(dve, q, t, MH, blocks)
            else:
                dve_onehots_of(dve, q, t, 0, dve.value_load(early[0:1, ds(t, 1)], min_val=1, max_val=MH))

        def dve_onehots_of(dve, q, t, j0, j1):
            first = dve.value_load(windows[0:1, ds(t, 1)], min_val=0, max_val=CHUNKS - 1)
            before = dve.value_load(windows[0:1, ds(t + 2 * NT, 1)], min_val=0, max_val=NT * CHUNKS // U)
            base = tbase[:, ds(t, 1)]

            def block_onehots(j):
                n = dve.snap(before + j)
                k = narrow(dve.snap(first + j * U), 0, CHUNKS - 1)
                slot = ring(dve, n, MH)
                dve.wait_ge(q.used, n + 1)
                last = nc.vector.scalar_tensor_tensor(
                    onehot[:, ds(slot, U), :], iota_row[:, :].unsqueeze(1).to_broadcast([P, U, P]), base,
                    dstT[:, ds(k, U)].unsqueeze(2).to_broadcast([P, U, P]), ALU.add, ALU.is_equal)
                if q.with_types:
                    last = nc.vector.tensor_tensor(
                        typehot[:, ds(slot, U), :], iota_row[:, 0:RELS].unsqueeze(1).to_broadcast([P, U, RELS]),
                        typeT[:, ds(k, U)].unsqueeze(2).to_broadcast([P, U, RELS]), ALU.is_equal)
                last.then_inc(q.hot, 1)

            with dve.Fori(j0, j1) as j:
                block_onehots(j)

        def pe_window(pe, q, t, acc):
            first, blocks, before = window_values(pe, t)
            wide, low = acc
            ring_rows, hots, types = (ring_[:, :, :].rearrange("p s d -> p (s d)") for ring_ in (rows, onehot, typehot))
            width = D + RELS if q.with_types else D
            nc.tensor.matmul(wide[:, 0:2 * D], zlhs, zrhs[:, 0:2 * D], start=True, stop=False, skip_group_check=True)
            nc.tensor.matmul(low[:, 0:width], zlhs, zrhs[:, 0:width], start=True, stop=False, skip_group_check=True)
            with pe.Fori(0, blocks) as j:
                n = pe.snap(before + j)
                slot, hot_slot = ring(pe, n, M), ring(pe, n, MH)
                row0 = narrow(pe.snap(slot * (PARTS * D)), 0, (M - 1) * U * PARTS * D)
                hot0 = narrow(pe.snap(hot_slot * P), 0, (MH - 1) * U * P)
                type0 = narrow(pe.snap(hot_slot * RELS), 0, (MH - 1) * U * RELS) if q.with_types else None
                pe.wait_ge(q.hot, n + 1)
                pe.wait_ge(q.rows_ready, n + M + 1)
                for s in range(U):
                    hot = hots[:, ds(hot0 + s * P, P)]
                    nc.tensor.matmul(wide[:, 0:2 * D], hot, ring_rows[:, ds(row0 + s * PARTS * D, 2 * D)],
                                     start=False, stop=False, skip_group_check=True)
                    last = nc.tensor.matmul(low[:, 0:D], hot, ring_rows[:, ds(row0 + (s * PARTS + 2) * D, D)],
                                            start=False, stop=False, skip_group_check=True)
                    if q.with_types:
                        last = nc.tensor.matmul(low[:, D:width], hot, types[:, ds(type0 + s * RELS, RELS)],
                                                start=False, stop=False, skip_group_check=True)
                last.then_inc(q.used, 1)
            nc.tensor.matmul(wide[:, 0:2 * D], zlhs, zrhs[:, 0:2 * D], start=False, stop=True, skip_group_check=True)
            nc.tensor.matmul(low[:, 0:width], zlhs, zrhs[:, 0:width], start=False, stop=True,
                             skip_group_check=True).then_inc(q.done, 1)

        def pe_windows(pe, q, g, i, banks):
            t = first_window(g) + i
            back = next(k for k in range(1, GW + 1) if banks[(i - k) % GW] == banks[i])
            if isinstance(t, int) and t == 0:
                i = GW - 1
            elif not (isinstance(t, int) and t < back):
                pe.wait_ge(q.evacuated, t + 1 - back)
            pe_window(pe, q, t, banks[i])

        def router_buffers(name, where):
            f = {k: sb(f"{name}_{k}", [P, GW, E1], F32, where) for k in ("lg", "ex", "p", "c", "eq1", "eq2", "p2")}
            f.update({k: sb(f"{name}_{k}", [P, GW], F32, where) for k in ("m", "m1", "m2", "i", "s", "w1", "w2", "e")})
            return f

        def router_logits(f, chain, logits, w, experts):
            lg = f["lg"][:, 0:w, 0:experts]
            chain.link(nc.vector.tensor_copy(lg, logits.rearrange("p (t e) -> p t e", e=experts)))
            chain.link(nc.vector.tensor_reduce(f["m"][:, 0:w], lg, AX, ALU.max))
            m = f["m"][:, 0:w].unsqueeze(2).to_broadcast([P, w, experts])
            return nc.vector.tensor_tensor(lg, lg, m, ALU.subtract)

        def router_choice(f, chain, w, experts):
            def wide(v):
                return v[:, 0:w].unsqueeze(2).to_broadcast([P, w, experts])
            ex, p, c, eq1, eq2, p2 = (f[k][:, 0:w, 0:experts] for k in ("ex", "p", "c", "eq1", "eq2", "p2"))
            index = ts_idx[:, 0:w, 0:experts]
            chain.link(nc.vector.tensor_reduce(f["s"][:, 0:w], ex, AX, ALU.add))
            chain.link(nc.vector.reciprocal(f["s"][:, 0:w], f["s"][:, 0:w]))
            chain.link(nc.vector.tensor_tensor(p, ex, wide(f["s"]), ALU.mult))
            for source, m, eq in ((p, f["m1"], eq1), (p2, f["m2"], eq2)):
                chain.link(nc.vector.tensor_reduce(m[:, 0:w], source, AX, ALU.max))
                chain.link(nc.vector.tensor_tensor(c, source, wide(m), ALU.not_equal))
                chain.link(nc.vector.scalar_tensor_tensor(c, c, 16.0, index, ALU.mult, ALU.add))
                chain.link(nc.vector.tensor_reduce(f["i"][:, 0:w], c, AX, ALU.min))
                chain.link(nc.vector.tensor_tensor(eq, index, wide(f["i"]), ALU.is_equal))
                if eq is eq1:
                    chain.link(nc.vector.scalar_tensor_tensor(p2, eq1, -4.0, p, ALU.mult, ALU.add))

        work = sb("work", [P, 10, W], F32, layer0)
        rT, zT, tT, nT, hT = (work[:, j:j + C, :] for j in range(0, 10, C))
        a1T, a2T, t0 = work[:, 0:6, :], work[:, 6:9, :], hT
        red4 = sb("red4", [P, GW, D + RELS], F32, layer0)
        ctT = sb("ctT", [RELS, W], F32, layer0)
        red_high, red_low = (sb(f"red_{n}", [P, C, W], FR, layer0) for n in ("high", "low"))
        t_high, t_low = (sb(f"t_{n}", [P, C, W], FR, layer0) for n in ("high", "low"))
        gate5 = sb("gate5", [P, GW, E1], F32, layer0)
        gT = ctT[0:E0 + 1, :]
        deg = sb("deg", [P, GW], F32, layer0)
        f0 = router_buffers("f0", layer0)
        q1 = Gather("g1", table1, True)
        names = ("h4_ready hT_ps ct_ps ct_sb redT_ps hT_high hT_low hT_sb red_high red_low r_ps z_ps in_ps hn_ps r_act z_act t1_done t2_done "
                 "n_act hnew back_ps x1_var x1_std h1_ready h1T_ps h1T_sb gate_ps l1_ps l1_act l2_ps l2_act "
                 "lg_ready ex_ready mm_ready em_ready gates_ready gT_ps gT_sb spread_ps gated l3_ps x2_var x2_std "
                 "h2_ready h2T_ps h2T_sb xt_ps hi_done r1_done mid_done r2_done lo_done table2_out").split()
        S = {n: sem("d_" + n) for n in names}
        BANKS1 = ((bank[6], bank[7]), (bank[5], bank[1]), (bank[6], bank[7]), (bank[6], bank[7]))
        BANKS2 = ((bank[4], bank[5]), (bank[6], bank[7])) * 2
        L1_BANKS = (4, 0, 3, 1, 5, 4)
        L2_BANKS = (0, 3, 4)

        def per_half(w):
            return 1 if w > 2 else 2

        def pe_d1(pe, g, w):
            n = w * P
            pe.wait_ge(S["h4_ready"], g + 1)
            for c in range(C):
                for i in range(w):
                    last = nc.tensor.transpose(bank[c][:, i * P:(i + 1) * P], h4[:, i, c * P:(c + 1) * P], ident[:, :])
            last.then_inc(S["hT_ps"], 1)
            pe.wait_ge(q1.evacuated, first_window(g) + w)
            for i in range(w):
                last = nc.tensor.transpose(bank[2][0:RELS, i * P:(i + 1) * P], red4[:, i, D:D + RELS], ident[:, :])
            last.then_inc(S["ct_ps"], 1)
            pe.wait_ge(S["hi_done"], CREDIT + 2 * g)
            pe.wait_ge(S["r1_done"], CREDIT + 2 * g)
            for c in range(C):
                for i in range(w):
                    nc.tensor.matmul(bank[3 + c][:, i * P:(i + 1) * P], red4[:, i, c * P:(c + 1) * P], ident[:, :],
                                     start=i == 0, stop=False, skip_group_check=True)
            pe.wait_ge(S["ct_sb"], g + 1)
            for c in range(C):
                last = nc.tensor.matmul(bank[3 + c][:, 0:n], relvec[:, c * P:(c + 1) * P], ctT[:, 0:n],
                                        start=False, stop=True, skip_group_check=True)
            last.then_inc(S["redT_ps"], 1)
            def products(acc, o, terms, begin, end, waits=()):
                steps = [(w_half, m_half, k) for w_, m_ in terms
                         for w_half, m_half in ((w_[0], m_[0]), (w_[1], m_[0]), (w_[0], m_[1])) for k in range(C)]
                for at, (w_half, m_half, k) in enumerate(steps):
                    for where, name in waits:
                        if where == at:
                            pe.wait_ge(S[name], g + 1)
                    last = nc.tensor.matmul(acc, w_half[:, k, o:o + P], m_half[:, k, 0:n],
                                            start=begin and at == 0, stop=end and at == len(steps) - 1)
                return last

            hidden, inputs = (whhT, (t_high, t_low)), (wihT, (red_high, red_low))
            for c in range(C):
                b_r, b_z, b_in, b_hn = ((2, 5, 3, 4), (0, 1, 2, 5))[c]
                for gate, b, name in ((0, b_r, "r_ps"), (1, b_z, "z_ps")):
                    if c == 1 and gate == 0:
                        pe.wait_ge(S["hT_sb"], g + 1)
                    waits = ((0, "hT_high"), (2 * C, "hT_low"), (3 * C, "red_high"), (5 * C, "red_low"))
                    products(bank[b][:, 0:n], gate * D + c * P, (hidden, inputs), True, True,
                             waits if c == 0 and gate == 0 else ()).then_inc(S[name], 1)
                if c == 1:
                    pe.wait_ge(S["z_act"], 2 * g + 1)
                o = 2 * D + c * P
                products(bank[b_hn][:, 0:n], o, (hidden,), True, True).then_inc(S["hn_ps"], 1)
                products(bank[b_in][:, 0:n], o, (inputs,), True, True).then_inc(S["in_ps"], 1)

        def pe_d2(pe, g, w):
            n = w * P
            pe.wait_ge(S["hnew"], 2 * g + 2)
            for i in range(w):
                for c in range(C):
                    o = (i % 2) * D + c * P
                    last = nc.tensor.transpose(bank[3 + i // 2][:, o:o + P], nT[:, c, i * P:(i + 1) * P], ident[:, :])
            last.then_inc(S["back_ps"], 1)

        def turn(g, w, b0, b1, ready, done, pe):
            pe.wait_ge(S[ready], g + 1)
            for c, b in enumerate((b0, b1)):
                for i in range(w):
                    last = nc.tensor.transpose(bank[b][:, i * P:(i + 1) * P], h4[:, i, c * P:(c + 1) * P], ident[:, :])
            last.then_inc(S[done], 1)

        def pe_d3(pe, g, w):
            n = w * P
            turn(g, w, 0, 3, "h1_ready", "h1T_ps", pe)
            pe.wait_ge(S["h1T_sb"], g + 1)
            for i in range(w):
                o = slice(i * E0, (i + 1) * E0)
                for c in range(C):
                    nc.tensor.matmul(bank[2][:, o], t0[:, c, i * P:(i + 1) * P], gW[:, c, :],
                                     start=i == 0 and c == 0, stop=False, skip_group_check=True)
                last = nc.tensor.matmul(bank[2][:, o], ones[0:1, :], gb[:, :], start=False, stop=True,
                                        skip_group_check=True)
            last.then_inc(S["gate_ps"], 1)
            for j, b in enumerate(L1_BANKS):
                if j == 3 and not isinstance(g, int) or j == 3 and g < GROUPS:
                    pe.wait_ge(q1.evacuated, first_window(g + 1) + 2)
                if j == 5:
                    pe.wait_ge(S["l1_act"], 6 * g + 1)
                for c in range(C):
                    w1 = sW1[:, c, j * P:(j + 1) * P] if j < 2 else eW1[:, j - 2, c, :]
                    last = nc.tensor.matmul(bank[b][:, 0:n], w1, t0[:, c, 0:n], start=c == 0, stop=c == C - 1)
                last.then_inc(S["l1_ps"], 1)
            pe.wait_ge(S["l1_act"], 6 * g + 2)
            for c in range(C):
                last = nc.tensor.matmul(bank[L2_BANKS[0]][:, 0:n], sW2[:, c, :], a1T[:, c, 0:n], start=c == 0, stop=c == C - 1)
            last.then_inc(S["l2_ps"], 1)
            for pair in range(2):
                pe.wait_ge(S["l1_act"], 6 * g + 4 + 2 * pair)
                for r in range(2):
                    e = 2 * pair + r
                    last = nc.tensor.matmul(bank[L2_BANKS[1 + pair]][r * 64:(r + 1) * 64, 0:n], eW2[:, e, :],
                                            a1T[:, 2 + e, 0:n], start=True, stop=True)
                last.then_inc(S["l2_ps"], 1)

        def pe_d4(pe, g, w):
            n = w * P
            pe.wait_ge(S["gates_ready"], g + 1)
            for i in range(w):
                last = nc.tensor.transpose(bank[2][0:E0 + 1, i * P:(i + 1) * P], gate5[:, i, 0:E0 + 1], ident[:, :])
            last.then_inc(S["gT_ps"], 1)
            pe.wait_ge(S["gT_sb"], g + 1)
            pe.wait_ge(S["l2_act"], 3 * g + 3)
            for pair, b in enumerate((1, 5)):
                nc.tensor.matmul(bank[b][:, 0:n], sel[:, pair * P:(pair + 1) * P], gT[0:E0, 0:n],
                                 start=True, stop=True).then_inc(S["spread_ps"], 1)
            for half, lo, k in halves(w):
                for i in range(lo, lo + k):
                    acc = bank[3 + half][:, (i - lo) * D:(i - lo + 1) * D]
                    nc.tensor.matmul(acc, a2T[:, 0, i * P:(i + 1) * P], sW3[:, :], start=i == lo, stop=False,
                                     skip_group_check=True)
                    nc.tensor.matmul(acc, gT[:, i * P:(i + 1) * P], b_l3[:, :], start=False, stop=False,
                                     skip_group_check=True)
            pe.wait_ge(S["gated"], 2 * g + 2)
            for half, lo, k in halves(w):
                for i in range(lo, lo + k):
                    acc = bank[3 + half][:, (i - lo) * D:(i - lo + 1) * D]
                    for pair in range(2):
                        last = nc.tensor.matmul(acc, a2T[:, 1 + pair, i * P:(i + 1) * P], eW3[:, pair, :],
                                                start=False, stop=pair == 1, skip_group_check=True)
                last.then_inc(S["l3_ps"], per_half(w))

        def pe_d5(pe, g, w):
            turn(g, w, 1, 5, "h2_ready", "h2T_ps", pe)
            pe.wait_ge(S["h2T_sb"], g + 1)
            for half, lo, k in halves(w):
                for i in range(lo, lo + k):
                    o = slice((i - lo) * D, (i - lo + 1) * D)
                    for c in range(C):
                        nc.tensor.matmul(bank[3 + half][:, o], t0[:, c, i * P:(i + 1) * P], gcnT[:, c, :],
                                         start=c == 0, stop=False)
                    last = nc.tensor.matmul(bank[3 + half][:, o], ones[0:1, :], gcn_b[:, :], start=False, stop=True)
                last.then_inc(S["xt_ps"], per_half(w))

        def act_d1(act, g, w):
            n = w * P
            act.wait_ge(S["hT_ps"], g + 1)
            for c in range(C):
                last = nc.scalar.activation(t_high[:, c, 0:n], bank[c][:, 0:n], ACT.Copy)
            last.then_inc(S["hT_high"], 1)
            act.wait_ge(S["ct_ps"], g + 1)
            nc.scalar.activation(ctT[:, 0:n], bank[2][0:RELS, 0:n], ACT.Copy).then_inc(S["ct_sb"], 1)
            act.wait_ge(S["hT_low"], g + 1)
            for c in range(C):
                last = nc.scalar.activation(hT[:, c, 0:n], bank[c][:, 0:n], ACT.Copy)
            last.then_inc(S["hT_sb"], 1)
            act.wait_ge(S["redT_ps"], g + 1)
            for c in range(C):
                last = nc.scalar.activation(red_high[:, c, 0:n], bank[3 + c][:, 0:n], ACT.Copy)
            last.then_inc(S["red_high"], 1)
            for c in range(C):
                b_r, b_z = ((2, 5), (0, 1))[c]
                act.wait_ge(S["r_ps"], 2 * g + c + 1)
                nc.scalar.activation(rT[:, c, 0:n], bank[b_r][:, 0:n], ACT.Sigmoid,
                                     bias=brz[:, c:c + 1]).then_inc(S["r_act"], 1)
                act.wait_ge(S["z_ps"], 2 * g + c + 1)
                nc.scalar.activation(zT[:, c, 0:n], bank[b_z][:, 0:n], ACT.Sigmoid,
                                     bias=brz[:, 2 + c:3 + c]).then_inc(S["z_act"], 1)
            for c in range(C):
                act.wait_ge(S["t2_done"], 2 * g + c + 1)
                nc.scalar.activation(nT[:, c, 0:n], tT[:, c, 0:n], ACT.Tanh,
                                     bias=bih[:, 4 + c:5 + c]).then_inc(S["n_act"], 1)

        def act_d2(act, g, w):
            ln_sqrt(act, S["x1_var"], S["x1_std"], g, w)

        def act_turned(act, g, w, b0, b1, done_ps, done_sb, credit=0):
            act.wait_ge(S[done_ps], credit + g + 1)
            for c, b in enumerate((b0, b1)):
                last = nc.scalar.activation(t0[:, c, 0:w * P], bank[b][:, 0:w * P], ACT.Copy)
            last.then_inc(S[done_sb], 1)

        def act_d3(act, g, w):
            n = w * P
            act_turned(act, g, w, 0, 3, "h1T_ps", "h1T_sb")
            for j, b in enumerate(L1_BANKS):
                act.wait_ge(S["l1_ps"], 6 * g + j + 1)
                nc.scalar.activation(a1T[:, j, 0:n], bank[b][:, 0:n], ACT.Relu,
                                     bias=b_l1[:, j:j + 1]).then_inc(S["l1_act"], 1)
            for j, b in enumerate(L2_BANKS):
                act.wait_ge(S["l2_ps"], 3 * g + j + 1)
                nc.scalar.activation(a2T[:, j, 0:n], bank[b][:, 0:n], ACT.Relu,
                                     bias=b_l2[:, j:j + 1]).then_inc(S["l2_act"], 1)
            act.wait_ge(S["lg_ready"], g + 1)
            nc.scalar.activation(f0["ex"][:, 0:w, 0:E0], f0["lg"][:, 0:w, 0:E0], ACT.Exp).then_inc(S["ex_ready"], 1)
            act.wait_ge(S["mm_ready"], g + 1)
            nc.scalar.activation(f0["e"][:, 0:w], f0["m"][:, 0:w], ACT.Exp).then_inc(S["em_ready"], 1)

        def act_d4(act, g, w):
            n = w * P
            act.wait_ge(S["gT_ps"], g + 1)
            nc.scalar.activation(gT[:, 0:n], bank[2][0:E0 + 1, 0:n], ACT.Copy).then_inc(S["gT_sb"], 1)
            ln_sqrt(act, S["x2_var"], S["x2_std"], g, w)

        def act_d5(act, g, w):
            act_turned(act, g, w, 1, 5, "h2T_ps", "h2T_sb", CREDIT)
            act.wait_ge(S["table2_out"], 16 * g + 16)
            for half, lo, k in halves(w):
                act.wait_ge(S["xt_ps"], 2 * g + half + 1)
                nc.scalar.activation(part[:, lo:lo + k, 0:D],
                                     bank[3 + half][:, 0:k * D].rearrange("p (t d) -> p t d", d=D),
                                     ACT.Copy).then_inc(S["hi_done"], per_half(w))
            for half, lo, k in halves(w):
                act.wait_ge(S["r1_done"], CREDIT + 2 * g + half + 1)
                nc.scalar.activation(part[:, lo:lo + k, D:2 * D], rest[:, half, 0:k, :],
                                     ACT.Copy).then_inc(S["mid_done"], per_half(w))
            for half, lo, k in halves(w):
                act.wait_ge(S["r2_done"], 2 * g + half + 1)
                nc.scalar.activation(part[:, lo:lo + k, 2 * D:3 * D], rest[:, half, 0:k, :],
                                     ACT.Copy).then_inc(S["lo_done"], per_half(w))
            act.wait_ge(S["lo_done"], CREDIT + 2 * g + 2)
            act.dma_start(table2[ds(first_window(g) * P, w * P), :].rearrange("(t p) d -> p t d", p=P),
                          part[:, 0:w, :]).then_inc(S["table2_out"], 16)

        def normalised(dve, g, w):
            dve.wait_ge(S["h2T_ps"], CREDIT + g)
            for i in range(w):
                t = first_window(g) + i
                last = nc.vector.tensor_scalar(h4[:, i, :], x_cols(t, 1), ln_mean[:, ds(t, 1)], ln_rstd[:, ds(t, 1)],
                                               ALU.subtract, ALU.mult)
            last.then_inc(S["h4_ready"], 1)

        def dve_low(dve, g, w, low, high, b0, b1, high_name, low_name):
            dve.wait_ge(S[high_name], g + 1)
            for c, b in enumerate((b0, b1)):
                last = nc.vector.tensor_tensor(low[:, c, 0:w * P], bank[b][:, 0:w * P], high[:, c, 0:w * P].bitcast(F32),
                                               ALU.subtract)
            last.then_inc(S[low_name], 1)

        def dve_d1(dve, chain, g, w):
            n = w * P
            chain.begin(g)
            dve_low(dve, g, w, t_low, t_high, 0, 1, "hT_high", "hT_low")
            dve.wait_ge(q1.evacuated, first_window(g) + w)
            chain.link(nc.vector.tensor_reduce(deg[:, 0:w], red4[:, 0:w, D:D + RELS], AX, ALU.add))
            chain.link(nc.vector.tensor_scalar(deg[:, 0:w], deg[:, 0:w], 1.0, None, ALU.add))
            nc.vector.reciprocal(inv_deg[:, ds(first_window(g), w)], deg[:, 0:w])
            dve_low(dve, g, w, red_low, red_high, 3, 4, "red_high", "red_low")
            for c in range(C):
                b_in, b_hn = ((3, 4), (2, 5))[c]
                dve.wait_ge(S["hn_ps"], 2 * g + c + 1)
                dve.wait_ge(S["r_act"], 2 * g + c + 1)
                nc.vector.scalar_tensor_tensor(tT[:, c, 0:n], bank[b_hn][:, 0:n], bhh[:, 4 + c:5 + c], rT[:, c, 0:n],
                                               ALU.add, ALU.mult).then_inc(S["t1_done"], 1)
                dve.wait_ge(S["t1_done"], 2 * g + c + 1)
                dve.wait_ge(S["in_ps"], 2 * g + c + 1)
                nc.vector.tensor_tensor(tT[:, c, 0:n], tT[:, c, 0:n], bank[b_in][:, 0:n],
                                        ALU.add).then_inc(S["t2_done"], 1)
            for c in range(C):
                dve.wait_ge(S["n_act"], 2 * g + c + 1)
                chain.link(nc.vector.tensor_tensor(tT[:, c, 0:n], hT[:, c, 0:n], nT[:, c, 0:n], ALU.subtract))
                chain.link(nc.vector.tensor_tensor(tT[:, c, 0:n], tT[:, c, 0:n], zT[:, c, 0:n], ALU.mult))
                nc.vector.tensor_tensor(nT[:, c, 0:n], nT[:, c, 0:n], tT[:, c, 0:n], ALU.add).then_inc(S["hnew"], 1)

        def dve_d2(dve, chain, g, w):
            dve.wait_ge(S["back_ps"], g + 1)
            for half, lo, k in halves(w):
                xs = x_cols(first_window(g) + lo, k)
                last = nc.vector.tensor_tensor(xs, xs, bank[3 + half][:, 0:k * D], ALU.add)
            chain.link(last)
            ln_stats(dve, chain, S["x1_var"], S["x1_std"], g, w, first_window(g))
            ln_apply(first_window(g), w).then_inc(S["h1_ready"], 1)

        def dve_d3(dve, chain, g, w):
            dve.wait_ge(S["gate_ps"], g + 1)
            router_logits(f0, chain, bank[2][:, 0:w * E0], w, E0).then_inc(S["lg_ready"], 1)
            dve.wait_ge(S["ex_ready"], g + 1)
            router_choice(f0, chain, w, E0)
            m1, m2, w1, w2, e = (f0[k][:, 0:w] for k in ("m1", "m2", "w1", "w2", "e"))
            nc.vector.tensor_tensor(f0["m"][:, 0:w], m2, m1, ALU.subtract).then_inc(S["mm_ready"], 1)
            dve.wait_ge(S["em_ready"], g + 1)
            chain.link(nc.vector.tensor_scalar(w1, e, 1.0, None, ALU.add))
            chain.link(nc.vector.reciprocal(w1, w1))
            chain.link(nc.vector.tensor_tensor(w2, e, w1, ALU.mult))
            eq1, eq2 = (f0[k][:, 0:w, 0:E0] for k in ("eq1", "eq2"))
            wide = [v.unsqueeze(2).to_broadcast([P, w, E0]) for v in (w1, w2)]
            chain.link(nc.vector.tensor_tensor(eq1, eq1, wide[0], ALU.mult))
            chain.link(nc.vector.tensor_tensor(eq2, eq2, wide[1], ALU.mult))
            nc.vector.memset(gate5[:, 0:w, E0:E0 + 1], 1.0)
            chain.link(nc.vector.tensor_tensor(gate5[:, 0:w, 0:E0], eq1, eq2, ALU.add))
            dve.sem_inc(S["gates_ready"], 1)

        def dve_d4(dve, chain, g, w):
            dve.wait_ge(S["l2_act"], 3 * g + 3)
            for pair, b in enumerate((1, 5)):
                dve.wait_ge(S["spread_ps"], 2 * g + pair + 1)
                hidden = a2T[:, 1 + pair, 0:w * P]
                nc.vector.tensor_tensor(hidden, hidden, bank[b][:, 0:w * P], ALU.mult).then_inc(S["gated"], 1)
            for half, lo, k in halves(w):
                dve.wait_ge(S["l3_ps"], 2 * g + half + 1)
                xs = x_cols(first_window(g) + lo, k)
                last = nc.vector.tensor_tensor(xs, xs, bank[3 + half][:, 0:k * D], ALU.add)
            chain.link(last)
            ln_stats(dve, chain, S["x2_var"], S["x2_std"], g, w, first_window(g))
            ln_apply(first_window(g), w).then_inc(S["h2_ready"], 1)

        def dve_d5(dve, chain, g, w):
            if not (isinstance(g, int) and g == GROUPS):
                normalised(dve, g + 1, GW)
            for half, lo, k in halves(w):
                dve.wait_ge(S["hi_done"], CREDIT + 2 * g + half + 1)
                dve.wait_ge(S["lo_done"], CREDIT + 2 * g)
                nc.vector.tensor_tensor(rest[:, half, 0:k, :], bank[3 + half][:, 0:k * D].rearrange("p (t d) -> p t d", d=D),
                                        part[:, lo:lo + k, 0:D], ALU.subtract).then_inc(S["r1_done"], per_half(w))
            for half, lo, k in halves(w):
                dve.wait_ge(S["mid_done"], 2 * g + half + 1)
                nc.vector.tensor_tensor(rest[:, half, 0:k, :], rest[:, half, 0:k, :],
                                        part[:, lo:lo + k, D:2 * D], ALU.subtract).then_inc(S["r2_done"], per_half(w))
            chain.end()

        sum_chain = [None, None]

        def evacuate1(dve, g, i):
            t = first_window(g) + i
            sums = sum_chain[0]
            sums.begin(t)
            wide, low = BANKS1[i] if not (isinstance(t, int) and t == 0) else BANKS1[GW - 1]
            if not (isinstance(g, int) and g == 0):
                dve.wait_ge(S["redT_ps"], g)
            dve.wait_ge(q1.done, t + 1)
            sums.link(nc.vector.tensor_copy(red4[:, i, :], low[:, 0:D + RELS]))
            for part_ in range(2):
                last = nc.vector.tensor_tensor(red4[:, i, 0:D], red4[:, i, 0:D], wide[:, part_ * D:(part_ + 1) * D],
                                               ALU.add)
                if part_ == 0:
                    sums.link(last)
            last.then_inc(q1.evacuated, 1)

        def run_graph(gather, steps, eng):
            gather(0, 0)
            for i in range(GW):
                steps[i](0, 1)
                gather(1, i)
            steps[GW](0, 1)
            with eng.Fori(2, GROUPS + 1) as g:
                for i in range(GW):
                    steps[i](g - 1, GW)
                    gather(g, i)
                steps[GW](g - 1, GW)
            for i in range(GW + 1):
                steps[i](GROUPS, GW)

        def dve_gather(dve, q, evacuate):
            def gather(g, i):
                t = first_window(g) + i
                if isinstance(t, int) and t == 0:
                    dve_onehots(dve, q, 0, False)
                dve_onehots(dve, q, t, True)
                if i < GW - 1 or isinstance(t, int):
                    dve_onehots(dve, q, t + 1, False)
                else:
                    with dve.If(t + 1 < NT):
                        dve_onehots(dve, q, narrow(t + 1, 0, NT - 1), False)
                evacuate(dve, g, i)
            return gather

        with nc.Block() as block:
            @block.gpsimd
            def _(pool):
                pool_begin(pool, q1, 0)
                total_rounds = rounds_value(pool, NT, 1)
                pool_rounds(pool, q1, 0, total_rounds)
                pool_end(pool, q1, total_rounds)

            @block.tensor
            def _(pe):
                pe.sem_inc(q1.used, MH)
                pe.sem_inc(S["h2T_ps"], CREDIT)
                run_graph(lambda g, i: pe_windows(pe, q1, g, i, BANKS1),
                          [lambda g, w, f=f: f(pe, g, w) for f in (pe_d1, pe_d2, pe_d3, pe_d4, pe_d5)], pe)

            @block.scalar
            def _(act):
                act.sem_inc(S["hi_done"], CREDIT)
                act.sem_inc(S["lo_done"], CREDIT)
                act.dma_start(spare[:, 1:2], zeros[:, 0:1], allow_slow_non_contiguous=True).then_inc(S["table2_out"], 16)
                run_graph(lambda g, i: None,
                          [lambda g, w, f=f: f(act, g, w) for f in (act_d1, act_d2, act_d3, act_d4, act_d5)], act)
                act.wait_ge(S["table2_out"], 16 * (GROUPS + 2))

            @block.vector
            def _(dve):
                chain = Chain(dve, "layer0_chain", 64)
                sum_chain[0] = Chain(dve, "g1_sum_chain", 2)
                dve.sem_inc(S["r1_done"], CREDIT)

                normalised(dve, 0, 1)
                run_graph(dve_gather(dve, q1, evacuate1),
                          [lambda g, w, f=f: f(dve, chain, g, w) for f in (dve_d1, dve_d2, dve_d3, dve_d4, dve_d5)], dve)

            @block.sync
            def _(sp):
                sp_indices(sp, q1)

        layer0.close()

        ffn = ctx.enter_context(ExitStack())
        W1 = sb("W1", [P, C, H], F32, ffn)
        W2 = sb("W2", [P, HC, D], F32, ffn)
        W1_high, W1_low = ([sb(f"W1_{n}0", [P, C, H], FR, ffn)] for n in ("high", "low"))
        W2_high, W2_low = ([sb(f"W2_{n}0", [P, HC, D], FR, ffn)] for n in ("high", "low"))
        b2 = sb("b2", [1, D], F32, ffn)
        b2_high, b2_low = ([sb(f"b2_{n}{b}", [1, D], FR, ffn) for b in range(2)] for n in ("high", "low"))
        b1 = [sb(f"b1_{b}", [P, HC], F32, ffn) for b in range(2)]
        lng = [sb(f"lng_{b}", [P, 2 * C], F32, ffn) for b in range(2)]
        names = ("tail_done raw_loaded small_loaded first_raw_loaded first_small_loaded high_ready b2_split weights_ready one_ready xs_loaded xs_turned xs_read xe_high "
                 "xe_ready g1_ps gelu_done hid_high hid_ready y_ps y_ready y_out expert_done").split()
        X = {n: sem("x_" + n) for n in names}
        SMALL = 4

        def expert_loads(b, e):
            raw = ((W1[:, :, :], a["L1_ffn_W1"][ds(e, 1), :, :].rearrange("a (c p) h -> p (a c) h", p=P)),
                   (W2[:, :, :], a["L1_ffn_W2"][ds(e, 1), :, :].rearrange("a (c p) h -> p (a c) h", p=P)))
            small = ((b1[b][:, :], a["L1_ffn_b1"][ds(e, 1), :].rearrange("a (c p) -> p (a c)", p=P)),
                     (b2[:, :], a["L1_ffn_b2"][ds(e, 1), :]),
                     (lng[b][:, 0:C], a["L1_ffn_ln_g"][ds(e, 1), :].rearrange("a (c p) -> p (a c)", p=P)),
                     (lng[b][:, C:2 * C], a["L1_ffn_ln_b"][ds(e, 1), :].rearrange("a (c p) -> p (a c)", p=P)))
            assert len(small) == SMALL
            return raw, small

        def first_expert(e):
            return "first_" if isinstance(e, int) and e == 0 else ""

        def load_expert(eng, b, e):
            raw, small = expert_loads(b, e)
            for loads, name in ((raw, "raw_loaded"), (small, "small_loaded")):
                for dst, src in loads:
                    eng.dma_start(dst, src, allow_slow_non_contiguous=True).then_inc(X[first_expert(e) + name], 16)

        def act_split(act, b, e):
            act.wait_ge(X[first_expert(e) + "raw_loaded"], e * 32 if not first_expert(e) else 32)
            nc.scalar.activation(W1_high[b][:, :, :], W1[:, :, :], ACT.Copy).then_inc(X["high_ready"], 1)
            nc.scalar.activation(W2_high[b][:, :, :], W2[:, :, :], ACT.Copy).then_inc(X["high_ready"], 1)

        def dve_split(dve, b, e):
            dve.wait_ge(X["high_ready"], e * 2 + 1)
            nc.vector.tensor_tensor(W1_low[b][:, :, :], W1[:, :, :], W1_high[b][:, :, :].bitcast(F32),
                                    ALU.subtract).then_inc(X["weights_ready"], 1)
            dve.wait_ge(X[first_expert(e) + "small_loaded"], e * (16 * SMALL) if not first_expert(e) else 16 * SMALL)
            nc.vector.tensor_copy(b2_high[b][:, :], b2[:, :]).then_inc(X["b2_split"], 1)
            dve.wait_ge(X["high_ready"], e * 2 + 2)
            nc.vector.tensor_tensor(W2_low[b][:, :, :], W2[:, :, :], W2_high[b][:, :, :].bitcast(F32),
                                    ALU.subtract).then_inc(X["weights_ready"], 1)
            dve.wait_ge(X["b2_split"], e + 1)
            nc.vector.tensor_tensor(b2_low[b][:, :], b2[:, :], b2_high[b][:, :].bitcast(F32),
                                    ALU.subtract).then_inc(X["weights_ready"], 1)

        layer1 = ctx.enter_context(ExitStack())
        rows, idx, onehot, spare, stats, mean_var, stdev, rstd = layer_buffers(1, layer1)
        f1 = router_buffers("f1", layer1)
        xnT = sb("xnT", [P, C, W], F32, layer1)
        window_sum = sb("window_sum", [P, D], F32, layer1)
        chosen = sb("chosen", [P, GW, E1], F32, layer1)
        rank = sb("rank", [P, GW, E1], F32, layer1)
        total = sb("total", [P, GW, E1], F32, layer1)
        region = sb("region", [P, E1], F32, layer1)
        count = sb("count", [P, E1], F32, layer1)
        pos_f = sb("pos_f", [P, GW, 2], F32, layer1)
        pos = sb("pos", [P, 2 * GW], I32, layer1)
        xr = sb("xr", [P, GW, 2, RW], F32, layer1)
        q2 = Gather("g2", table2, False)
        names = ("var std xn_ready xnT_ps xnT_sb logit_ps lg_ready ex_ready chosen_ready rank_ps pos_ready "
                 "scattered").split()
        R = {n: sem("r_" + n) for n in names}

        def pe_e1(pe, g, w):
            n = w * P
            pe.wait_ge(R["xn_ready"], g + 1)
            for c in range(C):
                for i in range(w):
                    last = nc.tensor.transpose(bank[c][:, i * P:(i + 1) * P], xr[:, i, 0, c * P:(c + 1) * P],
                                               ident[:, :])
            last.then_inc(R["xnT_ps"], 1)
            pe.wait_ge(R["xnT_sb"], g + 1)
            for i in range(w):
                o = slice(i * E1, (i + 1) * E1)
                for c in range(C):
                    nc.tensor.matmul(bank[2][:, o], xnT[:, c, i * P:(i + 1) * P], Wr[:, c, :],
                                     start=i == 0 and c == 0, stop=False, skip_group_check=True)
                last = nc.tensor.matmul(bank[2][:, o], ones[0:1, :], br[:, :], start=False, stop=True,
                                        skip_group_check=True)
            last.then_inc(R["logit_ps"], 1)

        def pe_e2(pe, g, w):
            flat = chosen[:, 0:w, :].rearrange("p t e -> p (t e)")
            pe.wait_ge(R["chosen_ready"], g + 1)
            nc.tensor.matmul(bank[3][:, 0:w * E1], ustrict[:, :], flat, start=True, stop=True)
            nc.tensor.matmul(bank[2][:, W // 2:W // 2 + w * E1], ones[:, :], flat, start=True, stop=True).then_inc(R["rank_ps"], 1)

        def act_e1(act, g, w):
            n = w * P
            act.wait_ge(R["xnT_ps"], g + 1)
            for c in range(C):
                last = nc.scalar.activation(xnT[:, c, 0:n], bank[c][:, 0:n], ACT.Copy)
            last.then_inc(R["xnT_sb"], 1)
            act.wait_ge(R["lg_ready"], g + 1)
            nc.scalar.activation(f1["ex"][:, 0:w, :], f1["lg"][:, 0:w, :], ACT.Exp).then_inc(R["ex_ready"], 1)

        def dve_e1(dve, chain, g, w):
            if isinstance(g, int) and g == 0:
                dve_split(dve, 0, 0)
            chain.begin(g)
            dve.wait_ge(q2.evacuated, first_window(g) + w)
            ln_stats(dve, chain, R["var"], R["std"], g, w, first_window(g))
            dve.wait_ge(R["scattered"], 16 * 2 * first_window(g) + 16)
            for i in range(w):
                t = first_window(g) + i
                for s_ in range(2):
                    nc.vector.tensor_scalar(xr[:, i, s_, 0:D], x_cols(t, 1), mean_var[:, i, 0:1], rstd[:, i:i + 1],
                                            ALU.subtract, ALU.mult)
            last = nc.vector.tensor_copy(xr[:, 0:w, :, D:RW].bitcast(I32),
                                         place[:, ds(first_window(g) * 2, w * 2)].rearrange("p (t s a) -> p t s a", s=2, a=1))
            last.then_inc(R["xn_ready"], 1)

        def dve_e2(dve, chain, g, w):
            dve.wait_ge(R["logit_ps"], g + 1)
            router_logits(f1, chain, bank[2][:, 0:w * E1], w, E1).then_inc(R["lg_ready"], 1)

            dve.wait_ge(R["ex_ready"], g + 1)
            router_choice(f1, chain, w, E1)
            m1, m2, s = (f1[k][:, 0:w] for k in ("m1", "m2", "s"))
            chain.link(nc.vector.tensor_tensor(s, m1, m2, ALU.add))
            chain.link(nc.vector.reciprocal(s, s))
            wts = row_wt[:, ds(first_window(g) * 2, w * 2)].rearrange("p (t s) -> p t s", s=2)
            nc.vector.tensor_tensor(wts[:, :, 0], m1, s, ALU.mult)
            nc.vector.tensor_tensor(wts[:, :, 1], m2, s, ALU.mult)
            eq = [f1[k][:, 0:w, :] for k in ("eq1", "eq2")]
            nc.vector.tensor_tensor(chosen[:, 0:w, :], eq[0], eq[1], ALU.add).then_inc(R["chosen_ready"], 1)

        def dve_e3(dve, chain, g, w):
            eq = [f1[k][:, 0:w, :] for k in ("eq1", "eq2")]
            dve.wait_ge(R["rank_ps"], g + 1)
            nc.vector.tensor_copy(rank[:, 0:w, :], bank[3][:, 0:w * E1].rearrange("p (t e) -> p t e", e=E1))
            chain.link(nc.vector.tensor_copy(total[:, 0:w, :], bank[2][:, W // 2:W // 2 + w * E1].rearrange("p (t e) -> p t e", e=E1)))
            for i in range(w):
                nc.vector.tensor_tensor(rank[:, i, :], rank[:, i, :], count[:, :], ALU.add)
                chain.link(nc.vector.tensor_tensor(count[:, :], count[:, :], total[:, i, :], ALU.add))
            for s_ in range(2):
                chain.link(nc.vector.tensor_tensor(eq[s_], eq[s_], rank[:, 0:w, :], ALU.mult))
                chain.link(nc.vector.tensor_reduce(pos_f[:, 0:w, s_], eq[s_], AX, ALU.add))
            flat = pos_f[:, 0:w, :].rearrange("p t s -> p (t s)")
            nc.vector.tensor_copy(pos[:, 0:2 * w], flat).then_inc(R["pos_ready"], 1)
            chain.end()

        def evacuate2(dve, g, i):
            t = first_window(g) + i
            sums = sum_chain[1]
            sums.begin(t)
            wide, low = BANKS2[i] if not (isinstance(t, int) and t == 0) else BANKS2[GW - 1]
            dve.wait_ge(q2.done, t + 1)
            if not (isinstance(t, int) and t == 0):
                dve.wait_ge(q2.evacuated, t)
            sums.link(nc.vector.tensor_copy(window_sum[:, :], low[:, 0:D]))
            for part_ in range(2):
                sums.link(nc.vector.tensor_tensor(window_sum[:, :], window_sum[:, :], wide[:, part_ * D:(part_ + 1) * D],
                                                  ALU.add))
            xs = x_cols(t, 1)
            nc.vector.scalar_tensor_tensor(xs, window_sum[:, :], inv_deg[:, ds(t, 1)], xs,
                                           ALU.mult, ALU.add).then_inc(q2.evacuated, 1)

        def scatter(pool, g, w):
            pool.wait_ge(R["pos_ready"], g + 1)
            settled(pool)
            for i in range(w):
                for s_ in range(2):
                    nc.gpsimd.indirect_dma_start(
                        out=routed, out_offset=bass.IndirectOffsetOnAxis(pos[:, 2 * i + s_:2 * i + s_ + 1], axis=0),
                        in_=xr[:, i, s_, :], in_offset=None).then_inc(R["scattered"], 16)

        def nothing(g, w):
            return None

        with nc.Block() as block:
            @block.gpsimd
            def _(pool):
                pool.dma_start(spare[:, 3:4], zeros[:, 0:1], allow_slow_non_contiguous=True).then_inc(R["scattered"], 16)
                pool_begin(pool, q2, 2)
                pool_rounds(pool, q2, 0, rounds_value(pool, 1, 1))

                def rounds_between(t0_, t1):
                    r0, r1 = rounds_value(pool, t0_, 1), rounds_value(pool, t1, 1)
                    with pool.If(r1 > r0):
                        pool_rounds(pool, q2, r0, r1)

                def group(g, w):
                    t = first_window(g)
                    rounds_between(t, t + GW - 1)
                    scatter(pool, g - 1, w)
                    rounds_between(t + GW - 1, t + GW)

                group(1, 1)
                with pool.Fori(2, GROUPS + 1) as g:
                    group(g, GW)
                pool_end(pool, q2, rounds_value(pool, NT, 1))
                scatter(pool, GROUPS, GW)
                pool.wait_ge(R["scattered"], 16 * 2 * NT + 16)

            @block.sync
            def _(sp):
                sp_indices(sp, q2)

            @block.tensor
            def _(pe):
                pe.sem_inc(q2.used, MH)
                steps = [nothing, lambda g, w: pe_e1(pe, g, w), lambda g, w: pe_e2(pe, g, w), nothing, nothing]
                run_graph(lambda g, i: pe_windows(pe, q2, g, i, BANKS2), steps, pe)

            @block.scalar
            def _(act):
                load_expert(act, 0, 0)
                act_split(act, 0, 0)
                run_graph(lambda g, i: None, [lambda g, w: ln_sqrt(act, R["var"], R["std"], g, w), lambda g, w: act_e1(act, g, w),
                                              nothing, nothing, nothing], act)

            @block.vector
            def _(dve):
                start = Chain(dve, "count_chain", 32)
                start.begin(0)
                start.link(nc.vector.tensor_scalar(region[:, :], ts_idx[:, 0, :], float(CAP), None, ALU.mult))
                start.link(nc.vector.tensor_copy(count[:, :], region[:, :]))
                chain = Chain(dve, "layer1_chain", 64)
                sum_chain[1] = Chain(dve, "g2_sum_chain", 3)

                run_graph(dve_gather(dve, q2, evacuate2),
                          [lambda g, w, f=f: f(dve, chain, g, w) for f in (dve_e1, dve_e2, dve_e3)] + [nothing, nothing], dve)
                rows_i, tiles_i = lists[0:1, 0:E1], lists[0:1, E1:2 * E1]
                start.link(nc.vector.tensor_tensor(rows_i, count[0:1, :], region[0:1, :], ALU.subtract))
                start.link(nc.vector.tensor_scalar(tiles_i, rows_i, float(TT - 1), float(TT), ALU.add, ALU.max))
                start.link(nc.vector.tensor_single_scalar(tiles_i, tiles_i, TT.bit_length() - 1, ALU.arith_shift_right))
                start.link(nc.vector.memset(lists[0:1, 2 * E1:2 * E1 + 1], 0))
                for e in range(E1):
                    start.link(nc.vector.tensor_tensor(lists[0:1, 2 * E1 + e + 1:2 * E1 + e + 2],
                                                       lists[0:1, 2 * E1 + e:2 * E1 + e + 1],
                                                       lists[0:1, E1 + e:E1 + e + 1], ALU.add))

        layer1.close()
        for halves_, name, shape in ((W1_high, "W1_high1", [P, C, H]), (W1_low, "W1_low1", [P, C, H]),
                                     (W2_high, "W2_high1", [P, HC, D]), (W2_low, "W2_low1", [P, HC, D])):
            halves_.append(sb(name, shape, FR, ffn))
        one_row = sb("one_row", [1, P], FR, ffn)
        xs = sb("xs", [P, SUB, RW], F32, ffn)
        ys = sb("ys", [P, SUB, D], F32, ffn)
        to = sb("to", [P, SUB], I32, ffn)
        to_next = sb("to_next", [P, SUB], I32, ffn)
        xe = sb("xe", [P, C, TT], F32, ffn)
        xe_high, xe_low = (sb(f"xe_{n}", [P, C, TT], FR, ffn) for n in ("high", "low"))
        hid = sb("hid", [P, HC, TT], F32, ffn)
        hid_high, hid_low = (sb(f"hid_{n}", [P, HC, TT], FR, ffn) for n in ("high", "low"))
        PAIRS = HC // 2

        def expert_tiles(eng, body, before_expert=None, after_expert=None):
            with eng.Fori(0, E1 // 2) as pair:
                for b in range(2):
                    e = pair * 2 + b
                    if before_expert:
                        before_expert(b, e, pair)
                    tiles = eng.value_load(lists[0:1, ds(e + E1, 1)], min_val=1, max_val=NPAD // TT + 1)
                    first = eng.value_load(lists[0:1, ds(e + 2 * E1, 1)], min_val=0, max_val=E1 * (NPAD // TT + 1))
                    with eng.Fori(0, tiles) as j:
                        body(b, e, j, eng.snap(first + j))
                    if after_expert:
                        after_expert(b, e, pair)

        def all_tiles(eng):
            return eng.value_load(lists[0:1, 3 * E1:3 * E1 + 1], min_val=E1, max_val=E1 * (NPAD // TT + 1))

        def weights_ready(eng):
            return lambda b, e, pair: eng.wait_ge(X["weights_ready"], e * 3 + 3)

        def unless_last(eng, b, pair, step):
            if b == 0:
                step()
            else:
                with eng.If(pair < E1 // 2 - 1):
                    step()

        with nc.Block() as block:
            @block.sync
            def _(sp):
                def fill(e):
                    rows_ = sp.value_load(lists[0:1, ds(e, 1)], min_val=0, max_val=NPAD)
                    at = narrow(rows_ + e * CAP, 0, E1 * CAP - TT)
                    sp.dma_start(routed[ds(at, TT), :].rearrange("(p s) d -> p s d", p=P),
                                 filler[:, :, :]).then_inc(X["tail_done"], 16)

                def next_tail(b, e, pair):
                    sp.wait_ge(X["tail_done"], e * 16 + 16)
                    settled(sp)
                    unless_last(sp, b, pair, lambda: fill(narrow(e + 1, 1, E1 - 1)))

                def load(b, e, j, n):
                    at = narrow(sp.snap(e * CAP + j * TT), 0, E1 * CAP - TT)
                    sp.wait_ge(X["xs_turned"], n + CREDIT)
                    sp.wait_ge(X["xs_read"], n + CREDIT)
                    sp.dma_start(xs[:, :, :],
                                 routed[ds(at, TT), :].rearrange("(p s) d -> p s d", p=P)).then_inc(X["xs_loaded"], 16)

                fill(0)
                expert_tiles(sp, load, next_tail)
                n = all_tiles(sp)
                sp.wait_ge(X["xs_turned"], n + CREDIT)
                sp.wait_ge(X["xs_read"], n + CREDIT)
                sp.dma_start(xs[:, :, :], routed[0:TT, :].rearrange("(p s) d -> p s d", p=P)).then_inc(X["xs_loaded"], 16)
                sp.wait_ge(X["xs_loaded"], n * 16 + 16)
                settled(sp)

            @block.gpsimd
            def _(pool):
                nc.gpsimd.tensor_copy(one_row[:, :], ones[0:1, :]).then_inc(X["one_ready"], 1)
                for s in range(SUB):
                    pool.dma_start(results[2 * NPAD + s * P:2 * NPAD + (s + 1) * P, :],
                                   filler[:, s, 0:D]).then_inc(X["y_out"], 16)

                def next_expert(b, e, pair):
                    pool.wait_ge(X["weights_ready"], e * 3 + 3)
                    pool.wait_ge(X["expert_done"], e + CREDIT)
                    settled(pool)

                    def load():
                        load_expert(pool, 1 - b, narrow(e + 1, 1, E1 - 1))

                    unless_last(pool, b, pair, load)

                def store(b, e, j, n):
                    for s in range(SUB):
                        pool.wait_ge(X["y_ready"], n * SUB + s + 1)
                        settled(pool)
                        nc.gpsimd.indirect_dma_start(
                            out=results, out_offset=bass.IndirectOffsetOnAxis(to[:, s:s + 1], axis=0),
                            in_=ys[:, s, :], in_offset=None).then_inc(X["y_out"], 16)

                expert_tiles(pool, store, next_expert)
                n = all_tiles(pool)
                store(0, 0, 0, n)
                pool.wait_ge(X["y_out"], n * (16 * SUB) + 2 * 16 * SUB)

            @block.tensor
            def _(pe):
                def turn_tile(n):
                    pe.wait_ge(X["xs_loaded"], n * 16 + 16)
                    for c in range(C):
                        for s in range(SUB):
                            o = c * TT + s * P
                            last = nc.tensor.transpose(bank[0][:, o:o + P], xs[:, s, c * P:(c + 1) * P],
                                                       ident[:, :])
                    last.then_inc(X["xs_turned"], 1)

                def halves_product(acc, weights_, moving, start, stop):
                    w_high, w_low = weights_
                    m_high, m_low = moving
                    nc.tensor.matmul(acc, w_high, m_high, start=start, stop=False)
                    nc.tensor.matmul(acc, w_high, m_low, start=False, stop=False)
                    return nc.tensor.matmul(acc, w_low, m_high, start=False, stop=stop)

                def tile(b, e, j, n):
                    pe.wait_ge(X["xe_ready"], n + 1)
                    for hc in range(HC):
                        if hc % 2 == 0:
                            pe.wait_ge(X["gelu_done"], n * HC + hc + 2)
                        o = (hc % 2) * TT
                        for c in range(C):
                            block_ = slice(hc * P, (hc + 1) * P)
                            last = halves_product(bank[1 + hc // 2][:, o:o + TT],
                                                  (W1_high[b][:, c, block_], W1_low[b][:, c, block_]),
                                                  (xe_high[:, c, :], xe_low[:, c, :]), c == 0, c == C - 1)
                        if hc % 2 == 1:
                            last.then_inc(X["g1_ps"], 1)
                    turn_tile(n + 1)
                    pe.wait_ge(X["y_ready"], n * SUB + SUB)
                    for s in range(SUB):
                        for b2_half in (b2_high, b2_low):
                            nc.tensor.matmul(bank[5 + s][:, 0:D], one_row[:, :], b2_half[b][:, :],
                                             start=b2_half is b2_high, stop=False)
                    for hc in range(HC):
                        if hc % 2 == 0:
                            pe.wait_ge(X["hid_ready"], n * PAIRS + hc // 2 + 1)
                        for s in range(SUB):
                            tokens = slice(s * P, (s + 1) * P)
                            last = halves_product(bank[5 + s][:, 0:D], (hid_high[:, hc, tokens], hid_low[:, hc, tokens]),
                                                  (W2_high[b][:, hc, :], W2_low[b][:, hc, :]), False, hc == HC - 1)
                    last.then_inc(X["y_ps"], 1)

                def expert_end(b, e, pair):
                    nc.tensor.matmul(bank[7][:, 0:P], zeros[:, 0:P], zeros[:, 0:P], start=True,
                                     stop=True).then_inc(X["expert_done"], 1)

                for s in range(SUB):
                    last = nc.tensor.matmul(bank[5 + s][:, 0:D], zeros[:, 0:P], zeros[:, 0:D], start=True, stop=True)
                last.then_inc(X["y_ps"], 1)
                pe.sem_inc(X["xs_turned"], CREDIT)
                pe.sem_inc(X["expert_done"], CREDIT)
                pe.wait_ge(X["one_ready"], 1)
                turn_tile(0)
                expert_tiles(pe, tile, weights_ready(pe), expert_end)

            @block.scalar
            def _(act):
                act.sem_inc(X["gelu_done"], HC)

                def tile(b, e, j, n):
                    for pair in range(PAIRS):
                        act.wait_ge(X["g1_ps"], n * PAIRS + pair + 1)
                        for hc in (2 * pair, 2 * pair + 1):
                            o = (hc % 2) * TT
                            nc.scalar.activation(hid[:, hc, :], bank[1 + pair][:, o:o + TT], ACT.Gelu,
                                                 bias=b1[b][:, hc:hc + 1]).then_inc(X["gelu_done"], 1)
                        act.wait_ge(X["gelu_done"], n * HC + HC + 2 * pair + 2)
                        both = slice(2 * pair, 2 * pair + 2)
                        nc.scalar.activation(hid_high[:, both, :], hid[:, both, :], ACT.Copy).then_inc(X["hid_high"], 1)

                expert_tiles(act, tile, weights_ready(act), lambda b, e, pair: unless_last(
                    act, b, pair, lambda: act_split(act, 1 - b, e + 1)))

            @block.vector
            def _(dve):
                chain = Chain(dve, "tile_chain", 1)

                def leave(n):
                    dve.wait_ge(X["y_out"], n * (16 * SUB) + 16 * SUB)
                    chain.begin(n)
                    chain.link(nc.vector.tensor_copy(to[:, :], to_next[:, :]))

                def results_out(n):
                    dve.wait_ge(X["y_ps"], n + 1)
                    for s in range(SUB):
                        nc.vector.tensor_copy(ys[:, s, :], bank[5 + s][:, 0:D]).then_inc(X["y_ready"], 1)

                def tile(b, e, j, n):
                    dve.wait_ge(X["xs_turned"], CREDIT + n + 1)
                    for c in range(C):
                        last = nc.vector.tensor_scalar(xe[:, c, :], bank[0][:, c * TT:(c + 1) * TT], lng[b][:, c:c + 1],
                                                       lng[b][:, C + c:C + c + 1], ALU.mult, ALU.add)
                    last.then_inc(X["xe_high"], 1)
                    dve.wait_ge(X["xe_high"], 2 * n + 1)
                    nc.vector.tensor_copy(xe_high[:, :, :], xe[:, :, :]).then_inc(X["xe_high"], 1)
                    dve.wait_ge(X["xe_high"], 2 * n + 2)
                    nc.vector.tensor_tensor(xe_low[:, :, :], xe[:, :, :], xe_high[:, :, :].bitcast(F32),
                                            ALU.subtract).then_inc(X["xe_ready"], 1)
                    leave(n)
                    dve.wait_ge(X["xs_loaded"], n * 16 + 16)
                    nc.vector.tensor_copy(to_next[:, :], xs[:, :, D].bitcast(I32)).then_inc(X["xs_read"], 1)
                    dve.wait_ge(X["xs_read"], CREDIT + n + 1)
                    results_out(n)
                    for pair in range(PAIRS):
                        dve.wait_ge(X["hid_high"], n * PAIRS + pair + 1)
                        both = slice(2 * pair, 2 * pair + 2)
                        nc.vector.tensor_tensor(hid_low[:, both, :], hid[:, both, :], hid_high[:, both, :].bitcast(F32),
                                                ALU.subtract).then_inc(X["hid_ready"], 1)

                nc.vector.tensor_copy(to_next[:, :], filler[:, :, D].bitcast(I32)).then_inc(X["xs_read"], CREDIT)
                dve.wait_ge(X["xs_read"], CREDIT)
                expert_tiles(dve, tile, weights_ready(dve), lambda b, e, pair: unless_last(
                    dve, b, pair, lambda: dve_split(dve, 1 - b, e + 1)))
                n = all_tiles(dve)
                leave(n)
                results_out(n)
        ffn.close()

        comb = ctx.enter_context(ExitStack())
        y = [sb(f"y{b}", [P, GW, 2 * D], F32, comb) for b in range(YB)]
        y_landed = [sem(f"y_landed{b}") for b in range(YB)]
        c_half, c_used, c_out = (sem("c_" + n) for n in ("half", "used", "out"))

        def all_groups(eng, body):
            with eng.Fori(0, GROUPS // YB) as round_:
                for b in range(YB):
                    body(round_ * YB + b, b, round_, GW)
            body(GROUPS, 0, GROUPS // YB, 1)

        assert GROUPS % YB == 0

        with nc.Block() as block:
            @block.scalar
            def _(act):
                def load(g, b, pair, w):
                    act.wait_ge(c_used, g * GW + GW)
                    act.dma_start(y[b][:, 0:w, :],
                                  results[ds(g * (2 * W), w * 2 * P), :].rearrange("(t p s) d -> p t (s d)", p=P, s=2)
                                  ).then_inc(y_landed[b], 16)

                all_groups(act, load)

            @block.vector
            def _(dve):
                dve.sem_inc(c_used, YB * GW)

                def group(g, b, pair, w):
                    dve.wait_ge(y_landed[b], pair * 16 + 16)
                    for s in range(2):
                        for i in range(w):
                            t = g * GW + i
                            if s == 1 and i == 0:
                                dve.wait_ge(c_half, g + 1)
                            last = nc.vector.scalar_tensor_tensor(
                                x_cols(t, 1), y[b][:, i, s * D:(s + 1) * D], row_wt[:, ds(t * 2 + s, 1)], x_cols(t, 1),
                                ALU.mult, ALU.add)
                            if s == 1:
                                last.then_inc(c_used, 1)
                        if s == 0:
                            last.then_inc(c_half, 1)

                all_groups(dve, group)

            @block.sync
            def _(sp):
                with sp.Fori(0, GROUPS) as g:
                    sp.wait_ge(c_used, g * GW + (YB + 1) * GW)
                    sp.dma_start(out[ds(g * W, W), :].rearrange("(t p) d -> p t d", p=P),
                                 x_cols(g * GW, GW).rearrange("p (t d) -> p t d", d=D)).then_inc(c_out, 16)
                sp.wait_ge(c_used, NT + YB * GW)
                sp.dma_start(out[GROUPS * W:N, :], x_res[0:N - GROUPS * W, (NT - 1) * D:NT * D]).then_inc(c_out, 16)
                sp.wait_ge(c_out, 16 * (GROUPS + 1))


_INS = ["x", "src", "dst", "edge_type_16", "L0_gnn_relvectors", "L0_gnn_w_ih", "L0_gnn_w_hh", "L0_gnn_b_ih",
        "L0_gnn_b_hh", "L0_ffn_sW1", "L0_ffn_sb1", "L0_ffn_sW2", "L0_ffn_sb2", "L0_ffn_sW3", "L0_ffn_sb3",
        "L0_ffn_eW1", "L0_ffn_eb1", "L0_ffn_eW2", "L0_ffn_eb2", "L0_ffn_eW3", "L0_ffn_eb3", "L0_ffn_gW",
        "L0_ffn_gb", "L1_gnn_W", "L1_gnn_b", "L1_ffn_Wr", "L1_ffn_br", "L1_ffn_ln_g", "L1_ffn_ln_b",
        "L1_ffn_W1", "L1_ffn_b1", "L1_ffn_W2", "L1_ffn_b2"]


def kernel(**inputs):
    import numpy as _np
    import concourse.bacc as _bacc
    from concourse import mybir as _mybir
    from concourse.bass_utils import run_bass_kernel_spmd as _run

    nc = _bacc.Bacc("TRN2", target_bir_lowering=False, num_devices=1)
    arrays, args = {}, {}
    for name in _INS:
        v = _np.ascontiguousarray(inputs[name])
        arrays[f"in_{name}_dram"] = v
        args[name] = nc.dram_tensor(f"in_{name}_dram", v.shape, _mybir.dt.from_np(v.dtype), kind="ExternalInput").ap()
    out = nc.dram_tensor("out_0_dram", (N, D), _mybir.dt.float32, kind="ExternalOutput").ap()
    program(nc, args, out)
    r = _run(nc, [arrays], core_ids=[0])
    return r.results[0]["out_0_dram"]
```
